# Optimizing a Trainium2 kernel written in Bass

```python
import numpy as np
import jax
import jax.numpy as jnp

def _softmax(x, axis=-1):
    return jax.nn.softmax(x, axis=axis)

def _gelu(x):
    return jax.nn.gelu(x, approximate=True)

def _silu(x):
    return jax.nn.silu(x)

def _sigmoid(x):
    return jax.nn.sigmoid(x)

def _layernorm(x, axis=-1, eps=1e-05):
    m = jnp.mean(x, axis=axis, keepdims=True)
    v = jnp.var(x, axis=axis, keepdims=True)
    return (x - m) / jnp.sqrt(v + eps)

def _scatter_add(tgt, idx, src, axis=0):
    return tgt.at[idx].add(src)

def _segment_sum(src, seg, n):
    return jax.ops.segment_sum(src, seg, n)
kernel_name = 'mk_adaln_d2_jaxref_r4_cce78c'

def setup_inputs(seed: int=0):
    np.random.seed(seed)
    _w = jnp.asarray

    def _L0_attn_setup():
        import jax, jax.numpy as jnp
        import numpy as np
        NEG_INF = -1e+30
        key = jax.random.key(seed)
        ks = jax.random.split(key, 6)
        B, T, C = (4, 512, 256)
        s = 1.0 / np.sqrt(C)
        x = jax.random.normal(ks[0], (B, T, C), dtype=jnp.float32)
        Wq = jax.random.normal(ks[1], (C, C), dtype=jnp.float32) * s
        Wk = jax.random.normal(ks[2], (C, C), dtype=jnp.float32) * s
        Wv = jax.random.normal(ks[3], (C, C), dtype=jnp.float32) * s
        Wo = jax.random.normal(ks[4], (C, C), dtype=jnp.float32) * s
        z = jnp.zeros((C,), dtype=jnp.float32)
        return {'x': x, 'Wq': Wq, 'bq': z, 'Wk': Wk, 'bk': z, 'Wv': Wv, 'bv': z, 'Wo': Wo, 'bo': z}
    _L0_attn_in = _L0_attn_setup()

    def _L0_ffn_setup():
        import jax, jax.numpy as jnp
        import numpy as np
        EPS = 1e-12

        def rms_norm(t, gamma):
            n = jnp.maximum(jnp.linalg.norm(t, axis=-1, keepdims=True), EPS)
            scale = jnp.sqrt(jnp.asarray(t.shape[-1], t.dtype))
            return t / n * scale * gamma
        key = jax.random.key(seed)
        ks = jax.random.split(key, 4)
        b, s, d = (4, 1024, 256)
        e, t = (8, 128)
        hidden = 4 * d
        return {'x': jax.random.normal(ks[0], (b, s, d), dtype=jnp.float32), 'gamma_x': jnp.ones((d,), dtype=jnp.float32), 'gamma_slot': jnp.ones((d,), dtype=jnp.float32), 'slot_embeds': jax.random.normal(ks[1], (e, t, d), dtype=jnp.float32), 'w1': jax.random.normal(ks[2], (d, hidden), dtype=jnp.float32) * (1.0 / np.sqrt(d)), 'w2': jax.random.normal(ks[3], (hidden, d), dtype=jnp.float32) * (1.0 / np.sqrt(hidden))}
    _L0_ffn_in = _L0_ffn_setup()
    _L0_c = _w((lambda *s: np.random.randn(*s).astype(np.float32) * 0.05)(2, 256))
    _L0_wmod = _w((lambda *s: np.random.randn(*s).astype(np.float32) * 0.05)(256, 6 * 256) * 256 ** (-0.5))

    def _L1_attn_setup():
        import jax, jax.numpy as jnp
        import numpy as np
        D_MODEL = 256
        STATE = 64
        HEADS = 8
        EXPAND = 2
        INNER = EXPAND * D_MODEL
        HEAD_DIM = INNER // HEADS
        PROJ_OUT = 2 * INNER + 2 * STATE + HEADS
        BATCH, SEQ = (2, 256)
        EPS = 1e-05

        def _layer_norm(x, gamma, beta):
            mu = jnp.mean(x, axis=-1, keepdims=True)
            xc = x - mu
            var = jnp.mean(xc * xc, axis=-1, keepdims=True)
            return xc * jax.lax.rsqrt(var + EPS) * gamma + beta

        def _mamba2(u, W_in, b_in, A_log, D_skip, dt_bias, W_out, b_out):
            B, L, _ = u.shape
            zxbcdt = u @ W_in + b_in
            z = zxbcdt[..., :INNER]
            xs = zxbcdt[..., INNER:2 * INNER].reshape(B, L, HEADS, HEAD_DIM)
            Bm = zxbcdt[..., 2 * INNER:2 * INNER + STATE]
            Cm = zxbcdt[..., 2 * INNER + STATE:2 * INNER + 2 * STATE]
            dt = jax.nn.softplus(zxbcdt[..., 2 * INNER + 2 * STATE:] + dt_bias)
            A = -jnp.exp(A_log)
            decay = jnp.exp(dt * A)
            dtx = dt[..., None] * xs

            def step(h, inp):
                dec_t, dtx_t, B_t, C_t = inp
                h = dec_t[:, :, None, None] * h + dtx_t[..., None] * B_t[:, None, None, :]
                y = jnp.einsum('bhpn,bn->bhp', h, C_t)
                return (h, y)
            h0 = jnp.zeros((B, HEADS, HEAD_DIM, STATE), u.dtype)
            scan_in = (jnp.moveaxis(decay, 1, 0), jnp.moveaxis(dtx, 1, 0), jnp.moveaxis(Bm, 1, 0), jnp.moveaxis(Cm, 1, 0))
            _, ys = jax.lax.scan(step, h0, scan_in)
            y = jnp.moveaxis(ys, 0, 1)
            y = y + D_skip[None, None, :, None] * xs
            y = y.reshape(B, L, INNER) * jax.nn.silu(z)
            return y @ W_out + b_out
        key = jax.random.key(seed)
        ks = jax.random.split(key, 6)
        g = lambda k, shape, sc: jax.random.normal(k, shape, jnp.float32) * sc
        return {'input_tensor': jax.random.normal(ks[0], (BATCH, SEQ, D_MODEL), jnp.float32), 'ln_gamma': jnp.ones((D_MODEL,), jnp.float32), 'ln_beta': jnp.zeros((D_MODEL,), jnp.float32), 'W_in': g(ks[1], (D_MODEL, PROJ_OUT), 0.02), 'b_in': jnp.zeros((PROJ_OUT,), jnp.float32), 'A_log': jnp.log(jnp.arange(1, HEADS + 1, dtype=jnp.float32)), 'D_skip': jnp.ones((HEADS,), jnp.float32), 'dt_bias': g(ks[2], (HEADS,), 0.1), 'W_out': g(ks[3], (INNER, D_MODEL), 0.02), 'b_out': jnp.zeros((D_MODEL,), jnp.float32)}
    _L1_attn_in = _L1_attn_setup()

    def _L1_ffn_setup():
        import jax, jax.numpy as jnp
        import numpy as np
        B, S, D = (4, 1024, 256)
        E, F_EXP = (16, 512)
        F_C = 2.0
        F_SH = 512
        key = jax.random.key(seed)
        ks = jax.random.split(key, 8)
        s = 0.02
        return {'hidden_states': jax.random.normal(ks[0], (B, S, D), jnp.float32), 'gate_w': jax.random.normal(ks[1], (E, D), jnp.float32) * s, 'Wg': jax.random.normal(ks[2], (E, F_EXP, D), jnp.float32) * s, 'Wu': jax.random.normal(ks[3], (E, F_EXP, D), jnp.float32) * s, 'Wd': jax.random.normal(ks[4], (E, D, F_EXP), jnp.float32) * s, 'Ws_g': jax.random.normal(ks[5], (F_SH, D), jnp.float32) * s, 'Ws_u': jax.random.normal(ks[6], (F_SH, D), jnp.float32) * s, 'Ws_d': jax.random.normal(ks[7], (D, F_SH), jnp.float32) * s}
    _L1_ffn_in = _L1_ffn_setup()
    _L1_c = _w((lambda *s: np.random.randn(*s).astype(np.float32) * 0.05)(2, 256))
    _L1_wmod = _w((lambda *s: np.random.randn(*s).astype(np.float32) * 0.05)(256, 6 * 256) * 256 ** (-0.5))
    _d = {'L0_attn_x': _L0_attn_in['x'], 'L0_attn_Wq': _L0_attn_in['Wq'], 'L0_attn_bq': _L0_attn_in['bq'], 'L0_attn_Wk': _L0_attn_in['Wk'], 'L0_attn_bk': _L0_attn_in['bk'], 'L0_attn_Wv': _L0_attn_in['Wv'], 'L0_attn_bv': _L0_attn_in['bv'], 'L0_attn_Wo': _L0_attn_in['Wo'], 'L0_attn_bo': _L0_attn_in['bo'], 'L0_ffn_gamma_x': _L0_ffn_in['gamma_x'], 'L0_ffn_gamma_slot': _L0_ffn_in['gamma_slot'], 'L0_ffn_slot_embeds': _L0_ffn_in['slot_embeds'], 'L0_ffn_w1': _L0_ffn_in['w1'], 'L0_ffn_w2': _L0_ffn_in['w2'], 'L0_c': _L0_c, 'L0_wmod': _L0_wmod, 'L1_attn_ln_gamma': _L1_attn_in['ln_gamma'], 'L1_attn_ln_beta': _L1_attn_in['ln_beta'], 'L1_attn_W_in': _L1_attn_in['W_in'], 'L1_attn_b_in': _L1_attn_in['b_in'], 'L1_attn_A_log': _L1_attn_in['A_log'], 'L1_attn_D_skip': _L1_attn_in['D_skip'], 'L1_attn_dt_bias': _L1_attn_in['dt_bias'], 'L1_attn_W_out': _L1_attn_in['W_out'], 'L1_attn_b_out': _L1_attn_in['b_out'], 'L1_ffn_gate_w': _L1_ffn_in['gate_w'], 'L1_ffn_Wg': _L1_ffn_in['Wg'], 'L1_ffn_Wu': _L1_ffn_in['Wu'], 'L1_ffn_Wd': _L1_ffn_in['Wd'], 'L1_ffn_Ws_g': _L1_ffn_in['Ws_g'], 'L1_ffn_Ws_u': _L1_ffn_in['Ws_u'], 'L1_ffn_Ws_d': _L1_ffn_in['Ws_d'], 'L1_c': _L1_c, 'L1_wmod': _L1_wmod}
    _x0 = _d['L0_attn_x']
    _d['L0_attn_x'] = jax.random.normal(jax.random.fold_in(jax.random.key(seed), 1), (2, 2048, 256), dtype=_x0.dtype)
    del _x0
    return _d

def reference(L0_attn_x, L0_attn_Wq, L0_attn_bq, L0_attn_Wk, L0_attn_bk, L0_attn_Wv, L0_attn_bv, L0_attn_Wo, L0_attn_bo, L0_ffn_gamma_x, L0_ffn_gamma_slot, L0_ffn_slot_embeds, L0_ffn_w1, L0_ffn_w2, L0_c, L0_wmod, L1_attn_ln_gamma, L1_attn_ln_beta, L1_attn_W_in, L1_attn_b_in, L1_attn_A_log, L1_attn_D_skip, L1_attn_dt_bias, L1_attn_W_out, L1_attn_b_out, L1_ffn_gate_w, L1_ffn_Wg, L1_ffn_Wu, L1_ffn_Wd, L1_ffn_Ws_g, L1_ffn_Ws_u, L1_ffn_Ws_d, L1_c, L1_wmod):

    def _L0_attn_ref(x, Wq, bq, Wk, bk, Wv, bv, Wo, bo):
        import jax, jax.numpy as jnp
        import numpy as np
        NEG_INF = -1e+30
        B, T, C = x.shape
        window = 16
        q = x @ Wq.T + bq
        k = x @ Wk.T + bk
        v = x @ Wv.T + bv
        i = jnp.arange(T)[:, None]
        j = jnp.arange(T)[None, :]
        keep = j >= i - window
        att = jnp.einsum('btc,bsc->bts', q, k) * (1.0 / jnp.sqrt(jnp.float32(C)))
        att = jnp.where(keep, att, NEG_INF)
        att = jax.nn.softmax(att, axis=-1)
        y = jnp.einsum('bts,bsc->btc', att, v)
        return y @ Wo.T + bo

    def _L0_ffn_ref(x, gamma_x, gamma_slot, slot_embeds, w1, w2):
        import jax, jax.numpy as jnp
        import numpy as np
        EPS = 1e-12

        def rms_norm(t, gamma):
            n = jnp.maximum(jnp.linalg.norm(t, axis=-1, keepdims=True), EPS)
            scale = jnp.sqrt(jnp.asarray(t.shape[-1], t.dtype))
            return t / n * scale * gamma
        b, s, d = x.shape
        e, t, _ = slot_embeds.shape
        xn = rms_norm(x, gamma_x)
        se = rms_norm(slot_embeds, gamma_slot)
        logits = jnp.einsum('bsd,etd->bset', xn, se)
        dispatch = jax.nn.softmax(logits, axis=1)
        slots = jnp.einsum('bsd,bset->betd', xn, dispatch)
        h = jax.nn.gelu(slots @ w1, approximate=False)
        processed = h @ w2
        combine = jax.nn.softmax(logits.reshape(b, s, e * t), axis=-1)
        out = jnp.einsum('bnd,bsn->bsd', processed.reshape(b, e * t, d), combine)
        return out

    def _L1_attn_ref(input_tensor, ln_gamma, ln_beta, W_in, b_in, A_log, D_skip, dt_bias, W_out, b_out):
        import jax, jax.numpy as jnp
        import numpy as np
        D_MODEL = 256
        STATE = 64
        HEADS = 8
        EXPAND = 2
        INNER = EXPAND * D_MODEL
        HEAD_DIM = INNER // HEADS
        PROJ_OUT = 2 * INNER + 2 * STATE + HEADS
        BATCH, SEQ = (2, 256)
        EPS = 1e-05

        def _layer_norm(x, gamma, beta):
            mu = jnp.mean(x, axis=-1, keepdims=True)
            xc = x - mu
            var = jnp.mean(xc * xc, axis=-1, keepdims=True)
            return xc * jax.lax.rsqrt(var + EPS) * gamma + beta

        def _mamba2(u, W_in, b_in, A_log, D_skip, dt_bias, W_out, b_out):
            B, L, _ = u.shape
            zxbcdt = u @ W_in + b_in
            z = zxbcdt[..., :INNER]
            xs = zxbcdt[..., INNER:2 * INNER].reshape(B, L, HEADS, HEAD_DIM)
            Bm = zxbcdt[..., 2 * INNER:2 * INNER + STATE]
            Cm = zxbcdt[..., 2 * INNER + STATE:2 * INNER + 2 * STATE]
            dt = jax.nn.softplus(zxbcdt[..., 2 * INNER + 2 * STATE:] + dt_bias)
            A = -jnp.exp(A_log)
            decay = jnp.exp(dt * A)
            dtx = dt[..., None] * xs

            def step(h, inp):
                dec_t, dtx_t, B_t, C_t = inp
                h = dec_t[:, :, None, None] * h + dtx_t[..., None] * B_t[:, None, None, :]
                y = jnp.einsum('bhpn,bn->bhp', h, C_t)
                return (h, y)
            h0 = jnp.zeros((B, HEADS, HEAD_DIM, STATE), u.dtype)
            scan_in = (jnp.moveaxis(decay, 1, 0), jnp.moveaxis(dtx, 1, 0), jnp.moveaxis(Bm, 1, 0), jnp.moveaxis(Cm, 1, 0))
            _, ys = jax.lax.scan(step, h0, scan_in)
            y = jnp.moveaxis(ys, 0, 1)
            y = y + D_skip[None, None, :, None] * xs
            y = y.reshape(B, L, INNER) * jax.nn.silu(z)
            return y @ W_out + b_out
        normed = _layer_norm(input_tensor, ln_gamma, ln_beta)
        out = _mamba2(normed, W_in, b_in, A_log, D_skip, dt_bias, W_out, b_out)
        return input_tensor + out

    def _L1_ffn_ref(hidden_states, gate_w, Wg, Wu, Wd, Ws_g, Ws_u, Ws_d):
        import jax, jax.numpy as jnp
        import numpy as np
        B, S, D = (4, 1024, 256)
        E, F_EXP = (16, 512)
        F_C = 2.0
        F_SH = 512
        b, s, d = hidden_states.shape
        e = gate_w.shape[0]
        cap = int(s * F_C / e)
        logits = jnp.einsum('bsd,ed->bse', hidden_states, gate_w)
        scores = jax.nn.softmax(logits, axis=-1).transpose(0, 2, 1)
        topk_w, topk_idx = jax.lax.top_k(scores, cap)
        x_tok = jnp.take_along_axis(hidden_states[:, None, :, :], topk_idx[..., None], axis=2)
        g = jnp.einsum('becd,efd->becf', x_tok, Wg)
        u = jnp.einsum('becd,efd->becf', x_tok, Wu)
        h = jax.nn.gelu(g, approximate=False) * u
        eo = jnp.einsum('becf,edf->becd', h, Wd) * topk_w[..., None]
        offs = (jnp.arange(b) * s)[:, None, None]
        flat_idx = (topk_idx + offs).reshape(-1)
        flat = jnp.zeros((b * s, d), hidden_states.dtype)
        flat = flat.at[flat_idx].add(eo.reshape(-1, d))
        out = flat.reshape(b, s, d)
        gs = jnp.einsum('bsd,fd->bsf', hidden_states, Ws_g)
        us = jnp.einsum('bsd,fd->bsf', hidden_states, Ws_u)
        shared = jnp.einsum('bsf,df->bsd', jax.nn.gelu(gs, approximate=False) * us, Ws_d)
        return out + shared
    x = L0_attn_x
    mod = (_silu(L0_c) @ L0_wmod).reshape(L0_c.shape[0], 6, 1, -1)
    sa, ca, ga, sb, cb, gb = (mod[:, 0], mod[:, 1], mod[:, 2], mod[:, 3], mod[:, 4], mod[:, 5])
    ga = (2 * (ga >= 0) - 1) * jnp.maximum(jnp.abs(ga), 0.25)
    gb = (2 * (gb >= 0) - 1) * jnp.maximum(jnp.abs(gb), 0.25)
    h = _layernorm(x, axis=-1) * (1 + ca) + sa
    x = x + ga * _L0_attn_ref(h, L0_attn_Wq, L0_attn_bq, L0_attn_Wk, L0_attn_bk, L0_attn_Wv, L0_attn_bv, L0_attn_Wo, L0_attn_bo)
    h = _layernorm(x, axis=-1) * (1 + cb) + sb
    x = x + gb * _L0_ffn_ref(h, L0_ffn_gamma_x, L0_ffn_gamma_slot, L0_ffn_slot_embeds, L0_ffn_w1, L0_ffn_w2)
    mod = (_silu(L1_c) @ L1_wmod).reshape(L1_c.shape[0], 6, 1, -1)
    sa, ca, ga, sb, cb, gb = (mod[:, 0], mod[:, 1], mod[:, 2], mod[:, 3], mod[:, 4], mod[:, 5])
    ga = (2 * (ga >= 0) - 1) * jnp.maximum(jnp.abs(ga), 0.25)
    gb = (2 * (gb >= 0) - 1) * jnp.maximum(jnp.abs(gb), 0.25)
    h = _layernorm(x, axis=-1) * (1 + ca) + sa
    x = x + ga * _L1_attn_ref(h, L1_attn_ln_gamma, L1_attn_ln_beta, L1_attn_W_in, L1_attn_b_in, L1_attn_A_log, L1_attn_D_skip, L1_attn_dt_bias, L1_attn_W_out, L1_attn_b_out)
    h = _layernorm(x, axis=-1) * (1 + cb) + sb
    x = x + gb * _L1_ffn_ref(h, L1_ffn_gate_w, L1_ffn_Wg, L1_ffn_Wu, L1_ffn_Wd, L1_ffn_Ws_g, L1_ffn_Ws_u, L1_ffn_Ws_d)
    return x

_drawn_inputs = setup_inputs


def setup_inputs(seed=0):
    import zlib

    import numpy as np

    out = dict(_drawn_inputs(seed))
    spreads = {'L0_attn_bq': (0.0, 0.1),
     'L0_attn_bk': (0.0, 0.1),
     'L0_attn_bv': (0.0, 0.1),
     'L0_attn_bo': (0.0, 0.1),
     'L0_ffn_gamma_x': (1.0, 0.2),
     'L0_ffn_gamma_slot': (1.0, 0.2),
     'L1_attn_ln_gamma': (1.0, 0.2),
     'L1_attn_ln_beta': (0.0, 0.1),
     'L1_attn_b_in': (0.0, 0.1),
     'L1_attn_D_skip': (1.0, 0.2),
     'L1_attn_b_out': (0.0, 0.1)}
    factors = {}
    for name, (base, spread) in spreads.items():
        noise = np.random.default_rng([zlib.crc32(name.encode()), seed]).standard_normal(out[name].shape)
        drawn = base * np.exp(spread * noise) if base else spread * noise
        out[name] = jnp.asarray(drawn.astype(out[name].dtype))
    for name, factor in factors.items():
        out[name] = (out[name] * factor).astype(out[name].dtype)
    return out
```

```python
import concourse.bass as bass
from concourse import mybir
from contextlib import ExitStack

F32 = mybir.dt.float32
BF16 = mybir.dt.bfloat16
I32 = mybir.dt.int32
U32 = mybir.dt.uint32
ALU = mybir.AluOpType
ACT = mybir.ActivationFunctionType
AX = mybir.AxisListType.X

P = 128
B, T, C = 2, 2048, 256
CH = C // P
NTB = T // P
NT = B * NTB
GT = 4
GW = GT * P
NG = NTB // GT
NMOD = 6
SA, CA, GA, SB, CB, GB = range(NMOD)
WINDOW = 16
NEG = -1e30
LN_EPS = 1e-5
ST = 64
USED = []


def setup(nc, ctx):
    def sb(name, shape, dt=F32):
        return ctx.enter_context(nc.sbuf_tensor(name, shape, dt))

    def ps(name, shape, dt=F32):
        return ctx.enter_context(nc.psum_tensor(name, shape, dt))

    def sem(name):
        USED.append(nc.alloc_semaphore(name))
        return USED[-1]
    return sb, ps, sem


def recycle(nc):
    nc.clear_and_free_semaphores(list(USED))
    USED.clear()
    nc.all_engine_barrier()


def over(row, n):
    return row.unsqueeze(1).to_broadcast([row.shape[0], n, row.shape[-1]])


def fresh(engine, i):
    with engine.register() as r:
        engine.reg_add(r, i, 0)
        return engine.snap(r, min_val=0, max_val=i.max_val)


class Shared:
    pass


def modulation(nc, m, layer, c_cols, wmod, mod_dram):
    with ExitStack() as ctx:
        sb, ps, sem = setup(nc, ctx)
        L = f"m{layer}_"
        cc = sb(L + "cc", [P, CH, B])
        cs = sb(L + "cs", [P, CH, B])
        wm = sb(L + "wm", [P, CH, NMOD * C])
        rows = sb(L + "rows", [B, NMOD, C])
        sgn = sb(L + "sgn", [B, 2, C])
        mag = sb(L + "mag", [B, 2, C])
        pm = ps(L + "pm", [B, NMOD * C])
        loaded, silu_done, rows_ps, rows_cp = sem(L + "loaded"), sem(L + "silu"), sem(L + "rows_ps"), sem(L + "rows_cp")
        neg_done, mag_done, sgn_done, sgn2, scaled, gated = [sem(L + n) for n in ("neg", "mag", "sgn", "sgn2", "scaled", "gated")]
        stored, spread = sem(L + "stored"), sem(L + "spread")
        block = ctx.enter_context(nc.Block())
        gates = rows[:, GA:GB + 1:GB - GA, :]
        scales = rows[:, CA:CB + 1:CB - CA, :]

        @block.sync
        def _(sp):
            sp.dma_start(cc[:], c_cols[layer]).then_inc(loaded, 16)
            sp.dma_start(wm[:], wmod.rearrange("(h p) n -> p h n", p=P)).then_inc(loaded, 16)
            sp.wait_ge(gated, 1)
            sp.wait_ge(scaled, 1)
            sp.dma_start(mod_dram[layer], rows[:]).then_inc(stored, 16)
            sp.wait_ge(stored, 16)
            sp.dma_start(m.mod[:].rearrange("p b m c -> p (b m c)"),
                         mod_dram[layer].rearrange("b m c -> (b m c)").partition_broadcast(P)).then_inc(spread, 16)
            sp.wait_ge(spread, 16)

        @block.scalar
        def _(act):
            act.wait_ge(loaded, 32)
            nc.scalar.activation(cs[:], cc[:], ACT.Silu).then_inc(silu_done, 1)

        @block.tensor
        def _(pe):
            pe.wait_ge(silu_done, 1)
            for n in range(NMOD * C // 512):
                for h in range(CH):
                    last = nc.tensor.matmul(pm[:, n * 512:(n + 1) * 512], cs[:, h, :], wm[:, h, n * 512:(n + 1) * 512],
                                            start=h == 0, stop=h == CH - 1)
            last.then_inc(rows_ps, 1)

        @block.vector
        def _(dve):
            dve.wait_ge(rows_ps, 1)
            nc.vector.tensor_copy(rows[:].rearrange("b m c -> b (m c)"), pm[:]).then_inc(rows_cp, 1)
            dve.wait_ge(rows_cp, 1)
            nc.vector.tensor_scalar(mag[:], gates, -1.0, None, ALU.mult).then_inc(neg_done, 1)
            nc.vector.tensor_scalar(sgn[:], gates, 0.0, 2.0, ALU.is_ge, ALU.mult).then_inc(sgn_done, 1)
            nc.vector.tensor_scalar_add(scales, scales, 1.0).then_inc(scaled, 1)
            dve.wait_ge(sgn_done, 1)
            nc.vector.tensor_scalar_add(sgn[:], sgn[:], -1.0).then_inc(sgn2, 1)
            dve.wait_ge(neg_done, 1)
            nc.vector.scalar_tensor_tensor(out=mag[:], in0=mag[:], scalar=0.25, in1=gates,
                                           op0=ALU.max, op1=ALU.max).then_inc(mag_done, 1)
            dve.wait_ge(mag_done, 1)
            dve.wait_ge(sgn2, 1)
            nc.vector.tensor_tensor(gates, mag[:], sgn[:], ALU.mult).then_inc(gated, 1)


def constants(nc, m, x):
    with ExitStack() as ctx:
        sb, ps, sem = setup(nc, ctx)
        zeroed, ones_set, neg_set, half_set, shaped = [sem(n) for n in ("c_zero", "c_ones", "c_neg", "c_half", "c_shape")]
        x_in = [sem(f"c_x{i}") for i in range(NT // GT)]
        block = ctx.enter_context(nc.Block())
        xt = x.rearrange("(t p) c -> p t c", p=P)

        @block.sync
        def _(sp):
            for i in range(NT // GT):
                sp.dma_start(m.x[:, i * GT:(i + 1) * GT, :], xt[:, i * GT:(i + 1) * GT, :]).then_inc(x_in[i], 16)

        @block.gpsimd
        def _(pool):
            nc.gpsimd.memset(m.ident[:], 0.0).then_inc(zeroed, 1)
            nc.gpsimd.memset(m.mask[:], 0.0).then_inc(zeroed, 1)
            nc.gpsimd.memset(m.upto[:], 1.0).then_inc(ones_set, 1)
            nc.gpsimd.memset(m.after[:], 1.0).then_inc(ones_set, 1)
            nc.gpsimd.memset(m.ones[:], 1.0).then_inc(ones_set, 1)
            nc.gpsimd.memset(m.neghalf[:], -0.5).then_inc(half_set, 1)
            pool.wait_ge(zeroed, 2)
            nc.gpsimd.affine_select(out=m.ident[:], in_=m.ident[:], compare_op=ALU.not_equal, fill=1.0,
                                    base=0, pattern=[[-1, P]], channel_multiplier=1).then_inc(shaped, 1)
            nc.gpsimd.affine_select(out=m.mask[:], in_=m.mask[:], compare_op=ALU.is_ge, fill=NEG,
                                    base=WINDOW - P, pattern=[[1, 2 * P]], channel_multiplier=-1).then_inc(shaped, 1)
            pool.wait_ge(ones_set, 3)
            nc.gpsimd.affine_select(out=m.upto[:], in_=m.upto[:], compare_op=ALU.is_ge, fill=0.0,
                                    base=0, pattern=[[1, P]], channel_multiplier=-1).then_inc(shaped, 1)
            nc.gpsimd.affine_select(out=m.after[:], in_=m.after[:], compare_op=ALU.is_gt, fill=0.0,
                                    base=0, pattern=[[-1, P]], channel_multiplier=1).then_inc(shaped, 1)

        @block.vector
        def _(dve):
            for i in range(NT // GT):
                dve.wait_ge(x_in[i], 16)
                for t in range(i * GT, (i + 1) * GT):
                    nc.vector.bn_stats(m.st[:, t, :], m.x[:, t, :])


def finish_stats(nc, sems, m, n0, n1, eps=LN_EPS):
    a, b, c, d, e = sems
    st = m.st[:, n0:n1, :]
    dve, pool = nc.vector, nc.gpsimd
    mean, rstd, tmp = m.mean[:, n0:n1], m.rstd[:, n0:n1], m.tmp[:, n0:n1]

    def vector():
        dve.tensor_tensor(mean, st[:, :, 1], st[:, :, 4], ALU.add).then_inc(a, 1)
        dve.tensor_tensor(tmp, st[:, :, 1], st[:, :, 4], ALU.subtract).then_inc(a, 1)
        dve.tensor_tensor(rstd, st[:, :, 2], st[:, :, 5], ALU.add).then_inc(a, 1)
        dve.wait_ge(a, 3)
        dve.tensor_scalar(mean, mean, 0.5, None, ALU.mult).then_inc(b, 1)
        dve.tensor_tensor(tmp, tmp, tmp, ALU.mult).then_inc(b, 1)
        dve.tensor_scalar(rstd, rstd, 1.0 / C, eps, ALU.mult, ALU.add).then_inc(b, 1)
        dve.wait_ge(b, 3)
        dve.scalar_tensor_tensor(out=rstd, in0=tmp, scalar=0.25, in1=rstd, op0=ALU.mult, op1=ALU.add).then_inc(c, 1)

    def gpsimd():
        pool.wait_ge(c, 1)
        pool.tensor_tensor(rstd, rstd, m.neghalf[:, n0:n1], ALU.pow).then_inc(e, 1)
    return vector, gpsimd


def attention_projections(nc, m, w):
    with ExitStack() as ctx:
        sb, ps, sem = setup(nc, ctx)
        wq, wk = sb("wq", [P, CH, C]), sb("wk", [P, CH, C])
        wv, wo = sb("wv", [P, CH, C]), sb("wo", [P, CH, C])
        wvo = sb("wvo", [P, B, CH, C])
        qb, kb, vb = sb("qb", [P, CH]), sb("kb", [P, CH]), sb("vb", [P, CH])
        vbb = sb("vbb", [P, CH, P])
        bo = sb("bo", [P, C])
        vrow = sb("vrow", [P, B, C])
        h = sb("a_h", [P, B, GT, C])
        hT = sb("a_hT", [P, B, CH, GW])
        pT = ps("a_pT", [P, CH, GW])
        pq = ps("a_pq", [P, CH, GW])
        pk = ps("a_pk", [P, CH, GW])
        pv = ps("a_pv", [P, GT, C])
        loaded = sem("a_loaded")
        vb_spread, fold_ps, fold1, fold_done = [sem("a_" + n) for n in ("vbs", "fold_ps", "fold1", "fold_done")]
        stat = [sem(f"a_stat{i}") for i in range(5)]
        normed, scaled, shifted, t_ready, t_copied, q_ready, q_copied, k_ready, k_copied, v_ready, v_copied = [
            sem("a_" + n) for n in ("normed", "scaled", "shifted", "t_ready", "t_copied", "q_ready", "q_copied",
                                    "k_ready", "k_copied", "v_ready", "v_copied")]
        block = ctx.enter_context(nc.Block())
        st_vector, st_gpsimd = finish_stats(nc, stat, m, 0, NT)
        NL = 8 * 16

        @block.sync
        def _(sp):
            for dst, src in ((wv, w["Wv"]), (wo, w["WoT"]), (wq, w["WqT"]), (wk, w["WkT"])):
                sp.dma_start(dst[:], src.rearrange("(h p) n -> p h n", p=P)).then_inc(loaded, 16)
            for dst, src in ((qb, w["bq"]), (kb, w["bk"]), (vb, w["bv"])):
                sp.dma_start(dst[:], src).then_inc(loaded, 16)
            sp.dma_start(bo[:], w["bo"].partition_broadcast(P)).then_inc(loaded, 16)

        @block.gpsimd
        def _(pool):
            st_gpsimd()
            with pool.Fori(0, NG) as i:
                for b in range(B):
                    n = i * B + b + 1
                    pool.wait_ge(normed, n * GT)
                    nc.gpsimd.tensor_tensor(h[:, b], h[:, b], over(m.mod[:, b, CA, :], GT), ALU.mult).then_inc(scaled, 1)
                    pool.wait_ge(scaled, n)
                    nc.gpsimd.tensor_tensor(h[:, b], h[:, b], over(m.mod[:, b, SA, :], GT), ALU.add).then_inc(shifted, 1)

        @block.vector
        def _(dve):
            st_vector()
            dve.wait_ge(loaded, NL)
            nc.vector.tensor_copy(vbb[:], vb[:].unsqueeze(2).to_broadcast([P, CH, P])).then_inc(vb_spread, 1)
            nc.vector.memset(m.v[:, :, C:C + 1], 1.0)
            dve.wait_ge(fold_ps, 1)
            for b in range(B):
                nc.vector.tensor_tensor(wvo[:, b], pv[:, 0:CH, :], over(m.mod[:, b, GA, :], CH), ALU.mult).then_inc(fold_done, 1)
                nc.vector.tensor_tensor(vrow[:, b], pv[:, CH, :], bo[:], ALU.add).then_inc(fold1, 1)
                dve.wait_ge(fold1, b + 1)
                nc.vector.tensor_tensor(vrow[:, b], vrow[:, b], m.mod[:, b, GA, :], ALU.mult).then_inc(fold_done, 1)
            dve.wait_ge(stat[4], 1)
            dve.wait_ge(fold_done, 2 * B)

            def normalise(i, b):
                for k in range(GT):
                    t = bass.ds(b * NTB + i * GT + k, 1)
                    nc.vector.tensor_scalar(h[:, b, k, :], m.x[:, t, :].squeeze(1), m.mean[:, t], m.rstd[:, t],
                                            ALU.subtract, ALU.mult).then_inc(normed, 1)

            def group(i, b, last):
                n = i * B + b + 1
                if not last:
                    normalise(i + b, 1 - b)
                dve.wait_ge(t_ready, n)
                nc.vector.tensor_copy(hT[:, b], pT[:]).then_inc(t_copied, 1)
                dve.wait_ge(k_ready, n)
                for o in range(CH):
                    ins = nc.vector.tensor_scalar(m.kT[:, o, bass.ds(b * T + i * GW, GW)], pk[:, o, :], kb[:, o:o + 1],
                                                  None, ALU.add)
                ins.then_inc(k_copied, 1)
                dve.wait_ge(v_ready, n)
                nc.vector.tensor_tensor(m.v[:, bass.ds(b * NTB + i * GT, GT), 0:C], pv[:], over(vrow[:, b], GT),
                                        ALU.add).then_inc(v_copied, 1)

            normalise(0, 0)
            with dve.Fori(0, NG - 1) as i:
                group(i, 0, False)
                group(i, 1, False)
            group(NG - 1, 0, False)
            group(NG - 1, 1, True)

        @block.scalar
        def _(act):
            act.wait_ge(loaded, NL)
            with act.Fori(0, NG) as i:
                for b in range(B):
                    n = i * B + b + 1
                    act.wait_ge(q_ready, n)
                    for o in range(CH):
                        ins = nc.scalar.activation(m.qT[:, o, bass.ds(b * T + i * GW, GW)], pq[:, o, :], ACT.Identity,
                                                   bias=qb[:, o:o + 1])
                    ins.then_inc(q_copied, 1)

        @block.tensor
        def _(pe):
            pe.wait_ge(loaded, NL)
            pe.wait_ge(vb_spread, 1)
            for o in range(CH):
                for k in range(CH):
                    nc.tensor.matmul(pv[:, o, :], wv[:, k, o * P:(o + 1) * P], wo[:, k, :], start=k == 0, stop=k == CH - 1)
            for k in range(CH):
                last = nc.tensor.matmul(pv[:, CH, :], vbb[:, k, :], wo[:, k, :], start=k == 0, stop=k == CH - 1)
            last.then_inc(fold_ps, 1)
            pe.wait_ge(fold_done, 2 * B)
            with pe.Fori(0, NG) as i:
                for b in range(B):
                    n = i * B + b + 1
                    pe.wait_ge(shifted, n)
                    pe.wait_ge(t_copied, n - 1)
                    for o in range(CH):
                        for k in range(GT):
                            last = nc.tensor.transpose(pT[:, o, k * P:(k + 1) * P], h[:, b, k, o * P:(o + 1) * P], m.ident[:])
                    last.then_inc(t_ready, 1)
                    pe.wait_ge(t_copied, n)
                    for dst, wt, free, done in ((pq, wq, q_copied, q_ready), (pk, wk, k_copied, k_ready)):
                        pe.wait_ge(free, n - 1)
                        for o in range(CH):
                            for k in range(CH):
                                last = nc.tensor.matmul(dst[:, o, :], wt[:, k, o * P:(o + 1) * P], hT[:, b, k, :],
                                                        start=k == 0, stop=k == CH - 1)
                        last.then_inc(done, 1)
                    pe.wait_ge(v_copied, n - 1)
                    for j in range(GT):
                        for k in range(CH):
                            last = nc.tensor.matmul(pv[:, j, :], hT[:, b, k, j * P:(j + 1) * P], wvo[:, b, k, :],
                                                    start=k == 0, stop=k == CH - 1)
                    last.then_inc(v_ready, 1)


def attention(nc, m):
    scale = float(C) ** -0.5
    with ExitStack() as ctx:
        sb, ps, sem = setup(nc, ctx)
        qs = sb("b_q", [P, 2, CH, P])
        nmax = sb("b_nmax", [P, 2])
        pr = sb("b_p", [P, 2, T])
        pT = sb("b_pT", [P, 2, GW])
        rden = sb("b_rden", [P, 2])
        pS = ps("b_pS", [P, T])
        pTp = ps("b_pTp", [P, 2, GW])
        pO = ps("b_pO", [P, 2, 512])
        q_staged, s_ready, masked, max_done, nmax_done, exp_done, t_ready, t_copied, pv_done, rden_done, x_done = [
            sem("b_" + n) for n in ("q_staged", "s_ready", "masked", "max_done", "nmax_done", "exp_done", "t_ready",
                                    "t_copied", "pv_done", "rden_done", "x_done")]
        block = ctx.enter_context(nc.Block())
        first = [max(it - 1, 0) for it in range(NTB)]
        nkeys = [NTB - f for f in first]
        ngroups = [-(-n // GT) for n in nkeys]
        before = [sum(ngroups[:it]) for it in range(NTB + 1)]

        def width(it, g):
            return min(GT, nkeys[it] - g * GT) * P

        @block.gpsimd
        def _(pool):
            with pool.Fori(0, B) as b:
                for it in range(NTB):
                    if it >= 2:
                        pool.wait_ge(s_ready, b * NTB + it - 1)
                    else:
                        pool.wait_ge(s_ready, b * NTB)
                    nc.gpsimd.tensor_copy(qs[:, it % 2], m.qT[:, :, bass.ds(b * T + it * P, P)]).then_inc(q_staged, 1)

        @block.tensor
        def _(pe):
            def scores(b, it):
                pe.wait_ge(q_staged, b * NTB + it + 1)
                pe.wait_ge(exp_done, b * NTB + it)
                for g in range(ngroups[it]):
                    w = width(it, g)
                    for k in range(CH):
                        last = nc.tensor.matmul(pS[:, g * GW:g * GW + w], qs[:, it % 2, k, :],
                                                m.kT[:, k, bass.ds(b * T + first[it] * P + g * GW, w)],
                                                start=k == 0, stop=k == CH - 1)
                last.then_inc(s_ready, 1)

            def transposes(b, it, g, n):
                pe.wait_ge(t_copied, b * before[-1] + max(n - 1, 0))
                for j in range(width(it, g) // P):
                    last = nc.tensor.transpose(pTp[:, n % 2, j * P:(j + 1) * P],
                                               pr[:, it % 2, g * GW + j * P:g * GW + (j + 1) * P], m.ident[:])
                last.then_inc(t_ready, 1)

            def values(b, it, g, n):
                pe.wait_ge(t_copied, b * before[-1] + n + 1)
                for j in range(width(it, g) // P):
                    last = nc.tensor.matmul(pO[:, it % 2, 0:C + 1], pT[:, n % 2, j * P:(j + 1) * P],
                                            m.v[:, bass.ds(b * NTB + first[it] + g * GT + j, 1), :].squeeze(1),
                                            start=g == 0 and j == 0, stop=g * GT + j == nkeys[it] - 1)
                last.then_inc(pv_done, 1)

            with pe.Fori(0, B) as b:
                scores(b, 0)
                for it in range(NTB):
                    b = fresh(pe, b)
                    if it + 1 < NTB:
                        scores(b, it + 1)
                    pe.wait_ge(x_done, b * NTB + max(it - 1, 0))
                    pe.wait_ge(exp_done, b * NTB + it + 1)
                    base = before[it]
                    transposes(b, it, 0, base)
                    for g in range(ngroups[it]):
                        if g + 1 < ngroups[it]:
                            transposes(b, it, g + 1, base + g + 1)
                        values(b, it, g, base + g)

        @block.scalar
        def _(act):
            def exps(b, it):
                act.wait_ge(nmax_done, b * NTB + it + 1)
                if it >= 2:
                    act.wait_ge(pv_done, b * before[-1] + before[it - 1])
                else:
                    act.wait_ge(pv_done, b * before[-1])
                nc.scalar.activation(pr[:, it % 2, 0:nkeys[it] * P], pS[:, 0:nkeys[it] * P], ACT.Exp,
                                     bias=nmax[:, it % 2:it % 2 + 1], scale=scale).then_inc(exp_done, 1)

            def copies(b, it):
                for g in range(ngroups[it]):
                    n = before[it] + g
                    act.wait_ge(t_ready, b * before[-1] + n + 1)
                    act.wait_ge(pv_done, b * before[-1] + max(n - 1, 0))
                    w = width(it, g)
                    nc.scalar.copy(pT[:, n % 2, 0:w], pTp[:, n % 2, 0:w]).then_inc(t_copied, 1)

            with act.Fori(0, B) as b:
                exps(b, 0)
                for it in range(NTB):
                    b = fresh(act, b)
                    copies(b, it)
                    if it + 1 < NTB:
                        exps(b, it + 1)

        @block.vector
        def _(dve):
            def maxima(b, it):
                dve.wait_ge(s_ready, b * NTB + it + 1)
                n, lo = min(it + 1, 2), max(1 - it, 0) * P
                nc.vector.tensor_tensor(pS[:, 0:n * P], pS[:, 0:n * P], m.mask[:, lo:2 * P], ALU.add).then_inc(masked, 1)
                dve.wait_ge(masked, b * NTB + it + 1)
                nc.vector.reduce_max(nmax[:, it % 2:it % 2 + 1], pS[:, 0:nkeys[it] * P], axis=AX).then_inc(max_done, 1)
                dve.wait_ge(max_done, b * NTB + it + 1)
                nc.vector.tensor_scalar(nmax[:, it % 2:it % 2 + 1], nmax[:, it % 2:it % 2 + 1], -scale, None,
                                        ALU.mult).then_inc(nmax_done, 1)

            def update(b, it):
                r = rden[:, it % 2:it % 2 + 1]
                xt = m.x[:, bass.ds(b * NTB + it, 1), :].squeeze(1)
                dve.wait_ge(pv_done, b * before[-1] + before[it + 1])
                nc.vector.reciprocal(r, pO[:, it % 2, C:C + 1]).then_inc(rden_done, 1)
                dve.wait_ge(rden_done, b * NTB + it + 1)
                nc.vector.scalar_tensor_tensor(out=xt, in0=pO[:, it % 2, 0:C], scalar=r, in1=xt,
                                               op0=ALU.mult, op1=ALU.add).then_inc(x_done, 1)
                dve.wait_ge(x_done, b * NTB + it + 1)
                nc.vector.bn_stats(m.st[:, bass.ds(b * NTB + it, 1), :].squeeze(1), xt)

            with dve.Fori(0, B) as b:
                maxima(b, 0)
                for it in range(NTB):
                    b = fresh(dve, b)
                    if it + 1 < NTB:
                        maxima(b, it + 1)
                    update(b, it)


E, SL = 8, 128
NS = E * SL
HID = 4 * C
HT = HID // P
SH = NS // 512


def row_norms(nc, m, ss, clamped, powed, n, value, dve_side):
    if dve_side:
        nc.vector.tensor_scalar(ss, ss, 1e-24, None, ALU.max).then_inc(clamped, 1)
    else:
        nc.gpsimd.wait_ge(clamped, value)
        nc.gpsimd.tensor_tensor(ss, ss, m.neghalf[:, 0:n], ALU.pow).then_inc(powed, 1)


def slot_embeddings(nc, m, w):
    with ExitStack() as ctx:
        sb, ps, sem = setup(nc, ctx)
        se = sb("s_se", [P, E, C])
        sq = sb("s_sq", [P, C])
        ss = sb("s_ss", [P, E])
        gamma = sb("s_gamma", [P, C])
        pT = ps("s_pT", [P, 2, CH, GW])
        loaded, squared, clamped, powed, scaled, gammaed, t_ready = [
            sem("s_" + n) for n in ("loaded", "squared", "clamped", "powed", "scaled", "gammaed", "t_ready")]
        block = ctx.enter_context(nc.Block())

        @block.sync
        def _(sp):
            sp.dma_start(se[:], w["slot_embeds"].rearrange("(t p) c -> p t c", p=P)).then_inc(loaded, 16)
            sp.dma_start(gamma[:], w["gamma_slot"].partition_broadcast(P)).then_inc(loaded, 16)
            sp.dma_start(m.gx[:], w["gamma_x"].partition_broadcast(P)).then_inc(loaded, 16)
            sp.dma_start(m.w1[:], w["w1"].rearrange("(h p) n -> p h n", p=P)).then_inc(loaded, 16)
            sp.dma_start(m.w2[:], w["w2"].rearrange("(h p) n -> p h n", p=P)).then_inc(loaded, 16)
            sp.wait_ge(loaded, 80)

        @block.scalar
        def _(act):
            act.wait_ge(loaded, 80)
            for t in range(E):
                if t:
                    act.wait_ge(squared, t)
                nc.scalar.activation(sq[:], se[:, t], ACT.Square, accum_out=ss[:, t:t + 1]).then_inc(squared, 1)

        @block.gpsimd
        def _(pool):
            row_norms(nc, m, ss[:], clamped, powed, E, 1, False)

        @block.vector
        def _(dve):
            dve.wait_ge(squared, E)
            row_norms(nc, m, ss[:], clamped, powed, E, 1, True)
            nc.vector.tensor_scalar(gamma[:], gamma[:], float(C) ** 0.5, None, ALU.mult).then_inc(gammaed, 1)
            nc.vector.tensor_scalar(m.gx[:], m.gx[:], float(C) ** 0.5, None, ALU.mult)
            dve.wait_ge(powed, 1)
            dve.wait_ge(gammaed, 1)
            for t in range(E):
                nc.vector.scalar_tensor_tensor(out=se[:, t], in0=se[:, t], scalar=ss[:, t:t + 1], in1=gamma[:],
                                               op0=ALU.mult, op1=ALU.mult).then_inc(scaled, 1)
            dve.wait_ge(t_ready, 1)
            nc.vector.tensor_copy(m.seT[:].rearrange("p h (a n) -> p a h n", a=2), pT[:])

        @block.tensor
        def _(pe):
            pe.wait_ge(scaled, E)
            for t in range(E):
                for h in range(CH):
                    last = nc.tensor.transpose(pT[:, t // GT, h, t % GT * P:(t % GT + 1) * P],
                                               se[:, t, h * P:(h + 1) * P], m.ident[:])
            last.then_inc(t_ready, 1)


def soft_mixture(nc, m):
    with ExitStack() as ctx:
        sb, ps, sem = setup(nc, ctx)
        xn = sb("d_xn", [P, NTB, C])
        xnT = sb("d_xnT", [P, CH, T])
        raw = sb("d_raw", [P, E, T])
        work = sb("d_work", [P, 2, T])
        slotsT = sb("d_slotsT", [P, CH, NS])
        proc = sb("d_proc", [P, E, C])
        sl = sb("d_sl", [P, 2, C])
        ss = sb("d_ss", [P, NTB])
        sq = sl[:, 0]
        nmax, esum = sb("d_nmax", [P, 2]), sb("d_esum", [P, 2])
        rsum = sb("d_rsum", [P, 2])
        cmax, csum, crs = sb("d_cmax", [P, 2]), sb("d_csum", [P, 2]), sb("d_crs", [P, 2])
        eT = sb("d_eT", [P, 2, GW])
        pL = ps("d_pL", [P, T])
        pT = ps("d_pT", [P, 2, GW])
        pO = ps("d_pO", [P, 2, 512])
        hg = work[:].rearrange("p s (k c) -> p s k c", c=C)[:, :, 0:GT, :]
        hid = work[:].rearrange("p s n -> p (s n)").rearrange("p (t n) -> p t n", n=512)
        pc = work[:, 0, :].rearrange("p (s n) -> p s n", s=2)
        pcT = work[:, 1, :].rearrange("p (s t n) -> p s t n", s=2, t=E)
        names = ("own stat0 stat1 stat2 stat3 stat4 normed scaled shifted squared clamped powed xn_done xT_ready xT_copied "
                 "l_ready max_done nmax_done exp_done raw_done t_ready t_copied sl_ready rsum_done sl_scaled "
                 "h_ready h_done y_ready y_done r_ready cmax_done cnmax_done cexp_done pt_ready pt_copied o_ready "
                 "crs_done x_done").split()
        s = {n: sem("d_" + n) for n in names}
        block = ctx.enter_context(nc.Block())
        st_vector, st_gpsimd = finish_stats(nc, [s[f"stat{i}"] for i in range(5)], m, 0, NT)
        seq = []
        for et in range(E):
            seq += [("exp", et, g) for g in range(NG)] + ([("slots", et - 1, 0)] if et else [])
        seq.append(("slots", E - 1, 0))
        at = {k: n for n, k in enumerate(seq)}
        NSEQ = len(seq)

        @block.gpsimd
        def _(pool):
            st_gpsimd()
            own = m.mod[:, 0, SA:CA + 1, :]
            with pool.Fori(0, B) as b:
                nc.gpsimd.tensor_copy(own, m.mod[:, bass.ds(b, 1), SB:CB + 1, :].squeeze(1)).then_inc(s["own"], 1)
                pool.wait_ge(s["own"], b + 1)
                for g in range(NG):
                    n = b * NG + g + 1
                    pool.wait_ge(s["normed"], n * GT)
                    hb = hg[:, g % 2]
                    nc.gpsimd.tensor_tensor(hb, hb, over(own[:, 1], GT), ALU.mult).then_inc(s["scaled"], 1)
                    pool.wait_ge(s["scaled"], n)
                    nc.gpsimd.tensor_tensor(hb, hb, over(own[:, 0], GT), ALU.add).then_inc(s["shifted"], 1)
                    row_norms(nc, m, ss[:, g * GT:(g + 1) * GT], s["clamped"], s["powed"], GT, n, False)

        @block.vector
        def _(dve):
            st_vector()
            dve.wait_ge(s["stat4"], 1)

            def normalise(b, g):
                for k in range(GT):
                    t = bass.ds(b * NTB + g * GT + k, 1)
                    nc.vector.tensor_scalar(hg[:, g % 2, k, :], m.x[:, t, :].squeeze(1), m.mean[:, t], m.rstd[:, t],
                                            ALU.subtract, ALU.mult).then_inc(s["normed"], 1)

            def rows(b, g):
                n = b * NG + g + 1
                dve.wait_ge(s["squared"], n * GT)
                row_norms(nc, m, ss[:, g * GT:(g + 1) * GT], s["clamped"], s["powed"], GT, n, True)
                dve.wait_ge(s["powed"], n)
                for k in range(GT):
                    t = g * GT + k
                    nc.vector.scalar_tensor_tensor(out=xn[:, t, :], in0=hg[:, g % 2, k, :], scalar=ss[:, t:t + 1],
                                                   in1=m.gx[:], op0=ALU.mult, op1=ALU.mult).then_inc(s["xn_done"], 1)

            def maxima(b, et):
                n = b * E + et + 1
                dve.wait_ge(s["l_ready"], n)
                nc.vector.reduce_max(nmax[:, et % 2:et % 2 + 1], pL[:], axis=AX).then_inc(s["max_done"], 1)
                dve.wait_ge(s["max_done"], n)
                nc.vector.tensor_scalar(nmax[:, et % 2:et % 2 + 1], nmax[:, et % 2:et % 2 + 1], -1.0, None,
                                        ALU.mult).then_inc(s["nmax_done"], 1)

            def copy_t(b, key):
                n = at[key]
                dve.wait_ge(s["t_ready"], b * NSEQ + n + 1)
                kind, et, g = key
                if kind == "exp":
                    nc.vector.tensor_copy(eT[:, g % 2], pT[:, n % 2]).then_inc(s["t_copied"], 1)
                else:
                    nc.vector.tensor_copy(slotsT[:, :, et * P:(et + 1) * P],
                                          pT[:, n % 2, 0:C].rearrange("p (h n) -> p h n", h=CH)).then_inc(s["t_copied"], 1)

            def scale_slots(b, et):
                n = b * E + et + 1
                r = rsum[:, et % 2:et % 2 + 1]
                dve.wait_ge(s["exp_done"], n)
                nc.vector.reciprocal(r, esum[:, et % 2:et % 2 + 1]).then_inc(s["rsum_done"], 1)
                dve.wait_ge(s["rsum_done"], n)
                dve.wait_ge(s["sl_ready"], n)
                nc.vector.tensor_scalar(sl[:, et % 2], pO[:, et % 2, 0:C], r, None, ALU.mult).then_inc(s["sl_scaled"], 1)

            with dve.Fori(0, B) as b:
                dve.wait_ge(s["o_ready"], b * NTB)
                normalise(b, 0)
                for g in range(NG):
                    if g + 1 < NG:
                        if g:
                            dve.wait_ge(s["xn_done"], b * NTB + g * GT)
                        normalise(b, g + 1)
                    rows(b, g)
                b0 = b
                maxima(b, 0)
                for et in range(E):
                    b = fresh(dve, b0)
                    if et + 1 < E:
                        maxima(b, et + 1)
                    for g in range(NG):
                        copy_t(b, ("exp", et, g))
                    scale_slots(b, et)
                    if et:
                        copy_t(b, ("slots", et - 1, 0))
                copy_t(b, ("slots", E - 1, 0))
                b = fresh(dve, b0)
                for et in range(E):
                    dve.wait_ge(s["y_ready"], b * E + et + 1)
                    nc.vector.tensor_tensor(proc[:, et], pO[:, et % 2, 0:C], m.mod[:, bass.ds(b, 1), GB, :].squeeze(1),
                                            ALU.mult).then_inc(s["y_done"], 1)

                def cmaxima(b, t):
                    n = b * NTB + t + 1
                    dve.wait_ge(s["r_ready"], n)
                    nc.vector.reduce_max(cmax[:, t % 2:t % 2 + 1], pL[:, t % 2 * NS:(t % 2 + 1) * NS], axis=AX).then_inc(s["cmax_done"], 1)
                    dve.wait_ge(s["cmax_done"], n)
                    nc.vector.tensor_scalar(cmax[:, t % 2:t % 2 + 1], cmax[:, t % 2:t % 2 + 1], -1.0, None,
                                            ALU.mult).then_inc(s["cnmax_done"], 1)

                def update(b, t):
                    n = b * NTB + t + 1
                    r = crs[:, t % 2:t % 2 + 1]
                    xt = m.x[:, bass.ds(b * NTB + t, 1), :].squeeze(1)
                    nc.vector.reciprocal(r, csum[:, t % 2:t % 2 + 1]).then_inc(s["crs_done"], 1)
                    dve.wait_ge(s["o_ready"], n)
                    dve.wait_ge(s["crs_done"], n)
                    nc.vector.scalar_tensor_tensor(out=xt, in0=pO[:, t % 2, 0:C], scalar=r, in1=xt,
                                                   op0=ALU.mult, op1=ALU.add).then_inc(s["x_done"], 1)
                    dve.wait_ge(s["x_done"], n)
                    nc.vector.bn_stats(m.st[:, bass.ds(b * NTB + t, 1), :].squeeze(1), xt)

                cmaxima(b, 0)
                for t in range(NTB):
                    b = fresh(dve, b0)
                    if t + 1 < NTB:
                        cmaxima(b, t + 1)
                    dve.wait_ge(s["pt_ready"], b * NTB + t + 1)
                    nc.vector.tensor_copy(pcT[:, t % 2].rearrange("p e n -> p (e n)"),
                                          pT[:].rearrange("p s n -> p (s n)")).then_inc(s["pt_copied"], 1)
                    update(b, t)

        @block.scalar
        def _(act):
            def exps(b, et):
                n = b * E + et + 1
                act.wait_ge(s["nmax_done"], n)
                act.wait_ge(s["sl_ready"], b * E + max(et - 1, 0))
                nc.scalar.activation(work[:, et % 2], pL[:], ACT.Exp, bias=nmax[:, et % 2:et % 2 + 1],
                                     accum_out=esum[:, et % 2:et % 2 + 1]).then_inc(s["exp_done"], 1)
                nc.scalar.copy(raw[:, et, :], pL[:]).then_inc(s["raw_done"], 1)

            def cexps(b, t):
                n = b * NTB + t + 1
                act.wait_ge(s["cnmax_done"], n)
                act.wait_ge(s["pt_ready"], b * NTB + max(t - 1, 0))
                act.wait_ge(s["crs_done"], b * NTB + max(t - 1, 0))
                nc.scalar.activation(pc[:, t % 2], pL[:, t % 2 * NS:(t % 2 + 1) * NS], ACT.Exp,
                                     bias=cmax[:, t % 2:t % 2 + 1], accum_out=csum[:, t % 2:t % 2 + 1]).then_inc(s["cexp_done"], 1)

            with act.Fori(0, B) as b0:
                b = b0
                for g in range(NG):
                    n = b * NG + g + 1
                    act.wait_ge(s["shifted"], n)
                    for k in range(GT):
                        if g or k:
                            act.wait_ge(s["squared"], b * NTB + g * GT + k)
                        nc.scalar.activation(sq, hg[:, g % 2, k, :], ACT.Square,
                                             accum_out=ss[:, g * GT + k:g * GT + k + 1]).then_inc(s["squared"], 1)
                for g in range(NG):
                    act.wait_ge(s["xT_ready"], b * NG + g + 1)
                    nc.scalar.copy(xnT[:, :, g * GW:(g + 1) * GW], (pT if g % 2 == 0 else pO)[:]).then_inc(s["xT_copied"], 1)
                b = fresh(act, b0)
                act.wait_ge(s["xn_done"], b * NTB + NTB)
                for et in range(E):
                    exps(b, et)
                b = fresh(act, b0)
                act.wait_ge(s["sl_ready"], b * E + E)
                for a in range(SH):
                    for j in range(HT):
                        n = b * SH * HT + a * HT + j + 1
                        act.wait_ge(s["h_ready"], n)
                        if a and j == 0:
                            act.wait_ge(s["y_ready"], b * E + a * E // SH)
                        nc.scalar.activation(hid[:, j, :], pL[:, j % 4 * 512:(j % 4 + 1) * 512], ACT.Gelu).then_inc(s["h_done"], 1)
                b = fresh(act, b0)
                act.wait_ge(s["y_ready"], b * E + E)
                for t in range(NTB):
                    cexps(b, t)

        @block.tensor
        def _(pe):
            def logits(b, et):
                pe.wait_ge(s["raw_done"], b * E + et)
                for g in range(NG):
                    for k in range(CH):
                        last = nc.tensor.matmul(pL[:, g * GW:(g + 1) * GW], m.seT[:, k, et * P:(et + 1) * P],
                                                xnT[:, k, g * GW:(g + 1) * GW], start=k == 0, stop=k == CH - 1)
                last.then_inc(s["l_ready"], 1)

            def transposes(b, key):
                n = at[key]
                kind, et, g = key
                pe.wait_ge(s["t_copied"], b * NSEQ + max(n - 1, 0))
                if kind == "exp":
                    for j in range(GT):
                        last = nc.tensor.transpose(pT[:, n % 2, j * P:(j + 1) * P],
                                                   work[:, et % 2, g * GW + j * P:g * GW + (j + 1) * P], m.ident[:])
                else:
                    for h in range(CH):
                        last = nc.tensor.transpose(pT[:, n % 2, h * P:(h + 1) * P], sl[:, et % 2, h * P:(h + 1) * P], m.ident[:])
                last.then_inc(s["t_ready"], 1)

            def slots(b, et, g):
                pe.wait_ge(s["t_copied"], b * NSEQ + at["exp", et, g] + 1)
                for j in range(GT):
                    last = nc.tensor.matmul(pO[:, et % 2, 0:C], eT[:, g % 2, j * P:(j + 1) * P], xn[:, g * GT + j, :],
                                            start=g == 0 and j == 0, stop=g == NG - 1 and j == GT - 1)
                if g == NG - 1:
                    last.then_inc(s["sl_ready"], 1)

            with pe.Fori(0, B) as b0:
                b = b0
                for g in range(NG):
                    pe.wait_ge(s["xn_done"], b * NTB + (g + 1) * GT)
                    if g == 0:
                        pe.wait_ge(s["pt_copied"], b * NTB)
                        pe.wait_ge(s["x_done"], b * NTB)
                    if g >= 2:
                        pe.wait_ge(s["xT_copied"], b * NG + g - 1)
                    for h in range(CH):
                        for k in range(GT):
                            last = nc.tensor.transpose((pT if g % 2 == 0 else pO)[:, h, k * P:(k + 1) * P],
                                                       xn[:, g * GT + k, h * P:(h + 1) * P], m.ident[:])
                    last.then_inc(s["xT_ready"], 1)
                pe.wait_ge(s["xT_copied"], b * NG + NG)
                logits(b, 0)
                for et in range(E):
                    b = fresh(pe, b0)
                    if et + 1 < E:
                        logits(b, et + 1)
                    pe.wait_ge(s["exp_done"], b * E + et + 1)
                    pe.wait_ge(s["sl_scaled"], b * E + max(et - 1, 0))
                    transposes(b, ("exp", et, 0))
                    for g in range(NG):
                        if g + 1 < NG:
                            transposes(b, ("exp", et, g + 1))
                        slots(b, et, g)
                    if et:
                        pe.wait_ge(s["sl_scaled"], b * E + et)
                        transposes(b, ("slots", et - 1, 0))
                pe.wait_ge(s["sl_scaled"], b * E + E)
                transposes(b, ("slots", E - 1, 0))
                b = fresh(pe, b0)
                pe.wait_ge(s["t_copied"], b * NSEQ + NSEQ)
                pe.wait_ge(s["raw_done"], b * E + E)
                for a in range(SH):
                    for j in range(HT):
                        n = b * SH * HT + a * HT + j
                        if a or j >= 4:
                            pe.wait_ge(s["h_done"], n - 3)
                        for k in range(CH):
                            last = nc.tensor.matmul(pL[:, j % 4 * 512:(j % 4 + 1) * 512], m.w1[:, k, j * P:(j + 1) * P],
                                                    slotsT[:, k, a * 512:(a + 1) * 512], start=k == 0, stop=k == CH - 1)
                        last.then_inc(s["h_ready"], 1)
                    pe.wait_ge(s["h_done"], b * SH * HT + (a + 1) * HT)
                    for e in range(4):
                        et = a * 4 + e
                        if et >= 2:
                            pe.wait_ge(s["y_done"], b * E + et - 1)
                        for j in range(HT):
                            last = nc.tensor.matmul(pO[:, et % 2, 0:C], hid[:, j, e * P:(e + 1) * P], m.w2[:, j, :],
                                                    start=j == 0, stop=j == HT - 1)
                        last.then_inc(s["y_ready"], 1)

                def by_token(b, t):
                    pe.wait_ge(s["cexp_done"], b * NTB + max(t - 1, 0))
                    for e in range(E):
                        o = t % 2 * NS + e * P
                        last = nc.tensor.transpose(pL[:, o:o + P], raw[:, e, t * P:(t + 1) * P], m.ident[:])
                    last.then_inc(s["r_ready"], 1)

                b = fresh(pe, b0)
                pe.wait_ge(s["y_done"], b * E + E)
                by_token(b, 0)
                for t in range(NTB):
                    b = fresh(pe, b0)
                    n = b * NTB + t + 1
                    if t + 1 < NTB:
                        by_token(b, t + 1)
                    pe.wait_ge(s["cexp_done"], n)
                    pe.wait_ge(s["pt_copied"], n - 1)
                    for e in range(E):
                        last = nc.tensor.transpose(pT[:, e // 4, e % 4 * P:(e % 4 + 1) * P], pc[:, t % 2, e * P:(e + 1) * P], m.ident[:])
                    last.then_inc(s["pt_ready"], 1)
                    pe.wait_ge(s["pt_copied"], n)
                    pe.wait_ge(s["x_done"], b * NTB + max(t - 1, 0))
                    for e in range(E):
                        last = nc.tensor.matmul(pO[:, t % 2, 0:C], pcT[:, t % 2, e, :], proc[:, e, :], start=e == 0, stop=e == E - 1)
                    last.then_inc(s["o_ready"], 1)


STATE, HEADS = 64, 8
INNER = 2 * C
HD = INNER // HEADS
PROJ = 2 * INNER + 2 * STATE + HEADS
ZX = 2 * INNER
DT0 = ZX + 2 * STATE


def least(v):
    return max(v, 0) if isinstance(v, int) else v


def state_inputs(nc, m, w):
    with ExitStack() as ctx:
        sb, ps, sem = setup(nc, ctx)
        hg, un = sb("e_hg", [P, B, GT, C]), sb("e_un", [P, B, GT, C])
        ug = sb("e_ug", [P, B, CH, GW])
        gated = sb("e_gated", [P, B, GT, C])
        wdt = sb("e_wdt", [P, CH, HEADS])
        gb = sb("e_gb", [P, 2, CH])
        bout = sb("e_bout", [P, C])
        bdt, bdt2 = sb("e_bdt", [P, HEADS]), sb("e_bdt2", [P, HEADS])
        st2, mv = sb("e_st2", [P, B, GT, 6]), sb("e_mv", [P, B, GT, 2])
        rs = sb("e_rs", [P, B, GT])
        pT = ps("e_pT", [P, 2, CH, GW])
        pd = ps("e_pd", [P, 2, 512])
        names = ("loaded bias stat0 stat1 stat2 stat3 stat4 normed scaled shifted st2 mv var_done powed un_done kept gated x_done t_ready "
                 "t_copied d_ready d_done").split()
        s = {n: sem("e_" + n) for n in names}
        u_out = [sem(f"e_u_out{b}") for b in range(B)]
        block = ctx.enter_context(nc.Block())
        st_vector, st_gpsimd = finish_stats(nc, [s[f"stat{i}"] for i in range(5)], m, 0, NT)

        @block.sync
        def _(sp):
            sp.dma_start(wdt[:], w["W_in"][:, DT0:PROJ].rearrange("(h p) n -> p h n", p=P)).then_inc(s["loaded"], 16)
            sp.dma_start(gb[:], w["ln_cols"]).then_inc(s["loaded"], 16)
            sp.dma_start(bout[:], w["b_out"].partition_broadcast(P)).then_inc(s["loaded"], 16)
            sp.dma_start(bdt[:], w["b_in"][DT0:PROJ].partition_broadcast(P)).then_inc(s["loaded"], 16)
            sp.dma_start(bdt2[:], w["dt_bias"].partition_broadcast(P)).then_inc(s["loaded"], 16)
            with sp.Fori(0, NG) as i:
                for b in range(B):
                    sp.wait_ge(s["t_copied"], i * B + b + 1)
                    sp.dma_start(m.uT[:, :, bass.ds(b * T + i * GW, GW)], ug[:, b]).then_inc(u_out[b], 16)
            for b in range(B):
                sp.wait_ge(u_out[b], 16 * NG)

        @block.gpsimd
        def _(pool):
            st_gpsimd()
            with pool.Fori(0, NG) as i:
                for b in range(B):
                    n = i * B + b + 1
                    pool.wait_ge(s["normed"], n * GT)
                    nc.gpsimd.tensor_tensor(hg[:, b], hg[:, b], over(m.mod[:, b, CA, :], GT), ALU.mult).then_inc(s["scaled"], 1)
                    pool.wait_ge(s["scaled"], n)
                    nc.gpsimd.tensor_tensor(hg[:, b], hg[:, b], over(m.mod[:, b, SA, :], GT), ALU.add).then_inc(s["shifted"], 1)
                    pool.wait_ge(s["var_done"], n)
                    nc.gpsimd.tensor_tensor(rs[:, b], rs[:, b], m.neghalf[:, 0:GT], ALU.pow).then_inc(s["powed"], 1)
                    pool.wait_ge(s["kept"], n)
                    nc.gpsimd.tensor_tensor(gated[:, b], gated[:, b], over(m.mod[:, b, GA, :], GT), ALU.mult).then_inc(s["gated"], 1)

        @block.vector
        def _(dve):
            st_vector()
            dve.wait_ge(s["loaded"], 80)
            nc.vector.tensor_tensor(bdt[:], bdt[:], bdt2[:], ALU.add).then_inc(s["bias"], 1)
            dve.wait_ge(s["stat4"], 1)
            dve.wait_ge(s["bias"], 1)

            def normalise(i, b):
                for k in range(GT):
                    t = bass.ds(b * NTB + i * GT + k, 1)
                    nc.vector.tensor_scalar(hg[:, b, k, :], m.x[:, t, :].squeeze(1), m.mean[:, t], m.rstd[:, t],
                                            ALU.subtract, ALU.mult).then_inc(s["normed"], 1)

            def group(i, b, first, last):
                n = i * B + b + 1
                if not last:
                    if not first:
                        dve.wait_ge(s["x_done"], n - 1)
                        dve.wait_ge(s["un_done"], (n - 1) * GT)
                    normalise(i + b, 1 - b)
                dve.wait_ge(s["shifted"], n)
                for k in range(GT):
                    nc.vector.bn_stats(st2[:, b, k, :], hg[:, b, k, :]).then_inc(s["st2"], 1)
                dve.wait_ge(s["st2"], n * GT)
                nc.vector.tensor_tensor(gated[:, b], hg[:, b], over(bout[:], GT), ALU.add).then_inc(s["kept"], 1)
                for k in range(GT):
                    nc.vector.bn_aggr(mv[:, b, k, :], st2[:, b, k, :]).then_inc(s["mv"], 1)
                dve.wait_ge(s["mv"], n * GT)
                nc.vector.tensor_scalar(rs[:, b], mv[:, b, :, 1], LN_EPS, None, ALU.add).then_inc(s["var_done"], 1)
                dve.wait_ge(s["powed"], n)
                dve.wait_ge(s["t_ready"], least(n - 2) if first else n - 2)
                for k in range(GT):
                    nc.vector.tensor_scalar(un[:, b, k, :], hg[:, b, k, :], mv[:, b, k, 0:1], rs[:, b, k:k + 1],
                                            ALU.subtract, ALU.mult).then_inc(s["un_done"], 1)
                xg = m.x[:, bass.ds(b * NTB + i * GT, GT), :]
                dve.wait_ge(s["gated"], n)
                nc.vector.tensor_tensor(xg, xg, gated[:, b], ALU.add).then_inc(s["x_done"], 1)
                dve.wait_ge(s["d_ready"], n)
                nc.vector.tensor_tensor(m.dt[:, bass.ds(b * NTB + i * GT, GT), :],
                                        pd[:, b, 0:GT * HEADS].rearrange("p (t h) -> p t h", h=HEADS),
                                        bdt[:].unsqueeze(1).to_broadcast([P, GT, HEADS]), ALU.add).then_inc(s["d_done"], 1)

            normalise(0, 0)
            group(0, 0, True, False)
            group(0, 1, False, False)
            with dve.Fori(1, NG - 1) as i:
                group(i, 0, False, False)
                group(i, 1, False, False)
            group(NG - 1, 0, False, False)
            group(NG - 1, 1, False, True)

        @block.scalar
        def _(act):
            act.wait_ge(s["loaded"], 80)

            def group(i, b):
                n = i * B + b + 1
                act.wait_ge(s["t_ready"], n)
                if not isinstance(i, int):
                    act.wait_ge(u_out[b], 16 * i)
                    act.wait_ge(s["d_ready"], n - 2)
                for h in range(CH):
                    last = nc.scalar.activation(ug[:, b, h, :], pT[:, b, h, :], ACT.Identity,
                                                scale=gb[:, 0, h:h + 1], bias=gb[:, 1, h:h + 1])
                last.then_inc(s["t_copied"], 1)

            group(0, 0)
            group(0, 1)
            with act.Fori(1, NG) as i:
                group(i, 0)
                group(i, 1)

        @block.tensor
        def _(pe):
            pe.wait_ge(s["loaded"], 80)
            with pe.Fori(0, NG) as i:
                for b in range(B):
                    n = i * B + b + 1
                    pe.wait_ge(s["un_done"], n * GT)
                    for h in range(CH):
                        for k in range(GT):
                            last = nc.tensor.transpose(pT[:, b, h, k * P:(k + 1) * P], un[:, b, k, h * P:(h + 1) * P], m.ident[:])
                    last.then_inc(s["t_ready"], 1)
                    pe.wait_ge(s["t_copied"], n)
                    for k in range(GT):
                        for h in range(CH):
                            last = nc.tensor.matmul(pd[:, b, k * HEADS:(k + 1) * HEADS], ug[:, b, h, k * P:(k + 1) * P],
                                                    wdt[:, h, :], start=h == 0, stop=h == CH - 1)
                    last.then_inc(s["d_ready"], 1)


def decays(nc, m, w):
    with ExitStack() as ctx:
        sb, ps, sem = setup(nc, ctx)
        NC_ = NT * HEADS
        raw = m.dt[:].rearrange("p t h -> p (t h)")
        a, e, u, d, z, l, lw, dA, cum = [sb("f_" + n, [P, NC_]) for n in ("a", "e", "u", "d", "z", "l", "lw", "dA", "cum")]
        neg = sb("f_neg", [P, HEADS])
        cumT = sb("f_cumT", [P, 2, P])
        pc, psf, pt, pT = [ps("f_" + n, [P, 512]) for n in ("pc", "psf", "pt", "pT")]
        names = ("loaded a0 a1 a2 a3 a4 v0 v1 v2 v3 v4 v5 v6 v7 v8 cum_ready cum_copied t_ready t_copied suf tot").split()
        s = {n: sem("f_" + n) for n in names}
        block = ctx.enter_context(nc.Block())
        dt, wdt, ecum, cums = [m.cs[:, :, k, :] for k in range(4)]
        tiles = lambda t: t.rearrange("p (t h) -> p t h", h=HEADS)

        @block.sync
        def _(sp):
            sp.dma_start(neg[:], w["A_log"].partition_broadcast(P)).then_inc(s["loaded"], 16)
            sp.wait_ge(s["t_copied"], 1)
            sp.dma_start(m.cum_dram.rearrange("(a p) t -> p a t", p=P), cumT[:]).then_inc(s["loaded"], 16)
            sp.wait_ge(s["loaded"], 32)

        @block.scalar
        def _(act):
            nc.scalar.activation(a[:], raw, ACT.Abs).then_inc(s["a0"], 1)
            act.wait_ge(s["a0"], 1)
            nc.scalar.activation(e[:], a[:], ACT.Exp, scale=-1.0).then_inc(s["a1"], 1)
            act.wait_ge(s["loaded"], 16)
            nc.scalar.activation(neg[:], neg[:], ACT.Exp).then_inc(s["a2"], 1)
            act.wait_ge(s["v0"], 1)
            nc.scalar.activation(lw[:], u[:], ACT.Ln).then_inc(s["a3"], 1)
            act.wait_ge(s["cum_ready"], 1)
            nc.scalar.activation(ecum, tiles(pc[:, 0:NC_]), ACT.Exp)
            nc.scalar.activation(m.etot[:].rearrange("p t h -> p (t h)"), pt[0:STATE, 0:NC_], ACT.Exp)
            nc.scalar.activation(z[:], psf[:, 0:NC_], ACT.Exp).then_inc(s["a4"], 1)

        @block.vector
        def _(dve):
            dve.wait_ge(s["a1"], 1)
            nc.vector.tensor_scalar_add(u[:], e[:], 1.0).then_inc(s["v0"], 1)
            dve.wait_ge(s["v0"], 1)
            nc.vector.tensor_scalar_add(d[:], u[:], -1.0).then_inc(s["v1"], 1)
            dve.wait_ge(s["v1"], 1)
            nc.vector.tensor_scalar(z[:], d[:], 0.0, None, ALU.is_equal).then_inc(s["v2"], 1)
            dve.wait_ge(s["v2"], 1)
            nc.vector.tensor_tensor(d[:], d[:], z[:], ALU.add).then_inc(s["v3"], 1)
            dve.wait_ge(s["v3"], 1)
            nc.vector.reciprocal(d[:], d[:]).then_inc(s["v4"], 1)
            nc.vector.tensor_tensor(z[:], z[:], e[:], ALU.mult).then_inc(s["v4"], 1)
            dve.wait_ge(s["v4"], 2)
            nc.vector.tensor_tensor(d[:], d[:], e[:], ALU.mult).then_inc(s["v5"], 1)
            dve.wait_ge(s["a3"], 1)
            dve.wait_ge(s["v5"], 1)
            nc.vector.tensor_tensor(l[:], lw[:], d[:], ALU.mult).then_inc(s["v6"], 1)
            dve.wait_ge(s["v6"], 1)
            nc.vector.tensor_tensor(l[:], l[:], z[:], ALU.add).then_inc(s["v6"], 1)
            dve.wait_ge(s["v6"], 2)
            nc.vector.scalar_tensor_tensor(out=dt, in0=tiles(raw), scalar=0.0, in1=tiles(l[:]),
                                           op0=ALU.max, op1=ALU.add).then_inc(s["v7"], 1)
            dve.wait_ge(s["a2"], 1)
            dve.wait_ge(s["v7"], 1)
            nc.vector.scalar_tensor_tensor(out=tiles(dA[:]), in0=dt, scalar=-1.0,
                                           in1=neg[:].unsqueeze(1).to_broadcast([P, NT, HEADS]),
                                           op0=ALU.mult, op1=ALU.mult).then_inc(s["v8"], 1)
            dve.wait_ge(s["cum_ready"], 1)
            dve.wait_ge(s["a4"], 1)
            nc.vector.tensor_copy(cum[:], pc[:, 0:NC_]).then_inc(s["cum_copied"], 1)
            nc.vector.tensor_copy(cums, tiles(pc[:, 0:NC_]))
            nc.vector.tensor_tensor(wdt, dt, tiles(z[:]), ALU.mult)
            dve.wait_ge(s["t_ready"], 1)
            nc.vector.tensor_copy(cumT[:].rearrange("p a t -> p (a t)"), pT[:, 0:2 * P]).then_inc(s["t_copied"], 1)

        @block.tensor
        def _(pe):
            pe.wait_ge(s["v8"], 1)
            nc.tensor.matmul(pc[:, 0:NC_], m.upto[:], dA[:], start=True, stop=True)
            nc.tensor.matmul(psf[:, 0:NC_], m.after[:], dA[:], start=True, stop=True)
            nc.tensor.matmul(pt[0:STATE, 0:NC_], m.ones[:, 0:STATE], dA[:], start=True, stop=True).then_inc(s["cum_ready"], 1)
            pe.wait_ge(s["cum_copied"], 1)
            for k in range(2):
                last = nc.tensor.transpose(pT[:, k * P:(k + 1) * P], cum[:, k * P:(k + 1) * P], m.ident[:])
            last.then_inc(s["t_ready"], 1)


def state_space(nc, m, w):
    with ExitStack() as ctx:
        sb, ps, sem = setup(nc, ctx)
        win = sb("g_win", [P, CH, DT0])
        wout = sb("g_wout", [P, INNER // P, C])
        wog = sb("g_wog", [P, B, INNER // P, C])
        dskip = sb("g_dskip", [P, HEADS])
        bb = sb("g_bb", [3, 2, DT0], BF16)
        ones3 = sb("g_ones3", [3, P], BF16)
        us = sb("g_us", [P, B, CH, P])
        cs = sb("g_cs", [P, B, 4, HEADS])
        et = sb("g_et", [STATE, B, HEADS])
        cumb = sb("g_cumb", [P, B, HEADS, P])
        bc = sb("g_bc", [P, B, 2 * STATE])
        bcT = sb("g_bcT", [STATE, B, 2, P])
        wide6 = sb("g_wide", [P, 6, B, INNER])
        xs, dtx, xw, xD, zr, y = [wide6[:, k] for k in range(6)]
        b3 = wide6[0:3].rearrange("p k b n -> p (k b n)")[:, 0:3 * DT0].rearrange("p (k n) -> p k n", k=3)
        th = sb("g_th", [P, INNER])
        gm = sb("g_gm", [P, B, P])
        dd = sb("g_dd", [P, HEADS, P])
        le = sb("g_le", [P, HEADS, P])
        mt = sb("g_mt", [P, HEADS, P])
        H = sb("g_H", [STATE, B, INNER])
        yT = sb("g_yT", [P, INNER // P, P])
        pz, px, pbc, pbt, py, pi, pst, pyT = [ps("g_p" + n, [P, 512]) for n in ("z", "x", "bc", "bt", "y", "i", "st", "yT")]
        po = pyT[:, 0:C]
        names = ("loaded w0 w1 w2 w3 w4 w5 ip_ready bc_copied xs_copied th_done bt_ready bt_copied g_ready gm_done "
                 "zr_done lcm_done le_done m_done dtx_done xw_done xD_done i_ready st_ready y_ready "
                 "t1_done t2_done y_done hs_done h_done yg_done yT_ready yT_copied o_ready x_done").split()
        s = {n: sem("g_" + n) for n in names}
        u_in, cs_in = [sem(f"g_u_in{b}") for b in range(B)], [sem(f"g_cs_in{b}") for b in range(B)]
        block = ctx.enter_context(nc.Block())
        heads = lambda t: t.rearrange("p (h d) -> p h d", h=HEADS)
        wide = lambda col, p=P: col.unsqueeze(2).to_broadcast([p, HEADS, HD])

        def jobs(eng, step):
            step(None, (0, 0), (0, 1))
            step((0, 0), (0, 1), (1, 0))
            with eng.Fori(1, NTB - 1) as i:
                step((i - 1, 1), (i, 0), (i, 1))
                step((i, 0), (i, 1), (i + 1, 0))
            i = NTB - 1
            step((i - 1, 1), (i, 0), (i, 1))
            step((i, 0), (i, 1), None)
            step((i, 1), None, None)

        def num(job):
            return job[0] * B + job[1]

        @block.sync
        def _(sp):
            for dst, src in ((win, w["W_in"][:, 0:DT0].rearrange("(h p) n -> p h n", p=P)),
                             (wout, w["W_out"].rearrange("(h p) n -> p h n", p=P)),
                             (dskip, w["D_skip"].partition_broadcast(P))):
                sp.dma_start(dst[:], src).then_inc(s["loaded"], 16)
            sp.dma_start(b3[:, 0], w["b_in"][0:DT0].partition_broadcast(3)).then_inc(s["loaded"], 16)

            def stage(i, b):
                n = i * B + b
                t = b * NTB + i
                if not (isinstance(i, int) and i == 0):
                    sp.wait_ge(s["ip_ready"], n - 1)
                sp.dma_start(us[:, b], m.uT[:, :, bass.ds(t * P, P)]).then_inc(u_in[b], 16)
                if not (isinstance(i, int) and i == 0):
                    sp.wait_ge(s["lcm_done"], (n - 1) * HEADS)
                    sp.wait_ge(s["t1_done"], n - 1)
                    sp.wait_ge(s["hs_done"], n - 1)
                    sp.wait_ge(s["xw_done"], n - 1)
                sp.dma_start(cs[:, b], m.cs[:, bass.ds(t, 1)].squeeze(1)).then_inc(cs_in[b], 16)
                sp.dma_start(et[:, b], m.etot[:, bass.ds(t, 1)].squeeze(1)).then_inc(cs_in[b], 16)
                sp.dma_start(cumb[:, b].rearrange("p h t -> p (h t)"),
                             m.cum_dram[bass.ds(t * HEADS, HEADS), :].rearrange("h t -> (h t)").partition_broadcast(P)).then_inc(cs_in[b], 16)

            stage(0, 0)
            stage(0, 1)
            with sp.Fori(1, NTB) as i:
                stage(i, 0)
                stage(i, 1)

        @block.gpsimd
        def _(pool):
            def products(job):
                i, b = job
                n = num(job)
                pool.wait_ge(s["xs_copied"], n + 1)
                pool.wait_ge(cs_in[b], (i + 1) * 48)
                pool.wait_ge(s["y_ready"], least(n - 1))
                nc.gpsimd.tensor_tensor(heads(dtx[:, b]), heads(xs[:, b]), wide(cs[:, b, 0]), ALU.mult).then_inc(s["dtx_done"], 1)
                pool.wait_ge(s["st_ready"], least(n - 1))
                nc.gpsimd.tensor_tensor(heads(xw[:, b]), heads(xs[:, b]), wide(cs[:, b, 1]), ALU.mult).then_inc(s["xw_done"], 1)
                pool.wait_ge(s["t2_done"], least(n - 1))
                nc.gpsimd.tensor_tensor(heads(xD[:, b]), heads(xs[:, b]), wide(dskip[:]), ALU.mult).then_inc(s["xD_done"], 1)

            def gate(job):
                i, b = job
                n = num(job)
                pool.wait_ge(s["y_done"], n + 1)
                nc.gpsimd.tensor_tensor(y[:, b], y[:, b], zr[:, b], ALU.mult).then_inc(s["yg_done"], 1)

            pool.wait_ge(s["loaded"], 64)
            products((0, 0))

            def step(prev, cur, nxt):
                if nxt:
                    products(nxt)
                if cur:
                    gate(cur)
            jobs(pool, step)

        @block.scalar
        def _(act):
            def evacuate(job):
                i, b = job
                n = num(job)
                act.wait_ge(s["ip_ready"], n + 1)
                act.wait_ge(s["st_ready"], least(n - 1))
                nc.scalar.copy(bc[:, b], pbc[:, 0:2 * STATE]).then_inc(s["bc_copied"], 1)
                act.wait_ge(s["xD_done"], least(n - 1))
                nc.scalar.copy(xs[:, b], px[:]).then_inc(s["xs_copied"], 1)
                act.wait_ge(s["zr_done"], n)
                nc.scalar.activation(th[:], pz[:], ACT.Tanh, scale=0.5).then_inc(s["th_done"], 1)
                act.wait_ge(s["bt_ready"], n + 1)
                act.wait_ge(s["i_ready"], least(n - 1))
                nc.scalar.copy(bcT[:, b].rearrange("p a t -> p (a t)"), pbt[0:STATE, 0:2 * P]).then_inc(s["bt_copied"], 1)

            evacuate((0, 0))

            def step(prev, cur, nxt):
                if cur:
                    n = num(cur)
                    act.wait_ge(s["lcm_done"], (n + 1) * HEADS)
                    act.wait_ge(s["m_done"], n)
                    nc.scalar.activation(le[:], dd[:], ACT.Exp).then_inc(s["le_done"], 1)
                if nxt:
                    evacuate(nxt)
                if prev:
                    n = num(prev)
                    act.wait_ge(s["yT_ready"], n + 1)
                    act.wait_ge(s["o_ready"], n)
                    nc.scalar.copy(yT[:].rearrange("p k t -> p (k t)"), pyT[:]).then_inc(s["yT_copied"], 1)
            jobs(act, step)

        @block.vector
        def _(dve):
            dve.wait_ge(s["loaded"], 64)
            nc.vector.memset(ones3[:], 1.0)
            nc.vector.memset(H[:], 0.0)
            for b in range(B):
                nc.vector.scalar_tensor_tensor(out=wog[:, b], in0=wout[:], scalar=0.5, in1=over(m.mod[:, b, GA, :], INNER // P),
                                               op0=ALU.mult, op1=ALU.mult)
            for k in range(2):
                nc.vector.tensor_copy(bb[:, k], b3[:, k]).then_inc(s["w0"], 1)
                dve.wait_ge(s["w0"], k + 1)
                nc.vector.tensor_tensor(b3[:, k + 1], b3[:, k], bb[:, k], ALU.subtract).then_inc(s["w1"], 1)
                dve.wait_ge(s["w1"], k + 1)
            i3 = m.ident[0:3, :]
            nc.vector.tensor_scalar(b3[:, 0], bb[:, 0], i3[:, 0:1], None, ALU.mult).then_inc(s["w2"], 1)
            dve.wait_ge(s["w2"], 1)
            nc.vector.scalar_tensor_tensor(out=b3[:, 0], in0=bb[:, 1], scalar=i3[:, 1:2], in1=b3[:, 0],
                                           op0=ALU.mult, op1=ALU.add).then_inc(s["w3"], 1)
            dve.wait_ge(s["w3"], 1)
            nc.vector.scalar_tensor_tensor(out=bb[:, 0], in0=b3[:, 2], scalar=i3[:, 2:3], in1=b3[:, 0],
                                           op0=ALU.mult, op1=ALU.add).then_inc(s["w4"], 1)

            def gates(job):
                i, b = job
                n = num(job)
                dve.wait_ge(s["th_done"], n + 1)
                dve.wait_ge(s["yg_done"], least(n - 1))
                nc.vector.scalar_tensor_tensor(out=zr[:, b], in0=th[:], scalar=1.0, in1=pz[:],
                                               op0=ALU.add, op1=ALU.mult).then_inc(s["zr_done"], 1)
                dve.wait_ge(s["g_ready"], n + 1)
                nc.vector.tensor_tensor(gm[:, b], pbc[:, 2 * P:3 * P], m.upto[:], ALU.mult).then_inc(s["gm_done"], 1)

            def decay(job):
                i, b = job
                n = num(job)
                dve.wait_ge(cs_in[b], (i + 1) * 48)
                dve.wait_ge(s["le_done"], n)
                for h in range(HEADS):
                    nc.vector.tensor_scalar(dd[:, h, :], cumb[:, b, h, :], cs[:, b, 3, h:h + 1], 0.0,
                                            ALU.subtract, ALU.min).then_inc(s["lcm_done"], 1)

            def body(job):
                i, b = job
                n = num(job)
                dve.wait_ge(s["le_done"], n + 1)
                dve.wait_ge(s["gm_done"], n + 1)
                dve.wait_ge(s["y_ready"], n)
                nc.vector.tensor_tensor(mt[:], le[:], over(gm[:, b], HEADS), ALU.mult).then_inc(s["m_done"], 1)
                dve.wait_ge(s["i_ready"], n + 1)
                nc.vector.tensor_tensor(heads(y[:, b]), heads(pi[:]), wide(cs[:, b, 2]), ALU.mult).then_inc(s["t1_done"], 1)
                dve.wait_ge(s["h_done"], n)
                nc.vector.tensor_tensor(heads(H[:, b]), heads(H[:, b]), wide(et[:, b], STATE), ALU.mult).then_inc(s["hs_done"], 1)
                dve.wait_ge(s["hs_done"], n + 1)
                dve.wait_ge(s["st_ready"], n + 1)
                nc.vector.tensor_tensor(H[:, b], H[:, b], pst[0:STATE, :], ALU.add).then_inc(s["h_done"], 1)
                dve.wait_ge(s["y_ready"], n + 1)
                dve.wait_ge(s["xD_done"], n + 1)
                nc.vector.tensor_tensor(xD[:, b], py[:], xD[:, b], ALU.add).then_inc(s["t2_done"], 1)
                dve.wait_ge(s["t2_done"], n + 1)
                nc.vector.tensor_tensor(y[:, b], y[:, b], xD[:, b], ALU.add).then_inc(s["y_done"], 1)

            def finish(job):
                i, b = job
                n = num(job)
                t = bass.ds(b * NTB + i, 1)
                xt = m.x[:, t, :].squeeze(1)
                dve.wait_ge(s["o_ready"], n + 1)
                nc.vector.tensor_tensor(xt, xt, po, ALU.add).then_inc(s["x_done"], 1)
                dve.wait_ge(s["x_done"], n + 1)
                nc.vector.bn_stats(m.st[:, t, :].squeeze(1), xt)

            gates((0, 0))

            def step(prev, cur, nxt):
                if cur:
                    decay(cur)
                    body(cur)
                if prev:
                    finish(prev)
                if nxt:
                    gates(nxt)
            jobs(dve, step)

        @block.tensor
        def _(pe):
            pe.wait_ge(s["w4"], 1)

            def project(job):
                i, b = job
                n = num(job)
                pe.wait_ge(u_in[b], (i + 1) * 16)
                pe.wait_ge(s["gm_done"], n)
                pe.wait_ge(s["zr_done"], n)
                pe.wait_ge(s["xs_copied"], n)
                for dst, o, width in ((pbc, ZX, 2 * STATE), (px, INNER, INNER), (pz, 0, INNER)):
                    for k in range(CH):
                        nc.tensor.matmul(dst[:, 0:width], us[:, b, k, :], win[:, k, o:o + width], start=k == 0, stop=False)
                    last = nc.tensor.matmul(dst[:, 0:width], ones3[:], bb[:, 0, o:o + width], start=False, stop=True)
                last.then_inc(s["ip_ready"], 1)

            def correlate(job):
                i, b = job
                n = num(job)
                for k in range(2):
                    last = nc.tensor.transpose(pbt[0:STATE, k * P:(k + 1) * P], bc[:, b, k * STATE:(k + 1) * STATE], m.ident[:])
                last.then_inc(s["bt_ready"], 1)
                pe.wait_ge(s["bt_copied"], n + 1)
                nc.tensor.matmul(pbc[:, 2 * P:3 * P], bcT[:, b, 0, :], bcT[:, b, 1, :], start=True, stop=True).then_inc(s["g_ready"], 1)

            def await_bc(job):
                pe.wait_ge(s["bc_copied"], num(job) + 1)
                pe.wait_ge(s["bt_copied"], num(job))

            project((0, 0))
            await_bc((0, 0))
            correlate((0, 0))

            def step(prev, cur, nxt):
                if nxt:
                    project(nxt)
                if cur:
                    i, b = cur
                    n = num(cur)
                    pe.wait_ge(s["h_done"], n)
                    pe.wait_ge(s["t1_done"], n)
                    nc.tensor.matmul(pi[:], bcT[:, b, 1, :], H[:, b], start=True, stop=True).then_inc(s["i_ready"], 1)
                    pe.wait_ge(s["xw_done"], n + 1)
                    if nxt:
                        await_bc(nxt)
                    nc.tensor.matmul(pst[0:STATE, :], bc[:, b, 0:STATE], xw[:, b], start=True, stop=True).then_inc(s["st_ready"], 1)
                if nxt:
                    correlate(nxt)
                if cur:
                    pe.wait_ge(s["m_done"], n + 1)
                    pe.wait_ge(s["dtx_done"], n + 1)
                    pe.wait_ge(s["t2_done"], n)
                    for h in range(HEADS):
                        last = nc.tensor.matmul(py[:, h * HD:(h + 1) * HD], mt[:, h, :], dtx[:, b, h * HD:(h + 1) * HD],
                                                start=True, stop=True)
                    last.then_inc(s["y_ready"], 1)
                if prev:
                    i, b = prev
                    n = num(prev)
                    pe.wait_ge(s["yg_done"], n + 1)
                    pe.wait_ge(s["x_done"], n)
                    for k in range(INNER // P):
                        last = nc.tensor.transpose(pyT[:, k * P:(k + 1) * P], y[:, b, k * P:(k + 1) * P], m.ident[:])
                    last.then_inc(s["yT_ready"], 1)
                    pe.wait_ge(s["yT_copied"], n + 1)
                    for k in range(INNER // P):
                        last = nc.tensor.matmul(po, yT[:, k, :], wog[:, b, k, :], start=k == 0, stop=k == INNER // P - 1)
                    last.then_inc(s["o_ready"], 1)
            jobs(pe, step)


EX = 16
FE = 512
FT = FE // P
CAP = T * 2 // EX
ROW = C + EX
RX = B * EX
BITS = 30
RADIX = 16


def routing_scores(nc, m, w):
    with ExitStack() as ctx:
        sb, ps, sem = setup(nc, ctx)
        hx = sb("h_hx", [P, B, GT, ROW])
        hT = sb("h_hT", [P, B, CH, GW])
        gw = sb("h_gw", [P, CH, EX])
        mx, sm = sb("h_mx", [P, B, GT]), sb("h_sm", [P, B, GT])
        lg, ex = sb("h_lg", [P, B, GT, EX]), sb("h_ex", [P, B, GT, EX])
        by_tile = sb("h_by_tile", [P, NTB, B, EX])
        pT = ps("h_pT", [P, 2, CH, GW])
        pg = ps("h_pg", [P, 2, 512])
        pS = ps("h_pS", [RX, 2, 512])
        names = ("loaded stat0 stat1 stat2 stat3 stat4 normed scaled shifted t_ready t_copied g_ready mx_done lg_done ex_done "
                 "sm_done rs_done sc_done bt_done s_ready s_copied").split()
        s = {n: sem("h_" + n) for n in names}
        rows_out, hT_out = [sem(f"h_rows{b}") for b in range(B)], [sem(f"h_hT_out{b}") for b in range(B)]
        block = ctx.enter_context(nc.Block())
        st_vector, st_gpsimd = finish_stats(nc, [s[f"stat{i}"] for i in range(5)], m, 0, NT)

        def groups(eng, group):
            group(0, 0)
            group(0, 1)
            with eng.Fori(1, NG) as i:
                group(i, 0)
                group(i, 1)

        @block.sync
        def _(sp):
            sp.dma_start(gw[:], w["gate_wT"].rearrange("(h p) n -> p h n", p=P)).then_inc(s["loaded"], 16)
            with sp.Fori(0, NG) as i:
                for b in range(B):
                    n = i * B + b
                    sp.wait_ge(s["t_copied"], n + 1)
                    sp.dma_start(m.hT[:, :, bass.ds(b * T + i * GW, GW)], hT[:, b]).then_inc(hT_out[b], 16)
                    sp.wait_ge(s["sc_done"], n + 1)
                    sp.dma_start(m.rows.rearrange("(t p) c -> p t c", p=P)[:, bass.ds(b * NTB + i * GT, GT), :],
                                 hx[:, b]).then_inc(rows_out[b], 16)
            for b in range(B):
                sp.wait_ge(hT_out[b], 16 * NG)
                sp.wait_ge(rows_out[b], 16 * NG)

        @block.gpsimd
        def _(pool):
            st_gpsimd()
            with pool.Fori(0, NG) as i:
                for b in range(B):
                    n = i * B + b + 1
                    hb = hx[:, b, :, 0:C]
                    pool.wait_ge(s["normed"], n * GT)
                    nc.gpsimd.tensor_tensor(hb, hb, over(m.mod[:, b, CB, :], GT), ALU.mult).then_inc(s["scaled"], 1)
                    pool.wait_ge(s["scaled"], n)
                    nc.gpsimd.tensor_tensor(hb, hb, over(m.mod[:, b, SB, :], GT), ALU.add).then_inc(s["shifted"], 1)

        @block.vector
        def _(dve):
            st_vector()
            dve.wait_ge(s["stat4"], 1)

            def normalise(i, b):
                for k in range(GT):
                    t = bass.ds(b * NTB + i * GT + k, 1)
                    nc.vector.tensor_scalar(hx[:, b, k, 0:C], m.x[:, t, :].squeeze(1), m.mean[:, t], m.rstd[:, t],
                                            ALU.subtract, ALU.mult).then_inc(s["normed"], 1)

            def group(i, b, first=False, last=False):
                n = i * B + b + 1
                if not last:
                    if not first:
                        dve.wait_ge(rows_out[1 - b], 16 * (i - 1 + b) + 16)
                    normalise(i + b, 1 - b)
                dve.wait_ge(s["g_ready"], n)
                pl = pg[:, b, 0:GT * EX].rearrange("p (t e) -> p t e", e=EX)
                col = lambda t: t[:, b].unsqueeze(2).to_broadcast([P, GT, EX])
                nc.vector.tensor_reduce(mx[:, b], pl, AX, ALU.max).then_inc(s["mx_done"], 1)
                dve.wait_ge(s["mx_done"], n)
                nc.vector.tensor_tensor(lg[:, b], pl, col(mx), ALU.subtract).then_inc(s["lg_done"], 1)
                dve.wait_ge(s["ex_done"], n)
                nc.vector.tensor_reduce(sm[:, b], ex[:, b], AX, ALU.add).then_inc(s["sm_done"], 1)
                dve.wait_ge(s["sm_done"], n)
                nc.vector.reciprocal(sm[:, b], sm[:, b]).then_inc(s["rs_done"], 1)
                dve.wait_ge(s["rs_done"], n)
                nc.vector.tensor_tensor(hx[:, b, :, C:ROW], ex[:, b], col(sm), ALU.mult).then_inc(s["sc_done"], 1)
                nc.vector.tensor_tensor(by_tile[:, bass.ds(i * GT, GT), b, :], ex[:, b], col(sm), ALU.mult).then_inc(s["bt_done"], 1)

            normalise(0, 0)
            group(0, 0, first=True)
            group(0, 1)
            with dve.Fori(1, NG - 1) as i:
                group(i, 0)
                group(i, 1)
            group(NG - 1, 0)
            group(NG - 1, 1, last=True)
            for g in range(NG):
                dve.wait_ge(s["s_ready"], g + 1)
                nc.vector.tensor_copy(m.sc[:, g * GW:(g + 1) * GW], pS[:, g % 2, :]).then_inc(s["s_copied"], 1)

        @block.scalar
        def _(act):
            def group(i, b):
                n = i * B + b + 1
                act.wait_ge(s["t_ready"], n)
                if not isinstance(i, int):
                    act.wait_ge(hT_out[b], 16 * i)
                    act.wait_ge(s["g_ready"], n - 2)
                nc.scalar.copy(hT[:, b], pT[:, b]).then_inc(s["t_copied"], 1)
                act.wait_ge(s["lg_done"], n)
                nc.scalar.activation(ex[:, b], lg[:, b], ACT.Exp).then_inc(s["ex_done"], 1)
            groups(act, group)

        @block.tensor
        def _(pe):
            pe.wait_ge(s["loaded"], 16)
            with pe.Fori(0, NG) as i:
                for b in range(B):
                    n = i * B + b + 1
                    pe.wait_ge(s["shifted"], n)
                    for h in range(CH):
                        for k in range(GT):
                            last = nc.tensor.transpose(pT[:, b, h, k * P:(k + 1) * P], hx[:, b, k, h * P:(h + 1) * P], m.ident[:])
                    last.then_inc(s["t_ready"], 1)
                    pe.wait_ge(s["t_copied"], n)
                    for k in range(GT):
                        for h in range(CH):
                            last = nc.tensor.matmul(pg[:, b, k * EX:(k + 1) * EX], hT[:, b, h, k * P:(k + 1) * P],
                                                    gw[:, h, :], start=h == 0, stop=h == CH - 1)
                    last.then_inc(s["g_ready"], 1)
            pe.wait_ge(s["bt_done"], NG * B)
            for g in range(NG):
                pe.wait_ge(s["s_copied"], max(g - 1, 0))
                for k in range(GT):
                    last = nc.tensor.transpose(pS[:, g % 2, k * P:(k + 1) * P],
                                               by_tile[:, g * GT + k].rearrange("p b e -> p (b e)"), m.ident[:])
                last.then_inc(s["s_ready"], 1)


def shared_and_choice(nc, m, w, out):
    with ExitStack() as ctx:
        sb, ps, sem = setup(nc, ctx)
        wg, wu, wd = sb("i_wg", [P, CH, FE]), sb("i_wu", [P, CH, FE]), sb("i_wd", [P, FT, C])
        act_g = sb("i_act_g", [P, 2, GW])
        hid = sb("i_hid", [P, B, FT, GW])
        ob = sb("i_ob", [P, B, GT, C])
        prefix, cand, add = [sb("i_" + n, [RX, 1], I32) for n in ("prefix", "cand", "add")]
        bits = sb("i_bits", [RX, BITS + 2], I32)
        cnt, room = sb("i_cnt", [RX, 1]), sb("i_room", [RX, 1])
        junk, eq, rank = [sb("i_" + n, [RX, T]) for n in ("junk", "eq", "rank")]
        pg, pu, po = ps("i_pg", [P, 2, GW]), ps("i_pu", [P, 2, GW]), ps("i_po", [P, GT, C])
        names = ("loaded gu_ready gelu_done hid_done o_ready ga_done ob_done bit0 bits cand cnt add prefix c0 c1 c2 c3 c4 c5 c6 c7").split()
        s = {n: sem("i_" + n) for n in names}
        stored = [sem(f"i_stored{b}") for b in range(B)]
        block = ctx.enter_context(nc.Block())
        NQ = NG * B
        PER = -(-BITS // NQ)

        @block.sync
        def _(sp):
            for dst, src in ((wg, w["Ws_gT"]), (wu, w["Ws_uT"]), (wd, w["Ws_dT"])):
                sp.dma_start(dst[:], src.rearrange("(h p) n -> p h n", p=P)).then_inc(s["loaded"], 16)
            with sp.Fori(0, NG) as i:
                for b in range(B):
                    sp.wait_ge(s["ob_done"], i * B + b + 1)
                    sp.dma_start(out.rearrange("(t p) c -> p t c", p=P)[:, bass.ds(b * NTB + i * GT, GT), :],
                                 ob[:, b]).then_inc(stored[b], 16)
            for b in range(B):
                sp.wait_ge(stored[b], 16 * NG)

        @block.scalar
        def _(act):
            with act.Fori(0, NG) as i:
                for b in range(B):
                    for f in range(FT):
                        n = (i * B + b) * FT + f
                        act.wait_ge(s["gu_ready"], n + 1)
                        act.wait_ge(s["hid_done"], n - 1) if (f >= 2) else act.wait_ge(s["hid_done"], (i * B + b) * FT)
                        nc.scalar.activation(act_g[:, f % 2], pg[:, f % 2], ACT.Gelu).then_inc(s["gelu_done"], 1)

        @block.tensor
        def _(pe):
            pe.wait_ge(s["loaded"], 48)
            with pe.Fori(0, NG) as i:
                for b in range(B):
                    g = i * B + b
                    for f in range(FT):
                        n = g * FT + f
                        if f >= 2:
                            pe.wait_ge(s["hid_done"], n - 1)
                        else:
                            pe.wait_ge(s["hid_done"], g * FT)
                        for dst, wt in ((pg, wg), (pu, wu)):
                            for k in range(CH):
                                last = nc.tensor.matmul(dst[:, f % 2], wt[:, k, f * P:(f + 1) * P],
                                                        m.hT[:, k, bass.ds(b * T + i * GW, GW)], start=k == 0, stop=k == CH - 1)
                        last.then_inc(s["gu_ready"], 1)
                    pe.wait_ge(s["hid_done"], (g + 1) * FT)
                    pe.wait_ge(s["ga_done"], g)
                    for t in range(GT):
                        for f in range(FT):
                            last = nc.tensor.matmul(po[:, t], hid[:, b, f, t * P:(t + 1) * P], wd[:, f, :],
                                                    start=f == 0, stop=f == FT - 1)
                    last.then_inc(s["o_ready"], 1)

        @block.vector
        def _(dve):
            v = nc.vector
            prefix_f, cand_f = prefix[:].bitcast(F32), cand[:].bitcast(F32)
            v.memset(prefix[:], 0)
            v.memset(bits[:, BITS:], 0)
            v.memset(bits[:, 0:1], 1 << (BITS - 1)).then_inc(s["bit0"], 1)
            dve.wait_ge(s["bit0"], 1)
            for k in range(1, BITS):
                last = v.tensor_scalar(bits[:, k:k + 1], bits[:, 0:1], k, None, ALU.logical_shift_right)
            last.then_inc(s["bits"], 1)
            dve.wait_ge(s["bits"], 1)

            def search(j):
                bit = bits[:, bass.ds(j, 1)]
                dve.wait_ge(s["prefix"], j)
                v.tensor_tensor(cand[:], prefix[:], bit, ALU.bitwise_or).then_inc(s["cand"], 1)
                dve.wait_ge(s["cand"], j + 1)
                v.tensor_scalar(junk[:], m.sc[:], cand_f, 0.0, ALU.is_ge, ALU.add, accum_out=cnt[:]).then_inc(s["cnt"], 1)
                dve.wait_ge(s["cnt"], j + 1)
                v.scalar_tensor_tensor(out=add[:], in0=cnt[:], scalar=float(CAP), in1=bit, op0=ALU.is_ge, op1=ALU.mult).then_inc(s["add"], 1)
                dve.wait_ge(s["add"], j + 1)
                v.tensor_tensor(prefix[:], prefix[:], add[:], ALU.bitwise_or).then_inc(s["prefix"], 1)

            with dve.Fori(0, NG) as i:
                for b in range(B):
                    g = i * B + b
                    for f in range(FT):
                        n = g * FT + f
                        dve.wait_ge(s["gelu_done"], n + 1)
                        dve.wait_ge(s["o_ready"], g)
                        v.tensor_tensor(hid[:, b, f], act_g[:, f % 2], pu[:, f % 2], ALU.mult).then_inc(s["hid_done"], 1)
                        if f < PER:
                            search(g * PER + f)
                    dve.wait_ge(s["o_ready"], g + 1)
                    dve.wait_ge(stored[b], 16 * i)
                    v.tensor_tensor(ob[:, b], po[:], over(m.mod[:, b, GB, :], GT), ALU.mult).then_inc(s["ga_done"], 1)
                    dve.wait_ge(s["ga_done"], g + 1)
                    v.tensor_tensor(ob[:, b], ob[:, b], m.x[:, bass.ds(b * NTB + i * GT, GT), :], ALU.add).then_inc(s["ob_done"], 1)
            dve.wait_ge(s["prefix"], PER * NQ)
            v.tensor_scalar(junk[:], m.sc[:], prefix_f, 0.0, ALU.is_gt, ALU.add, accum_out=cnt[:]).then_inc(s["c0"], 1)
            v.tensor_scalar(eq[:], m.sc[:], prefix_f, None, ALU.is_equal).then_inc(s["c1"], 1)
            dve.wait_ge(s["c1"], 1)
            v.tensor_tensor_scan(rank[:], eq[:], eq[:], 0.0, ALU.add, ALU.bypass).then_inc(s["c2"], 1)
            dve.wait_ge(s["c0"], 1)
            v.tensor_scalar(room[:], cnt[:], -1.0, float(CAP), ALU.mult, ALU.add).then_inc(s["c3"], 1)
            dve.wait_ge(s["c2"], 1)
            dve.wait_ge(s["c3"], 1)
            v.scalar_tensor_tensor(out=eq[:], in0=rank[:], scalar=room[:], in1=eq[:], op0=ALU.is_le, op1=ALU.mult).then_inc(s["c4"], 1)
            dve.wait_ge(s["c4"], 1)
            v.tensor_tensor(eq[:], eq[:], junk[:], ALU.add).then_inc(s["c5"], 1)
            dve.wait_ge(s["c5"], 1)
            v.tensor_tensor_scan(rank[:], eq[:], eq[:], 0.0, ALU.add, ALU.bypass).then_inc(s["c6"], 1)
            dve.wait_ge(s["c6"], 1)
            v.tensor_tensor(m.place[:], rank[:], eq[:], ALU.mult)


def index_lists(nc, m):
    with ExitStack() as ctx:
        sb, ps, sem = setup(nc, ctx)
        NP = NTB * RX
        w = sb("j_w", [P, NP], I32)
        upper, lower = sb("j_upper", [P, NP], I32), sb("j_lower", [P, NP], I32)
        io = sb("j_io", [P, RADIX])
        tid, lid = sb("j_tid", [P, NT]), sb("j_lid", [P, 1])
        A = sb("j_A", [P, NTB, RX, RADIX], BF16)
        R = sb("j_R", [P, NTB, RX, 2, RADIX], BF16)
        dmask = sb("j_dmask", [P, 8])
        mk = sb("j_mk", [P, 4, 8, 2 * RADIX])
        red = sb("j_red", [P, 4, 2 * RADIX])
        ix = sb("j_ix", [P, 4, RADIX])
        rows = sb("j_rows", [2 * RX, P])
        pW, pI, pX = ps("j_pW", [P, 512]), ps("j_pI", [P, 4, 512]), ps("j_pX", [P, 512])
        names = "io w_ready w_done ul A0 B0 R0 R1 i_ready mk red ix rows_in x_ready dm".split()
        s = {n: sem("j_" + n) for n in names}
        block = ctx.enter_context(nc.Block())

        @block.gpsimd
        def _(pool):
            g = nc.gpsimd
            g.iota(io[:], pattern=[[1, RADIX]], base=0, channel_multiplier=0, allow_small_or_imprecise_dtypes=True).then_inc(s["io"], 1)
            g.iota(tid[:], pattern=[[1, NT]], base=0, channel_multiplier=0, allow_small_or_imprecise_dtypes=True).then_inc(s["io"], 1)
            g.iota(lid[:], pattern=[[0, 1]], base=0, channel_multiplier=1, allow_small_or_imprecise_dtypes=True).then_inc(s["io"], 1)
            g.memset(dmask[:], 1.0).then_inc(s["dm"], 1)
            pool.wait_ge(s["dm"], 1)
            g.affine_select(out=dmask[:], in_=dmask[:], compare_op=ALU.is_ge, fill=0.0, base=0,
                            pattern=[[-RADIX, 8]], channel_multiplier=1).then_inc(s["dm"], 1)
            pool.wait_ge(s["dm"], 2)
            g.affine_select(out=dmask[:], in_=dmask[:], compare_op=ALU.is_ge, fill=0.0, base=RADIX - 1,
                            pattern=[[RADIX, 8]], channel_multiplier=-1).then_inc(s["dm"], 1)

        @block.tensor
        def _(pe):
            for t in range(NTB):
                last = nc.tensor.transpose(pW[:, t * RX:(t + 1) * RX], m.place[:, t * P:(t + 1) * P], m.ident[0:RX, 0:RX])
            last.then_inc(s["w_ready"], 1)
            pe.wait_ge(s["R1"], 2 * B)
            for q in range(4):
                for t in range(NTB):
                    last = nc.tensor.matmul(pI[:, q, 0:8 * 2 * RADIX], A[:, t, q * 8:(q + 1) * 8, :].rearrange("p e a -> p (e a)"),
                                            R[:, t, q * 8:(q + 1) * 8].rearrange("p e k b -> p (e k b)"),
                                            start=t == 0, stop=t == NTB - 1)
            last.then_inc(s["i_ready"], 1)
            pe.wait_ge(s["rows_in"], 64)
            nc.tensor.transpose(pX[:, 0:2 * RX], rows[:], m.ident[0:2 * RX, 0:2 * RX]).then_inc(s["x_ready"], 1)

        @block.sync
        def _(sp):
            sp.wait_ge(s["ix"], 1)
            for q in range(4):
                sp.dma_start(rows[q * 16:(q + 1) * 16, :].rearrange("r (a b) -> r a b", a=8), ix[:, q, :]).then_inc(s["rows_in"], 16)

        @block.vector
        def _(dve):
            v = nc.vector
            dve.wait_ge(s["w_ready"], 1)
            v.tensor_scalar(w[:], pW[:], -1.0, None, ALU.add).then_inc(s["w_done"], 1)
            dve.wait_ge(s["w_done"], 1)
            v.tensor_scalar(upper[:], w[:], 4, None, ALU.arith_shift_right).then_inc(s["ul"], 1)
            v.tensor_scalar(lower[:], w[:], RADIX - 1, None, ALU.bitwise_and).then_inc(s["ul"], 1)
            dve.wait_ge(s["ul"], 2)
            dve.wait_ge(s["io"], 3)
            digits = io[:].unsqueeze(1).to_broadcast([P, NP, RADIX])
            v.tensor_tensor(A[:].rearrange("p t e a -> p (t e) a"), upper[:].unsqueeze(2).to_broadcast([P, NP, RADIX]),
                            digits, ALU.is_equal).then_inc(s["A0"], 1)
            one = R[:, :, :, 1, :].rearrange("p t e b -> p (t e) b")
            v.tensor_tensor(one, lower[:].unsqueeze(2).to_broadcast([P, NP, RADIX]), digits, ALU.is_equal).then_inc(s["B0"], 1)
            dve.wait_ge(s["B0"], 1)
            dve.wait_ge(s["A0"], 1)
            for b in range(B):
                e = slice(b * EX, (b + 1) * EX)
                tiles = tid[:, b * NTB:(b + 1) * NTB].unsqueeze(2).unsqueeze(3).to_broadcast([P, NTB, EX, RADIX])
                v.tensor_tensor(R[:, :, e, 0, :], R[:, :, e, 1, :], tiles, ALU.mult).then_inc(s["R0"], 1)
                dve.wait_ge(s["R0"], b + 1)
            for b in range(B):
                e = slice(b * EX, (b + 1) * EX)
                v.tensor_scalar(R[:, :, e, 1, :], R[:, :, e, 1, :], lid[:], None, ALU.mult).then_inc(s["R1"], 2)
            dve.wait_ge(s["i_ready"], 1)
            dve.wait_ge(s["dm"], 3)
            for q in range(4):
                v.tensor_tensor(mk[:, q], pI[:, q, 0:8 * 2 * RADIX].rearrange("p (e k) -> p e k", e=8),
                                dmask[:].unsqueeze(2).to_broadcast([P, 8, 2 * RADIX]), ALU.mult).then_inc(s["mk"], 1)
            dve.wait_ge(s["mk"], 4)
            v.tensor_reduce(red[:], mk[:].rearrange("p q e k -> p q k e"), AX, ALU.add).then_inc(s["red"], 1)
            dve.wait_ge(s["red"], 1)
            v.scalar_tensor_tensor(out=ix[:], in0=red[:, :, 0:RADIX], scalar=float(P), in1=red[:, :, RADIX:],
                                   op0=ALU.mult, op1=ALU.add).then_inc(s["ix"], 1)
            dve.wait_ge(s["x_ready"], 1)
            v.tensor_copy(m.idx[:], pX[:, 0:2 * RX])


def experts(nc, m, w, out):
    with ExitStack() as ctx:
        sb, ps, sem = setup(nc, ctx)
        NTOK = B * CAP // P
        xe = sb("k_xe", [P, 2, NTOK, ROW])
        xT = sb("k_xT", [P, 2, CH, GW])
        wg, wu, wd = sb("k_wg", [P, 2, CH, FE]), sb("k_wu", [P, 2, CH, FE]), sb("k_wd", [P, 2, FT, C])
        act_g = sb("k_act_g", [P, 2, GW])
        hid = sb("k_hid", [P, FT, GW])
        eo = sb("k_eo", [P, 2, NTOK, C])
        pg, pu, po, pT = ps("k_pg", [P, 2, GW]), ps("k_pu", [P, 2, GW]), ps("k_po", [P, NTOK, C]), ps("k_pT", [P, CH, GW])
        names = "t_ready t_copied gu_ready gelu_done hid_done o_ready eo_done".split()
        s = {n: sem("k_" + n) for n in names}
        gathered, w_in, added = [[sem(f"k_{n}{k}") for k in range(2)] for n in ("gathered", "w_in", "added")]
        block = ctx.enter_context(nc.Block())

        def column(e, t):
            b, half = divmod(t, 2)
            return m.idx[:, (b * EX + e) * 2 + half:(b * EX + e) * 2 + half + 1]

        @block.sync
        def _(sp):
            def load(i, k):
                e = i * 2 + k
                for dst, src in ((wg, w["WgT"]), (wu, w["WuT"]), (wd, w["WdT"])):
                    sp.dma_start(dst[:, k], src[bass.ds(e, 1)].squeeze(0).rearrange("(h p) n -> p h n", p=P)).then_inc(w_in[k], 16)
            load(0, 0)
            load(0, 1)
            with sp.Fori(1, EX // 2) as i:
                for k in range(2):
                    sp.wait_ge(s["o_ready"], (i - 1) * 2 + k + 1)
                    load(i, k)

        @block.gpsimd
        def _(pool):
            def gather(e):
                if e >= 2:
                    pool.wait_ge(s["t_ready"], e - 1)
                    pool.wait_ge(s["eo_done"], e - 1)
                for t in range(NTOK):
                    nc.gpsimd.indirect_dma_start(out=xe[:, e % 2, t, :], out_offset=None, in_=m.rows,
                                                 in_offset=bass.IndirectOffsetOnAxis(ap=column(e, t), axis=0)).then_inc(gathered[e % 2], 16)

            gather(0)
            gather(1)
            for e in range(EX):
                pool.wait_ge(s["eo_done"], e + 1)
                if e:
                    pool.wait_ge(added[(e - 1) % 2], 16 * NTOK * ((e - 1) // 2 + 1))
                for t in range(NTOK):
                    nc.gpsimd.indirect_dma_start(out=out, out_offset=bass.IndirectOffsetOnAxis(ap=column(e, t), axis=0),
                                                 in_=eo[:, e % 2, t, :], in_offset=None,
                                                 compute_op=ALU.add).then_inc(added[e % 2], 16)
                if e + 2 < EX:
                    gather(e + 2)
            for k in range(2):
                pool.wait_ge(added[k], 16 * NTOK * EX // 2)

        @block.scalar
        def _(act):
            def rows(i, k):
                n = i * 2 + k
                act.wait_ge(s["t_ready"], n + 1)
                act.wait_ge(s["o_ready"], least(n - 1))
                nc.scalar.copy(xT[:, k], pT[:]).then_inc(s["t_copied"], 1)

            def step(i, k, last=False):
                for f in range(FT):
                    n = (i * 2 + k) * FT + f
                    act.wait_ge(s["gu_ready"], n + 1)
                    act.wait_ge(s["hid_done"], least(n - 1))
                    nc.scalar.activation(act_g[:, f % 2], pg[:, f % 2], ACT.Gelu).then_inc(s["gelu_done"], 1)
                if not last:
                    rows(i + k, 1 - k)

            rows(0, 0)
            step(0, 0)
            step(0, 1)
            with act.Fori(1, EX // 2 - 1) as i:
                step(i, 0)
                step(i, 1)
            step(EX // 2 - 1, 0)
            step(EX // 2 - 1, 1, True)

        @block.vector
        def _(dve):
            def step(i, k):
                e = i * 2 + k
                for f in range(FT):
                    n = e * FT + f
                    dve.wait_ge(s["gelu_done"], n + 1)
                    dve.wait_ge(s["o_ready"], e)
                    nc.vector.tensor_tensor(hid[:, f], act_g[:, f % 2], pu[:, f % 2], ALU.mult).then_inc(s["hid_done"], 1)
                dve.wait_ge(s["o_ready"], e + 1)
                if not (isinstance(i, int) and i == 0):
                    dve.wait_ge(added[k], 16 * NTOK * i)
                for t in range(NTOK):
                    score = xe[:, k, t, C:ROW][:, bass.ds(e, 1)]
                    last = nc.vector.scalar_tensor_tensor(out=eo[:, k, t, :], in0=po[:, t], scalar=score,
                                                          in1=m.mod[:, t // 2, GB, :], op0=ALU.mult, op1=ALU.mult)
                last.then_inc(s["eo_done"], 1)

            step(0, 0)
            step(0, 1)
            with dve.Fori(1, EX // 2) as i:
                step(i, 0)
                step(i, 1)

        @block.tensor
        def _(pe):
            def rows(i, k):
                n = i * 2 + k
                pe.wait_ge(gathered[k], 16 * NTOK * (i + 1))
                pe.wait_ge(s["t_copied"], n)
                for h in range(CH):
                    for t in range(NTOK):
                        last = nc.tensor.transpose(pT[:, h, t * P:(t + 1) * P], xe[:, k, t, h * P:(h + 1) * P], m.ident[:])
                last.then_inc(s["t_ready"], 1)

            def step(i, k, last_one=False):
                e = i * 2 + k
                pe.wait_ge(w_in[k], 48 * (i + 1))
                pe.wait_ge(s["t_copied"], e + 1)
                for f in range(FT):
                    n = e * FT + f
                    pe.wait_ge(s["hid_done"], least(n - 1))
                    for dst, wt in ((pg, wg), (pu, wu)):
                        for h in range(CH):
                            last = nc.tensor.matmul(dst[:, f % 2], wt[:, k, h, f * P:(f + 1) * P], xT[:, k, h, :],
                                                    start=h == 0, stop=h == CH - 1)
                    last.then_inc(s["gu_ready"], 1)
                if not last_one:
                    rows(i + k, 1 - k)
                pe.wait_ge(s["hid_done"], (e + 1) * FT)
                pe.wait_ge(s["eo_done"], e)
                for t in range(NTOK):
                    for f in range(FT):
                        last = nc.tensor.matmul(po[:, t], hid[:, f, t * P:(t + 1) * P], wd[:, k, f, :],
                                                start=f == 0, stop=f == FT - 1)
                last.then_inc(s["o_ready"], 1)

            rows(0, 0)
            step(0, 0)
            step(0, 1)
            with pe.Fori(1, EX // 2 - 1) as i:
                step(i, 0)
                step(i, 1)
            step(EX // 2 - 1, 0)
            step(EX // 2 - 1, 1, True)


def program(nc, a, out):
    m = Shared()
    USED.clear()
    mod_dram = nc.dram_tensor("mod_dram", [2, B, NMOD, C], F32).ap()
    with ExitStack() as ctx:
        sb, ps, sem = setup(nc, ctx)
        m.x = sb("x", [P, NT, C])
        m.mod = sb("mod", [P, B, NMOD, C])
        m.ident, m.mask = sb("ident", [P, P]), sb("mask", [P, 2 * P])
        m.upto, m.after, m.ones = sb("upto", [P, P]), sb("after", [P, P]), sb("ones", [P, P])
        m.neghalf, m.st = sb("neghalf", [P, NT]), sb("st", [P, NT, 6])
        m.mean, m.rstd, m.tmp = sb("mean", [P, NT]), sb("rstd", [P, NT]), sb("tmp", [P, NT])
        constants(nc, m, a["x"])
        modulation(nc, m, 0, a["c_cols"], a["wmod0"], mod_dram)
        with ExitStack() as scope:
            sb, _, _ = setup(nc, scope)
            m.qT, m.kT = sb("qT", [P, CH, B * T]), sb("kT", [P, CH, B * T])
            m.v = sb("v", [P, NT, C + 1])
            attention_projections(nc, m, a)
            attention(nc, m)
        with ExitStack() as scope:
            sb, _, _ = setup(nc, scope)
            m.seT, m.gx = sb("seT", [P, CH, NS]), sb("gx", [P, C])
            m.w1, m.w2 = sb("w1", [P, CH, HID]), sb("w2", [P, HT, C])
            slot_embeddings(nc, m, a)
            soft_mixture(nc, m)
        recycle(nc)
        modulation(nc, m, 1, a["c_cols"], a["wmod1"], mod_dram)
        with ExitStack() as scope:
            sb, _, _ = setup(nc, scope)
            m.cum_dram = nc.dram_tensor("cum_dram", [NT * HEADS, P], F32).ap()
            m.uT = sb("uT", [P, CH, B * T])
            m.dt, m.cs = sb("dt", [P, NT, HEADS]), sb("cs", [P, NT, 4, HEADS])
            m.etot = sb("etot", [STATE, NT, HEADS])
            state_inputs(nc, m, a)
            decays(nc, m, a)
            state_space(nc, m, a)
        recycle(nc)
        with ExitStack() as scope:
            sb, _, _ = setup(nc, scope)
            m.rows = nc.dram_tensor("rows_dram", [B * T, ROW], F32).ap()
            m.hT, m.sc = sb("hT", [P, CH, B * T]), sb("sc", [RX, T])
            m.place, m.idx = sb("place", [RX, T]), sb("idx", [P, 2 * RX], I32)
            routing_scores(nc, m, a)
            shared_and_choice(nc, m, a, out)
            index_lists(nc, m)
            experts(nc, m, a, out)


def kernel(**inputs):
    import numpy as np
    import concourse.bacc as bacc
    from concourse.bass_utils import run_bass_kernel_spmd

    g = {k: np.asarray(v) for k, v in inputs.items()}
    cols = lambda v: np.ascontiguousarray(v.reshape(-1, P).T)
    arrays = {
        "x": g["L0_attn_x"].reshape(B * T, C),
        "c_cols": np.stack([np.ascontiguousarray(g[f"L{l}_c"].T.reshape(CH, P, B).transpose(1, 0, 2)) for l in range(2)]),
        "wmod0": g["L0_wmod"], "wmod1": g["L1_wmod"],
        "WqT": g["L0_attn_Wq"].T, "WkT": g["L0_attn_Wk"].T, "Wv": g["L0_attn_Wv"], "WoT": g["L0_attn_Wo"].T,
        "bq": cols(g["L0_attn_bq"]), "bk": cols(g["L0_attn_bk"]), "bv": cols(g["L0_attn_bv"]), "bo": g["L0_attn_bo"],
    }
    arrays |= {
        "slot_embeds": g["L0_ffn_slot_embeds"].reshape(NS, C), "gamma_slot": g["L0_ffn_gamma_slot"],
        "gamma_x": g["L0_ffn_gamma_x"], "w1": g["L0_ffn_w1"], "w2": g["L0_ffn_w2"],
    }
    arrays |= {n: g["L1_attn_" + n] for n in ("W_in", "b_in", "A_log", "D_skip", "dt_bias", "W_out", "b_out")}
    arrays["ln_cols"] = np.stack([cols(g["L1_attn_ln_gamma"]), cols(g["L1_attn_ln_beta"])], 1)
    arrays |= {
        "gate_wT": g["L1_ffn_gate_w"].T, "Ws_gT": g["L1_ffn_Ws_g"].T, "Ws_uT": g["L1_ffn_Ws_u"].T, "Ws_dT": g["L1_ffn_Ws_d"].T,
        "WgT": g["L1_ffn_Wg"].transpose(0, 2, 1), "WuT": g["L1_ffn_Wu"].transpose(0, 2, 1), "WdT": g["L1_ffn_Wd"].transpose(0, 2, 1),
    }
    nc = bacc.Bacc("TRN2", target_bir_lowering=False, num_devices=1)
    ins, feed = {}, {}
    for name, v in arrays.items():
        v = np.ascontiguousarray(v)
        feed[f"in_{name}"] = v
        ins[name] = nc.dram_tensor(f"in_{name}", v.shape, mybir.dt.from_np(v.dtype), kind="ExternalInput").ap()
    out = nc.dram_tensor("out", (B * T, C), F32, kind="ExternalOutput").ap()
    program(nc, ins, out)
    r = run_bass_kernel_spmd(nc, [feed], core_ids=[0])
    return r.results[0]["out"].reshape(B, T, C)
```

```python
import concourse.bass as bass
from concourse import mybir
from contextlib import ExitStack

F32 = mybir.dt.float32
BF16 = mybir.dt.bfloat16
I32 = mybir.dt.int32
U32 = mybir.dt.uint32
ALU = mybir.AluOpType
FR = mybir.dt.float32r
ACT = mybir.ActivationFunctionType
AX = mybir.AxisListType.X

P = 128
B, T, C = 2, 2048, 256
CH = C // P
NTB = T // P
NT = B * NTB
GT = 4
GW = GT * P
NG = NTB // GT
NMOD = 6
SA, CA, GA, SB, CB, GB = range(NMOD)
WINDOW = 16
NEG = -1e30
LN_EPS = 1e-5
ST = 64
USED = []


def setup(nc, ctx):
    def sb(name, shape, dt=F32):
        return ctx.enter_context(nc.sbuf_tensor(name, shape, dt))

    def ps(name, shape, dt=F32):
        return ctx.enter_context(nc.psum_tensor(name, shape, dt))

    def sem(name):
        USED.append(nc.alloc_semaphore(name))
        return USED[-1]
    return sb, ps, sem


def recycle(nc):
    nc.clear_and_free_semaphores(list(USED))
    USED.clear()
    nc.all_engine_barrier()


def over(row, n):
    return row.unsqueeze(1).to_broadcast([row.shape[0], n, row.shape[-1]])


def exact_matmul(nc, out, ah, al, bh, bl, start, stop):
    nc.tensor.matmul(out, ah, bh, start=start, stop=False)
    nc.tensor.matmul(out, al, bh, start=False, stop=False)
    return nc.tensor.matmul(out, ah, bl, start=False, stop=stop)


def fresh(engine, i):
    with engine.register() as r:
        engine.reg_add(r, i, 0)
        return engine.snap(r, min_val=0, max_val=i.max_val)


class Shared:
    pass


def modulation(nc, m, w):
    L = 2
    with ExitStack() as ctx:
        sb, ps, sem = setup(nc, ctx)
        cc, cs = sb("m_cc", [P, L, CH, B]), sb("m_cs", [P, L, CH, B])
        wm = sb("m_wm", [P, L, CH, NMOD * C])
        rows = sb("m_rows", [B, L, NMOD, C])
        sgn, mag = sb("m_sgn", [B, L, 2, C]), sb("m_mag", [B, L, 2, C])
        pm = ps("m_pm", [B, L, NMOD * C])
        c_in = sem("m_c_in")
        names = "silu rows_ps rows_cp neg mag sgn sgn2 scaled gated stored spread".split()
        s = {n: sem("m_" + n) for n in names}
        w_in = [sem(f"m_w_in{l}") for l in range(L)]
        block = ctx.enter_context(nc.Block())

        @block.sync
        def _(sp):
            sp.dma_start(cc[:], w["c_cols"].rearrange("l p h b -> p l h b")).then_inc(c_in, 16)
            for l in range(L):
                sp.dma_start(wm[:, l], w[f"wmod{l}"].rearrange("(h p) n -> p h n", p=P)).then_inc(w_in[l], 16)
            for l in range(L):
                sp.wait_ge(s["gated"], l + 1)
                sp.wait_ge(s["scaled"], l + 1)
                sp.dma_start(m.mod_dram[l], rows[:, l]).then_inc(s["stored"], 16)
                if l == 0:
                    sp.wait_ge(s["stored"], 16)
                    sp.dma_start(m.mod[:].rearrange("p b m c -> p (b m c)"),
                                 m.mod_dram[0].rearrange("b m c -> (b m c)").partition_broadcast(P)).then_inc(s["spread"], 16)
            sp.wait_ge(s["spread"], 16)
            sp.wait_ge(s["stored"], 16 * L)

        @block.scalar
        def _(act):
            act.wait_ge(c_in, 16)
            nc.scalar.activation(cs[:], cc[:], ACT.Silu).then_inc(s["silu"], 1)

        @block.tensor
        def _(pe):
            pe.wait_ge(s["silu"], 1)
            for l in range(L):
                pe.wait_ge(w_in[l], 16)
                for n in range(NMOD * C // 512):
                    for h in range(CH):
                        last = nc.tensor.matmul(pm[:, l, n * 512:(n + 1) * 512], cs[:, l, h, :],
                                                wm[:, l, h, n * 512:(n + 1) * 512], start=h == 0, stop=h == CH - 1)
                last.then_inc(s["rows_ps"], 1)

        @block.vector
        def _(dve):
            for l in range(L):
                gates, scales = rows[:, l, GA:GB + 1:GB - GA, :], rows[:, l, CA:CB + 1:CB - CA, :]
                mg, sg = mag[:, l], sgn[:, l]
                dve.wait_ge(s["rows_ps"], l + 1)
                nc.vector.tensor_copy(rows[:, l].rearrange("b m c -> b (m c)"), pm[:, l]).then_inc(s["rows_cp"], 1)
                dve.wait_ge(s["rows_cp"], l + 1)
                nc.vector.tensor_scalar(mg, gates, -1.0, None, ALU.mult).then_inc(s["neg"], 1)
                nc.vector.tensor_scalar(sg, gates, 0.0, 2.0, ALU.is_ge, ALU.mult).then_inc(s["sgn"], 1)
                nc.vector.tensor_scalar_add(scales, scales, 1.0).then_inc(s["scaled"], 1)
                dve.wait_ge(s["sgn"], l + 1)
                nc.vector.tensor_scalar_add(sg, sg, -1.0).then_inc(s["sgn2"], 1)
                dve.wait_ge(s["neg"], l + 1)
                nc.vector.scalar_tensor_tensor(out=mg, in0=mg, scalar=0.25, in1=gates,
                                               op0=ALU.max, op1=ALU.max).then_inc(s["mag"], 1)
                dve.wait_ge(s["mag"], l + 1)
                dve.wait_ge(s["sgn2"], l + 1)
                nc.vector.tensor_tensor(gates, mg, sg, ALU.mult).then_inc(s["gated"], 1)


def constants(nc, m, x):
    with ExitStack() as ctx:
        sb, ps, sem = setup(nc, ctx)
        zeroed, ones_set, neg_set, half_set, shaped = [sem(n) for n in ("c_zero", "c_ones", "c_neg", "c_half", "c_shape")]
        x_in = [sem(f"c_x{i}") for i in range(NT // GT)]
        block = ctx.enter_context(nc.Block())
        xt = x.rearrange("(t p) c -> p t c", p=P)

        @block.sync
        def _(sp):
            for i in range(NT // GT):
                sp.dma_start(m.x[:, i * GT:(i + 1) * GT, :], xt[:, i * GT:(i + 1) * GT, :]).then_inc(x_in[i], 16)

        @block.gpsimd
        def _(pool):
            nc.gpsimd.memset(m.ident[:], 0.0).then_inc(zeroed, 1)
            nc.gpsimd.memset(m.mask[:], 0.0).then_inc(zeroed, 1)
            nc.gpsimd.memset(m.upto[:], 1.0).then_inc(ones_set, 1)
            nc.gpsimd.memset(m.after[:], 1.0).then_inc(ones_set, 1)
            nc.gpsimd.memset(m.ones[:], 1.0).then_inc(ones_set, 1)
            nc.gpsimd.memset(m.neghalf[:], -0.5).then_inc(half_set, 1)
            pool.wait_ge(zeroed, 2)
            nc.gpsimd.affine_select(out=m.ident[:], in_=m.ident[:], compare_op=ALU.not_equal, fill=1.0,
                                    base=0, pattern=[[-1, P]], channel_multiplier=1).then_inc(shaped, 1)
            nc.gpsimd.affine_select(out=m.mask[:], in_=m.mask[:], compare_op=ALU.is_ge, fill=NEG,
                                    base=WINDOW - P, pattern=[[1, 2 * P]], channel_multiplier=-1).then_inc(shaped, 1)
            pool.wait_ge(ones_set, 3)
            nc.gpsimd.affine_select(out=m.upto[:], in_=m.upto[:], compare_op=ALU.is_ge, fill=0.0,
                                    base=0, pattern=[[1, P]], channel_multiplier=-1).then_inc(shaped, 1)
            nc.gpsimd.affine_select(out=m.after[:], in_=m.after[:], compare_op=ALU.is_gt, fill=0.0,
                                    base=0, pattern=[[-1, P]], channel_multiplier=1).then_inc(shaped, 1)

        @block.vector
        def _(dve):
            for i in range(NT // GT):
                dve.wait_ge(x_in[i], 16)
                for t in range(i * GT, (i + 1) * GT):
                    nc.vector.bn_stats(m.st[:, t, :], m.x[:, t, :])


def finish_stats(nc, sems, m, n0, n1, eps=LN_EPS):
    a, b, c, d, e = sems
    st = m.st[:, n0:n1, :]
    dve, pool = nc.vector, nc.gpsimd
    mean, rstd, tmp = m.mean[:, n0:n1], m.rstd[:, n0:n1], m.tmp[:, n0:n1]

    def vector():
        dve.tensor_tensor(mean, st[:, :, 1], st[:, :, 4], ALU.add).then_inc(a, 1)
        dve.tensor_tensor(tmp, st[:, :, 1], st[:, :, 4], ALU.subtract).then_inc(a, 1)
        dve.tensor_tensor(rstd, st[:, :, 2], st[:, :, 5], ALU.add).then_inc(a, 1)
        dve.wait_ge(a, 3)
        dve.tensor_scalar(mean, mean, 0.5, None, ALU.mult).then_inc(b, 1)
        dve.tensor_tensor(tmp, tmp, tmp, ALU.mult).then_inc(b, 1)
        dve.tensor_scalar(rstd, rstd, 1.0 / C, eps, ALU.mult, ALU.add).then_inc(b, 1)
        dve.wait_ge(b, 3)
        dve.scalar_tensor_tensor(out=rstd, in0=tmp, scalar=0.25, in1=rstd, op0=ALU.mult, op1=ALU.add).then_inc(c, 1)

    def gpsimd():
        pool.wait_ge(c, 1)
        pool.tensor_tensor(rstd, rstd, m.neghalf[:, n0:n1], ALU.pow).then_inc(e, 1)
    return vector, gpsimd


def attention_projections(nc, m, w):
    with ExitStack() as ctx:
        sb, ps, sem = setup(nc, ctx)
        wq, wk = sb("wq", [P, CH, C]), sb("wk", [P, CH, C])
        wv, wo = sb("wv", [P, CH, C]), sb("wo", [P, CH, C])
        wvo = sb("wvo", [P, B, CH, C])
        qb, kb, vb = sb("qb", [P, CH]), sb("kb", [P, CH]), sb("vb", [P, CH])
        vbb = sb("vbb", [P, CH, P])
        bo = sb("bo", [P, C])
        vrow = sb("vrow", [P, B, C])
        h = sb("a_h", [P, B, GT, C])
        hT = sb("a_hT", [P, B, CH, GW])
        pT = ps("a_pT", [P, CH, GW])
        pq = ps("a_pq", [P, CH, GW])
        pk = ps("a_pk", [P, CH, GW])
        pv = ps("a_pv", [P, GT, C])
        loaded = sem("a_loaded")
        vb_spread, fold_ps, fold1, fold_done = [sem("a_" + n) for n in ("vbs", "fold_ps", "fold1", "fold_done")]
        stat = [sem(f"a_stat{i}") for i in range(5)]
        normed, scaled, shifted, t_ready, t_copied, q_ready, q_copied, k_ready, k_copied, v_ready, v_copied = [
            sem("a_" + n) for n in ("normed", "scaled", "shifted", "t_ready", "t_copied", "q_ready", "q_copied",
                                    "k_ready", "k_copied", "v_ready", "v_copied")]
        block = ctx.enter_context(nc.Block())
        st_vector, st_gpsimd = finish_stats(nc, stat, m, 0, NT)
        NL = 8 * 16

        @block.sync
        def _(sp):
            for dst, src in ((wv, w["Wv"]), (wo, w["WoT"]), (wq, w["WqT"]), (wk, w["WkT"])):
                sp.dma_start(dst[:], src.rearrange("(h p) n -> p h n", p=P)).then_inc(loaded, 16)
            for dst, src in ((qb, w["bq"]), (kb, w["bk"]), (vb, w["bv"])):
                sp.dma_start(dst[:], src).then_inc(loaded, 16)
            sp.dma_start(bo[:], w["bo"].partition_broadcast(P)).then_inc(loaded, 16)

        @block.gpsimd
        def _(pool):
            st_gpsimd()
            with pool.Fori(0, NG) as i:
                for b in range(B):
                    n = i * B + b + 1
                    pool.wait_ge(normed, n * GT)
                    nc.gpsimd.tensor_tensor(h[:, b], h[:, b], over(m.mod[:, b, CA, :], GT), ALU.mult).then_inc(scaled, 1)
                    pool.wait_ge(scaled, n)
                    nc.gpsimd.tensor_tensor(h[:, b], h[:, b], over(m.mod[:, b, SA, :], GT), ALU.add).then_inc(shifted, 1)

        @block.vector
        def _(dve):
            st_vector()
            dve.wait_ge(loaded, NL)
            nc.vector.tensor_copy(vbb[:], vb[:].unsqueeze(2).to_broadcast([P, CH, P])).then_inc(vb_spread, 1)
            nc.vector.memset(m.v[:, :, C:C + 1], 1.0)
            dve.wait_ge(fold_ps, 1)
            for b in range(B):
                nc.vector.tensor_tensor(wvo[:, b], pv[:, 0:CH, :], over(m.mod[:, b, GA, :], CH), ALU.mult).then_inc(fold_done, 1)
                nc.vector.tensor_tensor(vrow[:, b], pv[:, CH, :], bo[:], ALU.add).then_inc(fold1, 1)
                dve.wait_ge(fold1, b + 1)
                nc.vector.tensor_tensor(vrow[:, b], vrow[:, b], m.mod[:, b, GA, :], ALU.mult).then_inc(fold_done, 1)
            dve.wait_ge(stat[4], 1)
            dve.wait_ge(fold_done, 2 * B)

            def normalise(i, b):
                for k in range(GT):
                    t = bass.ds(b * NTB + i * GT + k, 1)
                    nc.vector.tensor_scalar(h[:, b, k, :], m.x[:, t, :].squeeze(1), m.mean[:, t], m.rstd[:, t],
                                            ALU.subtract, ALU.mult).then_inc(normed, 1)

            def group(i, b, last):
                n = i * B + b + 1
                if not last:
                    normalise(i + b, 1 - b)
                dve.wait_ge(t_ready, n)
                nc.vector.tensor_copy(hT[:, b], pT[:]).then_inc(t_copied, 1)
                dve.wait_ge(k_ready, n)
                for o in range(CH):
                    ins = nc.vector.tensor_scalar(m.kT[:, o, bass.ds(b * T + i * GW, GW)], pk[:, o, :], kb[:, o:o + 1],
                                                  None, ALU.add)
                ins.then_inc(k_copied, 1)
                dve.wait_ge(v_ready, n)
                nc.vector.tensor_tensor(m.v[:, bass.ds(b * NTB + i * GT, GT), 0:C], pv[:], over(vrow[:, b], GT),
                                        ALU.add).then_inc(v_copied, 1)

            normalise(0, 0)
            with dve.Fori(0, NG - 1) as i:
                group(i, 0, False)
                group(i, 1, False)
            group(NG - 1, 0, False)
            group(NG - 1, 1, True)

        @block.scalar
        def _(act):
            act.wait_ge(loaded, NL)
            with act.Fori(0, NG) as i:
                for b in range(B):
                    n = i * B + b + 1
                    act.wait_ge(q_ready, n)
                    for o in range(CH):
                        ins = nc.scalar.activation(m.qT[:, o, bass.ds(b * T + i * GW, GW)], pq[:, o, :], ACT.Identity,
                                                   bias=qb[:, o:o + 1])
                    ins.then_inc(q_copied, 1)

        @block.tensor
        def _(pe):
            pe.wait_ge(loaded, NL)
            pe.wait_ge(vb_spread, 1)
            for o in range(CH):
                for k in range(CH):
                    nc.tensor.matmul(pv[:, o, :], wv[:, k, o * P:(o + 1) * P], wo[:, k, :], start=k == 0, stop=k == CH - 1)
            for k in range(CH):
                last = nc.tensor.matmul(pv[:, CH, :], vbb[:, k, :], wo[:, k, :], start=k == 0, stop=k == CH - 1)
            last.then_inc(fold_ps, 1)
            pe.wait_ge(fold_done, 2 * B)
            with pe.Fori(0, NG) as i:
                for b in range(B):
                    n = i * B + b + 1
                    pe.wait_ge(shifted, n)
                    pe.wait_ge(t_copied, n - 1)
                    for o in range(CH):
                        for k in range(GT):
                            last = nc.tensor.transpose(pT[:, o, k * P:(k + 1) * P], h[:, b, k, o * P:(o + 1) * P], m.ident[:])
                    last.then_inc(t_ready, 1)
                    pe.wait_ge(t_copied, n)
                    for dst, wt, free, done in ((pq, wq, q_copied, q_ready), (pk, wk, k_copied, k_ready)):
                        pe.wait_ge(free, n - 1)
                        for o in range(CH):
                            for k in range(CH):
                                last = nc.tensor.matmul(dst[:, o, :], wt[:, k, o * P:(o + 1) * P], hT[:, b, k, :],
                                                        start=k == 0, stop=k == CH - 1)
                        last.then_inc(done, 1)
                    pe.wait_ge(v_copied, n - 1)
                    for j in range(GT):
                        for k in range(CH):
                            last = nc.tensor.matmul(pv[:, j, :], hT[:, b, k, j * P:(j + 1) * P], wvo[:, b, k, :],
                                                    start=k == 0, stop=k == CH - 1)
                    last.then_inc(v_ready, 1)


def attention(nc, m):
    scale = float(C) ** -0.5
    with ExitStack() as ctx:
        sb, ps, sem = setup(nc, ctx)
        qs = sb("b_q", [P, 2, CH, P])
        nmax = sb("b_nmax", [P, 2])
        pr = sb("b_p", [P, 2, T])
        pT = sb("b_pT", [P, 2, GW])
        rden = sb("b_rden", [P, 2])
        pS = ps("b_pS", [P, T])
        pTp = ps("b_pTp", [P, 2, GW])
        pO = ps("b_pO", [P, 2, 512])
        q_staged, s_ready, masked, max_done, nmax_done, exp_done, t_ready, t_copied, pv_done, rden_done, x_done = [
            sem("b_" + n) for n in ("q_staged", "s_ready", "masked", "max_done", "nmax_done", "exp_done", "t_ready",
                                    "t_copied", "pv_done", "rden_done", "x_done")]
        block = ctx.enter_context(nc.Block())
        first = [max(it - 1, 0) for it in range(NTB)]
        nkeys = [NTB - f for f in first]
        ngroups = [-(-n // GT) for n in nkeys]
        before = [sum(ngroups[:it]) for it in range(NTB + 1)]

        def width(it, g):
            return min(GT, nkeys[it] - g * GT) * P

        @block.gpsimd
        def _(pool):
            with pool.Fori(0, B) as b:
                for it in range(NTB):
                    if it >= 2:
                        pool.wait_ge(s_ready, b * NTB + it - 1)
                    else:
                        pool.wait_ge(s_ready, b * NTB)
                    nc.gpsimd.tensor_copy(qs[:, it % 2], m.qT[:, :, bass.ds(b * T + it * P, P)]).then_inc(q_staged, 1)

        @block.tensor
        def _(pe):
            def scores(b, it):
                pe.wait_ge(q_staged, b * NTB + it + 1)
                pe.wait_ge(exp_done, b * NTB + it)
                for g in range(ngroups[it]):
                    w = width(it, g)
                    for k in range(CH):
                        last = nc.tensor.matmul(pS[:, g * GW:g * GW + w], qs[:, it % 2, k, :],
                                                m.kT[:, k, bass.ds(b * T + first[it] * P + g * GW, w)],
                                                start=k == 0, stop=k == CH - 1)
                last.then_inc(s_ready, 1)

            def transposes(b, it, g, n):
                pe.wait_ge(t_copied, b * before[-1] + max(n - 1, 0))
                for j in range(width(it, g) // P):
                    last = nc.tensor.transpose(pTp[:, n % 2, j * P:(j + 1) * P],
                                               pr[:, it % 2, g * GW + j * P:g * GW + (j + 1) * P], m.ident[:])
                last.then_inc(t_ready, 1)

            def values(b, it, g, n):
                pe.wait_ge(t_copied, b * before[-1] + n + 1)
                for j in range(width(it, g) // P):
                    last = nc.tensor.matmul(pO[:, it % 2, 0:C + 1], pT[:, n % 2, j * P:(j + 1) * P],
                                            m.v[:, bass.ds(b * NTB + first[it] + g * GT + j, 1), :].squeeze(1),
                                            start=g == 0 and j == 0, stop=g * GT + j == nkeys[it] - 1)
                last.then_inc(pv_done, 1)

            with pe.Fori(0, B) as b:
                scores(b, 0)
                for it in range(NTB):
                    b = fresh(pe, b)
                    if it + 1 < NTB:
                        scores(b, it + 1)
                    pe.wait_ge(x_done, b * NTB + max(it - 1, 0))
                    pe.wait_ge(exp_done, b * NTB + it + 1)
                    base = before[it]
                    transposes(b, it, 0, base)
                    for g in range(ngroups[it]):
                        if g + 1 < ngroups[it]:
                            transposes(b, it, g + 1, base + g + 1)
                        values(b, it, g, base + g)

        @block.scalar
        def _(act):
            def exps(b, it):
                act.wait_ge(nmax_done, b * NTB + it + 1)
                if it >= 2:
                    act.wait_ge(pv_done, b * before[-1] + before[it - 1])
                else:
                    act.wait_ge(pv_done, b * before[-1])
                nc.scalar.activation(pr[:, it % 2, 0:nkeys[it] * P], pS[:, 0:nkeys[it] * P], ACT.Exp,
                                     bias=nmax[:, it % 2:it % 2 + 1], scale=scale).then_inc(exp_done, 1)

            def copies(b, it):
                for g in range(ngroups[it]):
                    n = before[it] + g
                    act.wait_ge(t_ready, b * before[-1] + n + 1)
                    act.wait_ge(pv_done, b * before[-1] + max(n - 1, 0))
                    w = width(it, g)
                    nc.scalar.copy(pT[:, n % 2, 0:w], pTp[:, n % 2, 0:w]).then_inc(t_copied, 1)

            with act.Fori(0, B) as b:
                exps(b, 0)
                for it in range(NTB):
                    b = fresh(act, b)
                    copies(b, it)
                    if it + 1 < NTB:
                        exps(b, it + 1)

        @block.vector
        def _(dve):
            def maxima(b, it):
                dve.wait_ge(s_ready, b * NTB + it + 1)
                n, lo = min(it + 1, 2), max(1 - it, 0) * P
                nc.vector.tensor_tensor(pS[:, 0:n * P], pS[:, 0:n * P], m.mask[:, lo:2 * P], ALU.add).then_inc(masked, 1)
                dve.wait_ge(masked, b * NTB + it + 1)
                nc.vector.reduce_max(nmax[:, it % 2:it % 2 + 1], pS[:, 0:nkeys[it] * P], axis=AX).then_inc(max_done, 1)
                dve.wait_ge(max_done, b * NTB + it + 1)
                nc.vector.tensor_scalar(nmax[:, it % 2:it % 2 + 1], nmax[:, it % 2:it % 2 + 1], -scale, None,
                                        ALU.mult).then_inc(nmax_done, 1)

            def update(b, it):
                r = rden[:, it % 2:it % 2 + 1]
                xt = m.x[:, bass.ds(b * NTB + it, 1), :].squeeze(1)
                dve.wait_ge(pv_done, b * before[-1] + before[it + 1])
                nc.vector.reciprocal(r, pO[:, it % 2, C:C + 1]).then_inc(rden_done, 1)
                dve.wait_ge(rden_done, b * NTB + it + 1)
                nc.vector.scalar_tensor_tensor(out=xt, in0=pO[:, it % 2, 0:C], scalar=r, in1=xt,
                                               op0=ALU.mult, op1=ALU.add).then_inc(x_done, 1)
                dve.wait_ge(x_done, b * NTB + it + 1)
                nc.vector.bn_stats(m.st[:, bass.ds(b * NTB + it, 1), :].squeeze(1), xt)

            with dve.Fori(0, B) as b:
                maxima(b, 0)
                for it in range(NTB):
                    b = fresh(dve, b)
                    if it + 1 < NTB:
                        maxima(b, it + 1)
                    update(b, it)


E, SL = 8, 128
NS = E * SL
HID = 4 * C
HT = HID // P
SH = NS // 512


def row_norms(nc, m, ss, clamped, powed, n, value, dve_side):
    if dve_side:
        nc.vector.tensor_scalar(ss, ss, 1e-24, None, ALU.max).then_inc(clamped, 1)
    else:
        nc.gpsimd.wait_ge(clamped, value)
        nc.gpsimd.tensor_tensor(ss, ss, m.neghalf[:, 0:n], ALU.pow).then_inc(powed, 1)


def slot_embeddings(nc, m, w):
    with ExitStack() as ctx:
        sb, ps, sem = setup(nc, ctx)
        se = sb("s_se", [P, E, C])
        sq = sb("s_sq", [P, C])
        ss = sb("s_ss", [P, E])
        gamma = sb("s_gamma", [P, C])
        pT = ps("s_pT", [P, 2, CH, GW])
        loaded, squared, clamped, powed, scaled, gammaed, t_ready = [
            sem("s_" + n) for n in ("loaded", "squared", "clamped", "powed", "scaled", "gammaed", "t_ready")]
        block = ctx.enter_context(nc.Block())

        @block.sync
        def _(sp):
            sp.dma_start(se[:], w["slot_embeds"].rearrange("(t p) c -> p t c", p=P)).then_inc(loaded, 16)
            sp.dma_start(gamma[:], w["gamma_slot"].partition_broadcast(P)).then_inc(loaded, 16)
            sp.dma_start(m.gx[:], w["gamma_x"].partition_broadcast(P)).then_inc(loaded, 16)
            sp.dma_start(m.w1[:], w["w1"].rearrange("(h p) n -> p h n", p=P)).then_inc(loaded, 16)
            sp.dma_start(m.w2[:], w["w2"].rearrange("(h p) n -> p h n", p=P)).then_inc(loaded, 16)
            sp.wait_ge(loaded, 80)

        @block.scalar
        def _(act):
            act.wait_ge(loaded, 80)
            for t in range(E):
                if t:
                    act.wait_ge(squared, t)
                nc.scalar.activation(sq[:], se[:, t], ACT.Square, accum_out=ss[:, t:t + 1]).then_inc(squared, 1)

        @block.gpsimd
        def _(pool):
            row_norms(nc, m, ss[:], clamped, powed, E, 1, False)

        @block.vector
        def _(dve):
            dve.wait_ge(squared, E)
            row_norms(nc, m, ss[:], clamped, powed, E, 1, True)
            nc.vector.tensor_scalar(gamma[:], gamma[:], float(C) ** 0.5, None, ALU.mult).then_inc(gammaed, 1)
            nc.vector.tensor_scalar(m.gx[:], m.gx[:], float(C) ** 0.5, None, ALU.mult)
            dve.wait_ge(powed, 1)
            dve.wait_ge(gammaed, 1)
            for t in range(E):
                nc.vector.scalar_tensor_tensor(out=se[:, t], in0=se[:, t], scalar=ss[:, t:t + 1], in1=gamma[:],
                                               op0=ALU.mult, op1=ALU.mult).then_inc(scaled, 1)
            dve.wait_ge(t_ready, 1)
            nc.vector.tensor_copy(m.seT[:].rearrange("p h (a n) -> p a h n", a=2), pT[:])

        @block.tensor
        def _(pe):
            pe.wait_ge(scaled, E)
            for t in range(E):
                for h in range(CH):
                    last = nc.tensor.transpose(pT[:, t // GT, h, t % GT * P:(t % GT + 1) * P],
                                               se[:, t, h * P:(h + 1) * P], m.ident[:])
            last.then_inc(t_ready, 1)


def soft_mixture(nc, m):
    with ExitStack() as ctx:
        sb, ps, sem = setup(nc, ctx)
        xn = sb("d_xn", [P, NTB, C])
        xnT = sb("d_xnT", [P, CH, T])
        raw = sb("d_raw", [P, E, T])
        work = sb("d_work", [P, 2, T])
        slotsT = sb("d_slotsT", [P, CH, NS])
        proc = sb("d_proc", [P, E, C])
        sl = sb("d_sl", [P, 2, C])
        ss = sb("d_ss", [P, NTB])
        sq = sl[:, 0]
        nmax, esum = sb("d_nmax", [P, 2]), sb("d_esum", [P, 2])
        rsum = sb("d_rsum", [P, 2])
        cmax, csum, crs = sb("d_cmax", [P, 2]), sb("d_csum", [P, 2]), sb("d_crs", [P, 2])
        eT = sb("d_eT", [P, 2, GW])
        pL = ps("d_pL", [P, T])
        pT = ps("d_pT", [P, 2, GW])
        pO = ps("d_pO", [P, 2, 512])
        hg = work[:].rearrange("p s (k c) -> p s k c", c=C)[:, :, 0:GT, :]
        hid = work[:].rearrange("p s n -> p (s n)").rearrange("p (t n) -> p t n", n=512)
        pc = work[:, 0, :].rearrange("p (s n) -> p s n", s=2)
        pcT = work[:, 1, :].rearrange("p (s t n) -> p s t n", s=2, t=E)
        names = ("own stat0 stat1 stat2 stat3 stat4 normed scaled shifted squared clamped powed xn_done xT_ready xT_copied "
                 "l_ready max_done nmax_done exp_done raw_done t_ready t_copied_a t_copied_d sl_ready rsum_done sl_scaled "
                 "h_ready h_done y_ready y_done r_ready cmax_done cnmax_done cexp_done pt_ready pt_copied o_ready "
                 "crs_done x_done spread").split()
        s = {n: sem("d_" + n) for n in names}
        block = ctx.enter_context(nc.Block())

        @block.sync
        def _(sp):
            sp.wait_ge(s["y_done"], B * E)
            sp.dma_start(m.mod[:].rearrange("p b m c -> p (b m c)"),
                         m.mod_dram[1].rearrange("b m c -> (b m c)").partition_broadcast(P)).then_inc(s["spread"], 16)
            sp.wait_ge(s["spread"], 16)

        st_vector, st_gpsimd = finish_stats(nc, [s[f"stat{i}"] for i in range(5)], m, 0, NT)
        seq = []
        for et in range(E):
            seq += [("exp", et, g) for g in range(NG)] + ([("slots", et - 1, 0)] if et else [])
        seq.append(("slots", E - 1, 0))
        at = {k: n for n, k in enumerate(seq)}
        owner = ["a" if kind == "exp" and g < 2 else "d" for kind, et, g in seq]
        nth = [owner[:n + 1].count(o) for n, o in enumerate(owner)]

        def await_copy(engine, b, n):
            o = owner[n]
            engine.wait_ge(s["t_copied_" + o], b * owner.count(o) + nth[n])

        @block.gpsimd
        def _(pool):
            st_gpsimd()
            own = m.mod[:, 0, SA:CA + 1, :]
            with pool.Fori(0, B) as b:
                nc.gpsimd.tensor_copy(own, m.mod[:, bass.ds(b, 1), SB:CB + 1, :].squeeze(1)).then_inc(s["own"], 1)
                pool.wait_ge(s["own"], b + 1)
                for g in range(NG):
                    n = b * NG + g + 1
                    pool.wait_ge(s["normed"], n * GT)
                    hb = hg[:, g % 2]
                    nc.gpsimd.tensor_tensor(hb, hb, over(own[:, 1], GT), ALU.mult).then_inc(s["scaled"], 1)
                    pool.wait_ge(s["scaled"], n)
                    nc.gpsimd.tensor_tensor(hb, hb, over(own[:, 0], GT), ALU.add).then_inc(s["shifted"], 1)
                    row_norms(nc, m, ss[:, g * GT:(g + 1) * GT], s["clamped"], s["powed"], GT, n, False)

        @block.vector
        def _(dve):
            st_vector()
            dve.wait_ge(s["stat4"], 1)

            def normalise(b, g):
                for k in range(GT):
                    t = bass.ds(b * NTB + g * GT + k, 1)
                    nc.vector.tensor_scalar(hg[:, g % 2, k, :], m.x[:, t, :].squeeze(1), m.mean[:, t], m.rstd[:, t],
                                            ALU.subtract, ALU.mult).then_inc(s["normed"], 1)

            def rows(b, g):
                n = b * NG + g + 1
                dve.wait_ge(s["squared"], n * GT)
                row_norms(nc, m, ss[:, g * GT:(g + 1) * GT], s["clamped"], s["powed"], GT, n, True)
                dve.wait_ge(s["powed"], n)
                for k in range(GT):
                    t = g * GT + k
                    nc.vector.scalar_tensor_tensor(out=xn[:, t, :], in0=hg[:, g % 2, k, :], scalar=ss[:, t:t + 1],
                                                   in1=m.gx[:], op0=ALU.mult, op1=ALU.mult).then_inc(s["xn_done"], 1)

            def maxima(b, et):
                n = b * E + et + 1
                dve.wait_ge(s["l_ready"], n)
                nc.vector.reduce_max(nmax[:, et % 2:et % 2 + 1], pL[:], axis=AX).then_inc(s["max_done"], 1)
                dve.wait_ge(s["max_done"], n)
                nc.vector.tensor_scalar(nmax[:, et % 2:et % 2 + 1], nmax[:, et % 2:et % 2 + 1], -1.0, None,
                                        ALU.mult).then_inc(s["nmax_done"], 1)

            def copy_t(b, key):
                n = at[key]
                dve.wait_ge(s["t_ready"], b * len(seq) + n + 1)
                kind, et, g = key
                if kind == "exp":
                    nc.vector.tensor_copy(eT[:, g % 2], pT[:, n % 2]).then_inc(s["t_copied_d"], 1)
                else:
                    nc.vector.tensor_copy(slotsT[:, :, et * P:(et + 1) * P],
                                          pT[:, n % 2, 0:C].rearrange("p (h n) -> p h n", h=CH)).then_inc(s["t_copied_d"], 1)

            def scale_slots(b, et):
                n = b * E + et + 1
                r = rsum[:, et % 2:et % 2 + 1]
                dve.wait_ge(s["exp_done"], n)
                nc.vector.reciprocal(r, esum[:, et % 2:et % 2 + 1]).then_inc(s["rsum_done"], 1)
                dve.wait_ge(s["rsum_done"], n)
                dve.wait_ge(s["sl_ready"], n)
                nc.vector.tensor_scalar(sl[:, et % 2], pO[:, et % 2, 0:C], r, None, ALU.mult).then_inc(s["sl_scaled"], 1)

            with dve.Fori(0, B) as b:
                dve.wait_ge(s["o_ready"], b * NTB)
                normalise(b, 0)
                for g in range(NG):
                    if g + 1 < NG:
                        if g:
                            dve.wait_ge(s["xn_done"], b * NTB + g * GT)
                        normalise(b, g + 1)
                    rows(b, g)
                b0 = b
                maxima(b, 0)
                for et in range(E):
                    b = fresh(dve, b0)
                    if et + 1 < E:
                        maxima(b, et + 1)
                    for g in range(2, NG):
                        copy_t(b, ("exp", et, g))
                    scale_slots(b, et)
                    if et:
                        copy_t(b, ("slots", et - 1, 0))
                copy_t(b, ("slots", E - 1, 0))
                b = fresh(dve, b0)
                for et in range(E):
                    dve.wait_ge(s["y_ready"], b * E + et + 1)
                    nc.vector.tensor_tensor(proc[:, et], pO[:, et % 2, 0:C], m.mod[:, bass.ds(b, 1), GB, :].squeeze(1),
                                            ALU.mult).then_inc(s["y_done"], 1)

                def cmaxima(b, t):
                    n = b * NTB + t + 1
                    dve.wait_ge(s["r_ready"], n)
                    nc.vector.reduce_max(cmax[:, t % 2:t % 2 + 1], pL[:, t % 2 * NS:(t % 2 + 1) * NS], axis=AX).then_inc(s["cmax_done"], 1)
                    dve.wait_ge(s["cmax_done"], n)
                    nc.vector.tensor_scalar(cmax[:, t % 2:t % 2 + 1], cmax[:, t % 2:t % 2 + 1], -1.0, None,
                                            ALU.mult).then_inc(s["cnmax_done"], 1)

                def update(b, t):
                    n = b * NTB + t + 1
                    r = crs[:, t % 2:t % 2 + 1]
                    xt = m.x[:, bass.ds(b * NTB + t, 1), :].squeeze(1)
                    dve.wait_ge(s["o_ready"], n)
                    dve.wait_ge(s["crs_done"], n)
                    nc.vector.scalar_tensor_tensor(out=xt, in0=pO[:, t % 2, 0:C], scalar=r, in1=xt,
                                                   op0=ALU.mult, op1=ALU.add).then_inc(s["x_done"], 1)
                    dve.wait_ge(s["x_done"], n)
                    nc.vector.bn_stats(m.st[:, bass.ds(b * NTB + t, 1), :].squeeze(1), xt)

                cmaxima(b, 0)
                for t in range(NTB):
                    b = fresh(dve, b0)
                    if t + 1 < NTB:
                        cmaxima(b, t + 1)
                    dve.wait_ge(s["pt_ready"], b * NTB + t + 1)
                    nc.vector.tensor_copy(pcT[:, t % 2].rearrange("p e n -> p (e n)"),
                                          pT[:].rearrange("p s n -> p (s n)")).then_inc(s["pt_copied"], 1)
                    nc.vector.reciprocal(crs[:, t % 2:t % 2 + 1], csum[:, t % 2:t % 2 + 1]).then_inc(s["crs_done"], 1)
                    if t:
                        update(b, t - 1)
                update(b, NTB - 1)

        @block.scalar
        def _(act):
            def exps(b, et):
                n = b * E + et + 1
                act.wait_ge(s["nmax_done"], n)
                act.wait_ge(s["sl_ready"], b * E + max(et - 1, 0))
                nc.scalar.activation(work[:, et % 2], pL[:], ACT.Exp, bias=nmax[:, et % 2:et % 2 + 1],
                                     accum_out=esum[:, et % 2:et % 2 + 1]).then_inc(s["exp_done"], 1)
                nc.scalar.copy(raw[:, et, :], pL[:]).then_inc(s["raw_done"], 1)

            def cexps(b, t):
                n = b * NTB + t + 1
                act.wait_ge(s["cnmax_done"], n)
                act.wait_ge(s["pt_ready"], b * NTB + max(t - 1, 0))
                act.wait_ge(s["crs_done"], b * NTB + max(t - 1, 0))
                nc.scalar.activation(pc[:, t % 2], pL[:, t % 2 * NS:(t % 2 + 1) * NS], ACT.Exp,
                                     bias=cmax[:, t % 2:t % 2 + 1], accum_out=csum[:, t % 2:t % 2 + 1]).then_inc(s["cexp_done"], 1)

            with act.Fori(0, B) as b0:
                b = b0
                for g in range(NG):
                    n = b * NG + g + 1
                    act.wait_ge(s["shifted"], n)
                    for k in range(GT):
                        if g or k:
                            act.wait_ge(s["squared"], b * NTB + g * GT + k)
                        nc.scalar.activation(sq, hg[:, g % 2, k, :], ACT.Square,
                                             accum_out=ss[:, g * GT + k:g * GT + k + 1]).then_inc(s["squared"], 1)
                for g in range(NG):
                    act.wait_ge(s["xT_ready"], b * NG + g + 1)
                    nc.scalar.copy(xnT[:, :, g * GW:(g + 1) * GW], (pT if g % 2 == 0 else pO)[:]).then_inc(s["xT_copied"], 1)
                b = fresh(act, b0)
                act.wait_ge(s["xn_done"], b * NTB + NTB)
                exps(b, 0)
                for et in range(E):
                    b = fresh(act, b0)
                    for g in range(2):
                        n = at["exp", et, g]
                        act.wait_ge(s["t_ready"], b * len(seq) + n + 1)
                        nc.scalar.copy(eT[:, g % 2], pT[:, n % 2]).then_inc(s["t_copied_a"], 1)
                    if et + 1 < E:
                        exps(b, et + 1)
                b = fresh(act, b0)
                act.wait_ge(s["sl_ready"], b * E + E)
                for a in range(SH):
                    for j in range(HT):
                        n = b * SH * HT + a * HT + j + 1
                        act.wait_ge(s["h_ready"], n)
                        if a and j == 0:
                            act.wait_ge(s["y_ready"], b * E + a * E // SH)
                        nc.scalar.activation(hid[:, j, :], pL[:, j % 4 * 512:(j % 4 + 1) * 512], ACT.Gelu).then_inc(s["h_done"], 1)
                b = fresh(act, b0)
                act.wait_ge(s["y_ready"], b * E + E)
                for t in range(NTB):
                    cexps(b, t)

        @block.tensor
        def _(pe):
            def logits(b, et):
                pe.wait_ge(s["raw_done"], b * E + et)
                for g in range(NG):
                    for k in range(CH):
                        last = nc.tensor.matmul(pL[:, g * GW:(g + 1) * GW], m.seT[:, k, et * P:(et + 1) * P],
                                                xnT[:, k, g * GW:(g + 1) * GW], start=k == 0, stop=k == CH - 1)
                last.then_inc(s["l_ready"], 1)

            def transposes(b, key):
                n = at[key]
                kind, et, g = key
                if n >= 2:
                    await_copy(pe, b, n - 2)
                if kind == "exp":
                    for j in range(GT):
                        last = nc.tensor.transpose(pT[:, n % 2, j * P:(j + 1) * P],
                                                   work[:, et % 2, g * GW + j * P:g * GW + (j + 1) * P], m.ident[:])
                else:
                    for h in range(CH):
                        last = nc.tensor.transpose(pT[:, n % 2, h * P:(h + 1) * P], sl[:, et % 2, h * P:(h + 1) * P], m.ident[:])
                last.then_inc(s["t_ready"], 1)

            def slots(b, et, g):
                await_copy(pe, b, at["exp", et, g])
                for j in range(GT):
                    last = nc.tensor.matmul(pO[:, et % 2, 0:C], eT[:, g % 2, j * P:(j + 1) * P], xn[:, g * GT + j, :],
                                            start=g == 0 and j == 0, stop=g == NG - 1 and j == GT - 1)
                if g == NG - 1:
                    last.then_inc(s["sl_ready"], 1)

            with pe.Fori(0, B) as b0:
                b = b0
                for g in range(NG):
                    pe.wait_ge(s["xn_done"], b * NTB + (g + 1) * GT)
                    if g == 0:
                        pe.wait_ge(s["pt_copied"], b * NTB)
                        pe.wait_ge(s["x_done"], b * NTB)
                    if g >= 2:
                        pe.wait_ge(s["xT_copied"], b * NG + g - 1)
                    for h in range(CH):
                        for k in range(GT):
                            last = nc.tensor.transpose((pT if g % 2 == 0 else pO)[:, h, k * P:(k + 1) * P],
                                                       xn[:, g * GT + k, h * P:(h + 1) * P], m.ident[:])
                    last.then_inc(s["xT_ready"], 1)
                pe.wait_ge(s["xT_copied"], b * NG + NG)
                logits(b, 0)
                for et in range(E):
                    b = fresh(pe, b0)
                    if et + 1 < E:
                        logits(b, et + 1)
                    pe.wait_ge(s["exp_done"], b * E + et + 1)
                    pe.wait_ge(s["sl_scaled"], b * E + max(et - 1, 0))
                    transposes(b, ("exp", et, 0))
                    for g in range(NG):
                        if g + 1 < NG:
                            transposes(b, ("exp", et, g + 1))
                        slots(b, et, g)
                    if et:
                        pe.wait_ge(s["sl_scaled"], b * E + et)
                        transposes(b, ("slots", et - 1, 0))
                pe.wait_ge(s["sl_scaled"], b * E + E)
                transposes(b, ("slots", E - 1, 0))
                b = fresh(pe, b0)
                await_copy(pe, b, len(seq) - 1)
                pe.wait_ge(s["raw_done"], b * E + E)
                for a in range(SH):
                    for j in range(HT):
                        n = b * SH * HT + a * HT + j
                        if a or j >= 4:
                            pe.wait_ge(s["h_done"], n - 3)
                        for k in range(CH):
                            last = nc.tensor.matmul(pL[:, j % 4 * 512:(j % 4 + 1) * 512], m.w1[:, k, j * P:(j + 1) * P],
                                                    slotsT[:, k, a * 512:(a + 1) * 512], start=k == 0, stop=k == CH - 1)
                        last.then_inc(s["h_ready"], 1)
                    pe.wait_ge(s["h_done"], b * SH * HT + (a + 1) * HT)
                    for e in range(4):
                        et = a * 4 + e
                        if et >= 2:
                            pe.wait_ge(s["y_done"], b * E + et - 1)
                        for j in range(HT):
                            last = nc.tensor.matmul(pO[:, et % 2, 0:C], hid[:, j, e * P:(e + 1) * P], m.w2[:, j, :],
                                                    start=j == 0, stop=j == HT - 1)
                        last.then_inc(s["y_ready"], 1)

                def by_token(b, t):
                    pe.wait_ge(s["cexp_done"], b * NTB + max(t - 1, 0))
                    for e in range(E):
                        o = t % 2 * NS + e * P
                        last = nc.tensor.transpose(pL[:, o:o + P], raw[:, e, t * P:(t + 1) * P], m.ident[:])
                    last.then_inc(s["r_ready"], 1)

                def combine(b, t):
                    pe.wait_ge(s["pt_copied"], b * NTB + t + 1)
                    pe.wait_ge(s["x_done"], b * NTB + max(t - 1, 0))
                    for e in range(E):
                        last = nc.tensor.matmul(pO[:, t % 2, 0:C], pcT[:, t % 2, e, :], proc[:, e, :], start=e == 0, stop=e == E - 1)
                    last.then_inc(s["o_ready"], 1)

                b = fresh(pe, b0)
                pe.wait_ge(s["y_done"], b * E + E)
                by_token(b, 0)
                for t in range(NTB):
                    b = fresh(pe, b0)
                    n = b * NTB + t + 1
                    if t + 1 < NTB:
                        by_token(b, t + 1)
                    pe.wait_ge(s["cexp_done"], n)
                    pe.wait_ge(s["pt_copied"], n - 1)
                    for e in range(E):
                        last = nc.tensor.transpose(pT[:, e // 4, e % 4 * P:(e % 4 + 1) * P], pc[:, t % 2, e * P:(e + 1) * P], m.ident[:])
                    last.then_inc(s["pt_ready"], 1)
                    if t:
                        combine(b, t - 1)
                combine(b, NTB - 1)


STATE, HEADS = 64, 8
INNER = 2 * C
HD = INNER // HEADS
PROJ = 2 * INNER + 2 * STATE + HEADS
ZX = 2 * INNER
DT0 = ZX + 2 * STATE


def least(v):
    return max(v, 0) if isinstance(v, int) else v


def state_inputs(nc, m, w):
    with ExitStack() as ctx:
        sb, ps, sem = setup(nc, ctx)
        hg, un = sb("e_hg", [P, B, GT, C]), sb("e_un", [P, B, GT, C])
        ug = sb("e_ug", [P, B, CH, GW])
        gated = sb("e_gated", [P, B, GT, C])
        wdt = sb("e_wdt", [P, CH, HEADS])
        gb = sb("e_gb", [P, 2, CH])
        bout = sb("e_bout", [P, C])
        bdt, bdt2 = sb("e_bdt", [P, HEADS]), sb("e_bdt2", [P, HEADS])
        st2, mv = sb("e_st2", [P, B, GT, 6]), sb("e_mv", [P, B, GT, 2])
        rs = sb("e_rs", [P, B, GT])
        pT = ps("e_pT", [P, 2, CH, GW])
        pd = ps("e_pd", [P, 2, 512])
        names = ("loaded bias stat0 stat1 stat2 stat3 stat4 normed scaled shifted st2 mv var_done powed un_done kept gated x_done t_ready "
                 "t_copied d_ready d_done").split()
        s = {n: sem("e_" + n) for n in names}
        u_out = [sem(f"e_u_out{b}") for b in range(B)]
        block = ctx.enter_context(nc.Block())
        st_vector, st_gpsimd = finish_stats(nc, [s[f"stat{i}"] for i in range(5)], m, 0, NT)

        @block.sync
        def _(sp):
            sp.dma_start(wdt[:], w["W_in"][:, DT0:PROJ].rearrange("(h p) n -> p h n", p=P)).then_inc(s["loaded"], 16)
            sp.dma_start(gb[:], w["ln_cols"]).then_inc(s["loaded"], 16)
            sp.dma_start(bout[:], w["b_out"].partition_broadcast(P)).then_inc(s["loaded"], 16)
            sp.dma_start(bdt[:], w["b_in"][DT0:PROJ].partition_broadcast(P)).then_inc(s["loaded"], 16)
            sp.dma_start(bdt2[:], w["dt_bias"].partition_broadcast(P)).then_inc(s["loaded"], 16)
            with sp.Fori(0, NG) as i:
                for b in range(B):
                    sp.wait_ge(s["t_copied"], i * B + b + 1)
                    sp.dma_start(m.uT[:, :, bass.ds(b * T + i * GW, GW)], ug[:, b]).then_inc(u_out[b], 16)
            for b in range(B):
                sp.wait_ge(u_out[b], 16 * NG)

        def steps(eng, step):
            step(0, 0, 0, first=True)
            step(1, 0, 1)
            with eng.Fori(1, NG - 1) as i:
                step(i * B, i, 0)
                step(i * B + 1, i, 1)
            step(NG * B - 2, NG - 1, 0)
            step(NG * B - 1, NG - 1, 1, last=True)

        @block.gpsimd
        def _(pool):
            st_gpsimd()

            def shift(n, b):
                pool.wait_ge(s["scaled"], n + 1)
                nc.gpsimd.tensor_tensor(hg[:, b], hg[:, b], over(m.mod[:, b, SA, :], GT), ALU.add).then_inc(s["shifted"], 1)

            def step(n, i, b, first=False, last=False):
                if not last:
                    shift(n + 1, 1 - b)
                pool.wait_ge(s["var_done"], n + 1)
                nc.gpsimd.tensor_tensor(rs[:, b], rs[:, b], m.neghalf[:, 0:GT], ALU.pow).then_inc(s["powed"], 1)
                pool.wait_ge(s["kept"], n + 1)
                nc.gpsimd.tensor_tensor(gated[:, b], gated[:, b], over(m.mod[:, b, GA, :], GT), ALU.mult).then_inc(s["gated"], 1)

            shift(0, 0)
            steps(pool, step)

        @block.vector
        def _(dve):
            st_vector()
            dve.wait_ge(s["stat4"], 1)

            def normalise(n, i, b):
                for k in range(GT):
                    t = bass.ds(b * NTB + i * GT + k, 1)
                    nc.vector.tensor_scalar(hg[:, b, k, :], m.x[:, t, :].squeeze(1), m.mean[:, t], m.rstd[:, t],
                                            ALU.subtract, ALU.mult).then_inc(s["normed"], 1)
                dve.wait_ge(s["normed"], (n + 1) * GT)
                nc.vector.tensor_tensor(hg[:, b], hg[:, b], over(m.mod[:, b, CA, :], GT), ALU.mult).then_inc(s["scaled"], 1)

            def finish(n, i, b):
                xg = m.x[:, bass.ds(b * NTB + i * GT, GT), :]
                dve.wait_ge(s["gated"], n + 1)
                nc.vector.tensor_tensor(xg, xg, gated[:, b], ALU.add).then_inc(s["x_done"], 1)
                dve.wait_ge(s["d_ready"], n + 1)
                nc.vector.tensor_tensor(m.dt[:, bass.ds(b * NTB + i * GT, GT), :],
                                        pd[:, b, 0:GT * HEADS].rearrange("p (t h) -> p t h", h=HEADS),
                                        bdt[:].unsqueeze(1).to_broadcast([P, GT, HEADS]), ALU.add).then_inc(s["d_done"], 1)

            def step(n, i, b, first=False, last=False):
                if not last:
                    if not first:
                        dve.wait_ge(s["kept"], n)
                        dve.wait_ge(s["un_done"], n * GT)
                    normalise(n + 1, i + b, 1 - b)
                dve.wait_ge(s["shifted"], n + 1)
                for k in range(GT):
                    nc.vector.bn_stats(st2[:, b, k, :], hg[:, b, k, :]).then_inc(s["st2"], 1)
                dve.wait_ge(s["st2"], (n + 1) * GT)
                if not (isinstance(n, int) and n < 2):
                    dve.wait_ge(s["x_done"], n - 1)
                nc.vector.tensor_tensor(gated[:, b], hg[:, b], over(bout[:], GT), ALU.add).then_inc(s["kept"], 1)
                for k in range(GT):
                    nc.vector.bn_aggr(mv[:, b, k, :], st2[:, b, k, :]).then_inc(s["mv"], 1)
                dve.wait_ge(s["mv"], (n + 1) * GT)
                nc.vector.tensor_scalar(rs[:, b], mv[:, b, :, 1], LN_EPS, None, ALU.add).then_inc(s["var_done"], 1)
                if not first:
                    finish(n - 1, i - 1 + b, 1 - b)
                dve.wait_ge(s["powed"], n + 1)
                if not (isinstance(n, int) and n < 2):
                    dve.wait_ge(s["t_ready"], n - 1)
                for k in range(GT):
                    nc.vector.tensor_scalar(un[:, b, k, :], hg[:, b, k, :], mv[:, b, k, 0:1], rs[:, b, k:k + 1],
                                            ALU.subtract, ALU.mult).then_inc(s["un_done"], 1)
                if last:
                    finish(n, i, b)

            normalise(0, 0, 0)
            dve.wait_ge(s["loaded"], 80)
            nc.vector.tensor_tensor(bdt[:], bdt[:], bdt2[:], ALU.add).then_inc(s["bias"], 1)
            dve.wait_ge(s["bias"], 1)
            steps(dve, step)

        @block.scalar
        def _(act):
            act.wait_ge(s["loaded"], 80)

            def group(i, b):
                n = i * B + b + 1
                act.wait_ge(s["t_ready"], n)
                if not isinstance(i, int):
                    act.wait_ge(u_out[b], 16 * i)
                    act.wait_ge(s["d_ready"], n - 2)
                for h in range(CH):
                    last = nc.scalar.activation(ug[:, b, h, :], pT[:, b, h, :], ACT.Identity,
                                                scale=gb[:, 0, h:h + 1], bias=gb[:, 1, h:h + 1])
                last.then_inc(s["t_copied"], 1)

            group(0, 0)
            group(0, 1)
            with act.Fori(1, NG) as i:
                group(i, 0)
                group(i, 1)

        @block.tensor
        def _(pe):
            pe.wait_ge(s["loaded"], 80)
            with pe.Fori(0, NG) as i:
                for b in range(B):
                    n = i * B + b + 1
                    pe.wait_ge(s["un_done"], n * GT)
                    for h in range(CH):
                        for k in range(GT):
                            last = nc.tensor.transpose(pT[:, b, h, k * P:(k + 1) * P], un[:, b, k, h * P:(h + 1) * P], m.ident[:])
                    last.then_inc(s["t_ready"], 1)
                    pe.wait_ge(s["t_copied"], n)
                    for k in range(GT):
                        for h in range(CH):
                            last = nc.tensor.matmul(pd[:, b, k * HEADS:(k + 1) * HEADS], ug[:, b, h, k * P:(k + 1) * P],
                                                    wdt[:, h, :], start=h == 0, stop=h == CH - 1)
                    last.then_inc(s["d_ready"], 1)


def decays(nc, m, w):
    with ExitStack() as ctx:
        sb, ps, sem = setup(nc, ctx)
        NC_ = NT * HEADS
        raw = m.dt[:].rearrange("p t h -> p (t h)")
        a, e, u, d, z, l, lw, dA, cum = [sb("f_" + n, [P, NC_]) for n in ("a", "e", "u", "d", "z", "l", "lw", "dA", "cum")]
        neg = sb("f_neg", [P, HEADS])
        cumT = sb("f_cumT", [P, 2, P])
        pc, psf, pt, pT = [ps("f_" + n, [P, 512]) for n in ("pc", "psf", "pt", "pT")]
        names = ("loaded a0 a1 a2 a3 a4 v0 v1 v2 v3 v4 v5 v6 v7 v8 cum_ready cum_copied t_ready t_copied suf tot").split()
        s = {n: sem("f_" + n) for n in names}
        block = ctx.enter_context(nc.Block())
        dt, wdt, ecum, cums = [m.cs[:, :, k, :] for k in range(4)]
        tiles = lambda t: t.rearrange("p (t h) -> p t h", h=HEADS)

        @block.sync
        def _(sp):
            sp.dma_start(neg[:], w["A_log"].partition_broadcast(P)).then_inc(s["loaded"], 16)
            sp.wait_ge(s["t_copied"], 1)
            sp.dma_start(m.cum_dram.rearrange("(a p) t -> p a t", p=P), cumT[:]).then_inc(s["loaded"], 16)
            sp.wait_ge(s["loaded"], 32)

        @block.scalar
        def _(act):
            nc.scalar.activation(a[:], raw, ACT.Abs).then_inc(s["a0"], 1)
            act.wait_ge(s["a0"], 1)
            nc.scalar.activation(e[:], a[:], ACT.Exp, scale=-1.0).then_inc(s["a1"], 1)
            act.wait_ge(s["loaded"], 16)
            nc.scalar.activation(neg[:], neg[:], ACT.Exp).then_inc(s["a2"], 1)
            act.wait_ge(s["v0"], 1)
            nc.scalar.activation(lw[:], u[:], ACT.Ln).then_inc(s["a3"], 1)
            act.wait_ge(s["cum_ready"], 1)
            nc.scalar.activation(ecum, tiles(pc[:, 0:NC_]), ACT.Exp)
            nc.scalar.activation(m.etot[:].rearrange("p t h -> p (t h)"), pt[0:STATE, 0:NC_], ACT.Exp)
            nc.scalar.activation(z[:], psf[:, 0:NC_], ACT.Exp).then_inc(s["a4"], 1)

        @block.vector
        def _(dve):
            dve.wait_ge(s["a1"], 1)
            nc.vector.tensor_scalar_add(u[:], e[:], 1.0).then_inc(s["v0"], 1)
            dve.wait_ge(s["v0"], 1)
            nc.vector.tensor_scalar_add(d[:], u[:], -1.0).then_inc(s["v1"], 1)
            dve.wait_ge(s["v1"], 1)
            nc.vector.tensor_scalar(z[:], d[:], 0.0, None, ALU.is_equal).then_inc(s["v2"], 1)
            dve.wait_ge(s["v2"], 1)
            nc.vector.tensor_tensor(d[:], d[:], z[:], ALU.add).then_inc(s["v3"], 1)
            dve.wait_ge(s["v3"], 1)
            nc.vector.reciprocal(d[:], d[:]).then_inc(s["v4"], 1)
            nc.vector.tensor_tensor(z[:], z[:], e[:], ALU.mult).then_inc(s["v4"], 1)
            dve.wait_ge(s["v4"], 2)
            nc.vector.tensor_tensor(d[:], d[:], e[:], ALU.mult).then_inc(s["v5"], 1)
            dve.wait_ge(s["a3"], 1)
            dve.wait_ge(s["v5"], 1)
            nc.vector.tensor_tensor(l[:], lw[:], d[:], ALU.mult).then_inc(s["v6"], 1)
            dve.wait_ge(s["v6"], 1)
            nc.vector.tensor_tensor(l[:], l[:], z[:], ALU.add).then_inc(s["v6"], 1)
            dve.wait_ge(s["v6"], 2)
            nc.vector.scalar_tensor_tensor(out=dt, in0=tiles(raw), scalar=0.0, in1=tiles(l[:]),
                                           op0=ALU.max, op1=ALU.add).then_inc(s["v7"], 1)
            dve.wait_ge(s["a2"], 1)
            dve.wait_ge(s["v7"], 1)
            nc.vector.scalar_tensor_tensor(out=tiles(dA[:]), in0=dt, scalar=-1.0,
                                           in1=neg[:].unsqueeze(1).to_broadcast([P, NT, HEADS]),
                                           op0=ALU.mult, op1=ALU.mult).then_inc(s["v8"], 1)
            dve.wait_ge(s["cum_ready"], 1)
            dve.wait_ge(s["a4"], 1)
            nc.vector.tensor_copy(cum[:], pc[:, 0:NC_]).then_inc(s["cum_copied"], 1)
            nc.vector.tensor_copy(cums, tiles(pc[:, 0:NC_]))
            nc.vector.tensor_tensor(wdt, dt, tiles(z[:]), ALU.mult)
            dve.wait_ge(s["t_ready"], 1)
            nc.vector.tensor_copy(cumT[:].rearrange("p a t -> p (a t)"), pT[:, 0:2 * P]).then_inc(s["t_copied"], 1)

        @block.tensor
        def _(pe):
            pe.wait_ge(s["v8"], 1)
            nc.tensor.matmul(pc[:, 0:NC_], m.upto[:], dA[:], start=True, stop=True)
            nc.tensor.matmul(psf[:, 0:NC_], m.after[:], dA[:], start=True, stop=True)
            nc.tensor.matmul(pt[0:STATE, 0:NC_], m.ones[:, 0:STATE], dA[:], start=True, stop=True).then_inc(s["cum_ready"], 1)
            pe.wait_ge(s["cum_copied"], 1)
            for k in range(2):
                last = nc.tensor.transpose(pT[:, k * P:(k + 1) * P], cum[:, k * P:(k + 1) * P], m.ident[:])
            last.then_inc(s["t_ready"], 1)


def state_space(nc, m, w):
    with ExitStack() as ctx:
        sb, ps, sem = setup(nc, ctx)
        win = sb("g_win", [P, CH, DT0])
        wout = sb("g_wout", [P, INNER // P, C])
        wog = sb("g_wog", [P, B, INNER // P, C])
        dskip = sb("g_dskip", [P, HEADS])
        bb = sb("g_bb", [3, 2, DT0], BF16)
        ones3 = sb("g_ones3", [3, P], BF16)
        us = sb("g_us", [P, B, CH, P])
        cs = sb("g_cs", [P, B, 4, HEADS])
        et = sb("g_et", [STATE, B, HEADS])
        cumb = sb("g_cumb", [P, B, HEADS, P])
        bc = sb("g_bc", [P, B, 2 * STATE])
        bcT = sb("g_bcT", [STATE, B, 2, P])
        wide6 = sb("g_wide", [P, 6, B, INNER])
        xs, dtx, xw, xD, zr, y = [wide6[:, k] for k in range(6)]
        b3 = wide6[0:3].rearrange("p k b n -> p (k b n)")[:, 0:3 * DT0].rearrange("p (k n) -> p k n", k=3)
        th = sb("g_th", [P, INNER])
        gm = sb("g_gm", [P, B, P])
        dd = sb("g_dd", [P, HEADS, P])
        le = sb("g_le", [P, HEADS, P])
        mt = sb("g_mt", [P, HEADS, P])
        H = sb("g_H", [STATE, B, INNER])
        yT = sb("g_yT", [P, INNER // P, P])
        pz, px, pbc, pbt, py, pi, pst, pyT = [ps("g_p" + n, [P, 512]) for n in ("z", "x", "bc", "bt", "y", "i", "st", "yT")]
        po = pyT[:, 0:C]
        names = ("loaded w0 w1 w2 w3 w4 w5 ip_ready bc_copied xs_copied th_done bt_ready bt_copied g_ready gm_done "
                 "zr_done lcm_done le_done m_done dtx_done xw_done xD_done i_ready st_ready y_ready "
                 "t1_done t2_done y_done hs_done h_done yg_done yT_ready yT_copied o_ready x_done").split()
        s = {n: sem("g_" + n) for n in names}
        u_in, cs_in = [sem(f"g_u_in{b}") for b in range(B)], [sem(f"g_cs_in{b}") for b in range(B)]
        block = ctx.enter_context(nc.Block())
        heads = lambda t: t.rearrange("p (h d) -> p h d", h=HEADS)
        wide = lambda col, p=P: col.unsqueeze(2).to_broadcast([p, HEADS, HD])

        def jobs(eng, step):
            step(None, (0, 0), (0, 1))
            step((0, 0), (0, 1), (1, 0))
            with eng.Fori(1, NTB - 1) as i:
                step((i - 1, 1), (i, 0), (i, 1))
                step((i, 0), (i, 1), (i + 1, 0))
            i = NTB - 1
            step((i - 1, 1), (i, 0), (i, 1))
            step((i, 0), (i, 1), None)
            step((i, 1), None, None)

        def num(job):
            return job[0] * B + job[1]

        @block.sync
        def _(sp):
            for dst, src in ((win, w["W_in"][:, 0:DT0].rearrange("(h p) n -> p h n", p=P)),
                             (wout, w["W_out"].rearrange("(h p) n -> p h n", p=P)),
                             (dskip, w["D_skip"].partition_broadcast(P))):
                sp.dma_start(dst[:], src).then_inc(s["loaded"], 16)
            sp.dma_start(b3[:, 0], w["b_in"][0:DT0].partition_broadcast(3)).then_inc(s["loaded"], 16)

            def stage(i, b):
                n = i * B + b
                t = b * NTB + i
                if not (isinstance(i, int) and i == 0):
                    sp.wait_ge(s["ip_ready"], n - 1)
                sp.dma_start(us[:, b], m.uT[:, :, bass.ds(t * P, P)]).then_inc(u_in[b], 16)
                if not (isinstance(i, int) and i == 0):
                    sp.wait_ge(s["lcm_done"], (n - 1) * HEADS)
                    sp.wait_ge(s["t1_done"], n - 1)
                    sp.wait_ge(s["hs_done"], n - 1)
                    sp.wait_ge(s["xw_done"], n - 1)
                sp.dma_start(cs[:, b], m.cs[:, bass.ds(t, 1)].squeeze(1)).then_inc(cs_in[b], 16)
                sp.dma_start(et[:, b], m.etot[:, bass.ds(t, 1)].squeeze(1)).then_inc(cs_in[b], 16)
                sp.dma_start(cumb[:, b].rearrange("p h t -> p (h t)"),
                             m.cum_dram[bass.ds(t * HEADS, HEADS), :].rearrange("h t -> (h t)").partition_broadcast(P)).then_inc(cs_in[b], 16)

            stage(0, 0)
            stage(0, 1)
            with sp.Fori(1, NTB) as i:
                stage(i, 0)
                stage(i, 1)

        @block.gpsimd
        def _(pool):
            def products(job):
                i, b = job
                n = num(job)
                pool.wait_ge(s["xs_copied"], n + 1)
                pool.wait_ge(cs_in[b], (i + 1) * 48)
                pool.wait_ge(s["y_ready"], least(n - 1))
                nc.gpsimd.tensor_tensor(heads(dtx[:, b]), heads(xs[:, b]), wide(cs[:, b, 0]), ALU.mult).then_inc(s["dtx_done"], 1)
                pool.wait_ge(s["st_ready"], least(n - 1))
                nc.gpsimd.tensor_tensor(heads(xw[:, b]), heads(xs[:, b]), wide(cs[:, b, 1]), ALU.mult).then_inc(s["xw_done"], 1)
                pool.wait_ge(s["t2_done"], least(n - 1))
                nc.gpsimd.tensor_tensor(heads(xD[:, b]), heads(xs[:, b]), wide(dskip[:]), ALU.mult).then_inc(s["xD_done"], 1)

            def gate(job):
                i, b = job
                n = num(job)
                pool.wait_ge(s["y_done"], n + 1)
                nc.gpsimd.tensor_tensor(y[:, b], y[:, b], zr[:, b], ALU.mult).then_inc(s["yg_done"], 1)

            pool.wait_ge(s["loaded"], 64)
            products((0, 0))

            def step(prev, cur, nxt):
                if nxt:
                    products(nxt)
                if cur:
                    gate(cur)
            jobs(pool, step)

        @block.scalar
        def _(act):
            def evacuate(job):
                i, b = job
                n = num(job)
                act.wait_ge(s["ip_ready"], n + 1)
                act.wait_ge(s["st_ready"], least(n - 1))
                nc.scalar.copy(bc[:, b], pbc[:, 0:2 * STATE]).then_inc(s["bc_copied"], 1)
                act.wait_ge(s["xD_done"], least(n - 1))
                nc.scalar.copy(xs[:, b], px[:]).then_inc(s["xs_copied"], 1)
                act.wait_ge(s["zr_done"], n)
                nc.scalar.activation(th[:], pz[:], ACT.Tanh, scale=0.5).then_inc(s["th_done"], 1)

            def by_state(job):
                i, b = job
                n = num(job)
                act.wait_ge(s["bt_ready"], n + 1)
                act.wait_ge(s["i_ready"], least(n - 1))
                nc.scalar.copy(bcT[:, b].rearrange("p a t -> p (a t)"), pbt[0:STATE, 0:2 * P]).then_inc(s["bt_copied"], 1)

            evacuate((0, 0))
            by_state((0, 0))

            def step(prev, cur, nxt):
                if cur:
                    n = num(cur)
                    act.wait_ge(s["lcm_done"], (n + 1) * HEADS)
                    act.wait_ge(s["m_done"], n)
                    nc.scalar.activation(le[:], dd[:], ACT.Exp).then_inc(s["le_done"], 1)
                if nxt:
                    evacuate(nxt)
                if prev:
                    n = num(prev)
                    act.wait_ge(s["yT_ready"], n + 1)
                    act.wait_ge(s["o_ready"], n)
                    nc.scalar.copy(yT[:].rearrange("p k t -> p (k t)"), pyT[:]).then_inc(s["yT_copied"], 1)
                if nxt:
                    by_state(nxt)
            jobs(act, step)

        @block.vector
        def _(dve):
            dve.wait_ge(s["loaded"], 64)
            nc.vector.memset(ones3[:], 1.0)
            nc.vector.memset(H[:], 0.0)
            for b in range(B):
                nc.vector.scalar_tensor_tensor(out=wog[:, b], in0=wout[:], scalar=0.5, in1=over(m.mod[:, b, GA, :], INNER // P),
                                               op0=ALU.mult, op1=ALU.mult)
            for k in range(2):
                nc.vector.tensor_copy(bb[:, k], b3[:, k]).then_inc(s["w0"], 1)
                dve.wait_ge(s["w0"], k + 1)
                nc.vector.tensor_tensor(b3[:, k + 1], b3[:, k], bb[:, k], ALU.subtract).then_inc(s["w1"], 1)
                dve.wait_ge(s["w1"], k + 1)
            i3 = m.ident[0:3, :]
            nc.vector.tensor_scalar(b3[:, 0], bb[:, 0], i3[:, 0:1], None, ALU.mult).then_inc(s["w2"], 1)
            dve.wait_ge(s["w2"], 1)
            nc.vector.scalar_tensor_tensor(out=b3[:, 0], in0=bb[:, 1], scalar=i3[:, 1:2], in1=b3[:, 0],
                                           op0=ALU.mult, op1=ALU.add).then_inc(s["w3"], 1)
            dve.wait_ge(s["w3"], 1)
            nc.vector.scalar_tensor_tensor(out=bb[:, 0], in0=b3[:, 2], scalar=i3[:, 2:3], in1=b3[:, 0],
                                           op0=ALU.mult, op1=ALU.add).then_inc(s["w4"], 1)

            def gates(job):
                i, b = job
                n = num(job)
                dve.wait_ge(s["th_done"], n + 1)
                dve.wait_ge(s["yg_done"], least(n - 1))
                nc.vector.scalar_tensor_tensor(out=zr[:, b], in0=th[:], scalar=1.0, in1=pz[:],
                                               op0=ALU.add, op1=ALU.mult).then_inc(s["zr_done"], 1)
                dve.wait_ge(s["g_ready"], n + 1)
                nc.vector.tensor_tensor(gm[:, b], pbc[:, 2 * P:3 * P], m.upto[:], ALU.mult).then_inc(s["gm_done"], 1)

            def decay(job):
                i, b = job
                n = num(job)
                dve.wait_ge(cs_in[b], (i + 1) * 48)
                dve.wait_ge(s["le_done"], n)
                for h in range(HEADS):
                    nc.vector.tensor_scalar(dd[:, h, :], cumb[:, b, h, :], cs[:, b, 3, h:h + 1], 0.0,
                                            ALU.subtract, ALU.min).then_inc(s["lcm_done"], 1)

            def body(job):
                i, b = job
                n = num(job)
                dve.wait_ge(s["le_done"], n + 1)
                dve.wait_ge(s["gm_done"], n + 1)
                dve.wait_ge(s["y_ready"], n)
                nc.vector.tensor_tensor(mt[:], le[:], over(gm[:, b], HEADS), ALU.mult).then_inc(s["m_done"], 1)
                dve.wait_ge(s["i_ready"], n + 1)
                nc.vector.tensor_tensor(heads(y[:, b]), heads(pi[:]), wide(cs[:, b, 2]), ALU.mult).then_inc(s["t1_done"], 1)
                dve.wait_ge(s["h_done"], n)
                nc.vector.tensor_tensor(heads(H[:, b]), heads(H[:, b]), wide(et[:, b], STATE), ALU.mult).then_inc(s["hs_done"], 1)
                dve.wait_ge(s["hs_done"], n + 1)
                dve.wait_ge(s["st_ready"], n + 1)
                nc.vector.tensor_tensor(H[:, b], H[:, b], pst[0:STATE, :], ALU.add).then_inc(s["h_done"], 1)
                dve.wait_ge(s["y_ready"], n + 1)
                dve.wait_ge(s["xD_done"], n + 1)
                nc.vector.tensor_tensor(xD[:, b], py[:], xD[:, b], ALU.add).then_inc(s["t2_done"], 1)
                dve.wait_ge(s["t2_done"], n + 1)
                nc.vector.tensor_tensor(y[:, b], y[:, b], xD[:, b], ALU.add).then_inc(s["y_done"], 1)

            def finish(job):
                i, b = job
                n = num(job)
                t = bass.ds(b * NTB + i, 1)
                xt = m.x[:, t, :].squeeze(1)
                dve.wait_ge(s["o_ready"], n + 1)
                nc.vector.tensor_tensor(xt, xt, po, ALU.add).then_inc(s["x_done"], 1)
                dve.wait_ge(s["x_done"], n + 1)
                nc.vector.bn_stats(m.st[:, t, :].squeeze(1), xt)

            gates((0, 0))

            def step(prev, cur, nxt):
                if cur:
                    decay(cur)
                    body(cur)
                if nxt:
                    gates(nxt)
                if prev:
                    finish(prev)
            jobs(dve, step)

        @block.tensor
        def _(pe):
            pe.wait_ge(s["w4"], 1)

            def project(job):
                i, b = job
                n = num(job)
                pe.wait_ge(u_in[b], (i + 1) * 16)
                pe.wait_ge(s["gm_done"], n)
                pe.wait_ge(s["zr_done"], n)
                pe.wait_ge(s["xs_copied"], n)
                for dst, o, width in ((pbc, ZX, 2 * STATE), (px, INNER, INNER), (pz, 0, INNER)):
                    for k in range(CH):
                        nc.tensor.matmul(dst[:, 0:width], us[:, b, k, :], win[:, k, o:o + width], start=k == 0, stop=False)
                    last = nc.tensor.matmul(dst[:, 0:width], ones3[:], bb[:, 0, o:o + width], start=False, stop=True)
                last.then_inc(s["ip_ready"], 1)

            def state_rows(job):
                i, b = job
                for k in range(2):
                    last = nc.tensor.transpose(pbt[0:STATE, k * P:(k + 1) * P], bc[:, b, k * STATE:(k + 1) * STATE], m.ident[:])
                last.then_inc(s["bt_ready"], 1)

            def await_bc(job):
                pe.wait_ge(s["bc_copied"], num(job) + 1)
                pe.wait_ge(s["bt_copied"], num(job))

            def correlate(job):
                i, b = job
                n = num(job)
                pe.wait_ge(s["bt_copied"], n + 1)
                nc.tensor.matmul(pbc[:, 2 * P:3 * P], bcT[:, b, 0, :], bcT[:, b, 1, :], start=True, stop=True).then_inc(s["g_ready"], 1)

            project((0, 0))
            await_bc((0, 0))
            state_rows((0, 0))
            correlate((0, 0))

            def step(prev, cur, nxt):
                if nxt:
                    project(nxt)
                if prev:
                    i, b = prev
                    n = num(prev)
                    pe.wait_ge(s["yg_done"], n + 1)
                    pe.wait_ge(s["x_done"], n)
                    for k in range(INNER // P):
                        last = nc.tensor.transpose(pyT[:, k * P:(k + 1) * P], y[:, b, k * P:(k + 1) * P], m.ident[:])
                    last.then_inc(s["yT_ready"], 1)
                if cur:
                    i, b = cur
                    n = num(cur)
                    pe.wait_ge(s["h_done"], n)
                    pe.wait_ge(s["t1_done"], n)
                    nc.tensor.matmul(pi[:], bcT[:, b, 1, :], H[:, b], start=True, stop=True).then_inc(s["i_ready"], 1)
                    pe.wait_ge(s["xw_done"], n + 1)
                    if nxt:
                        await_bc(nxt)
                    nc.tensor.matmul(pst[0:STATE, :], bc[:, b, 0:STATE], xw[:, b], start=True, stop=True).then_inc(s["st_ready"], 1)
                if nxt:
                    state_rows(nxt)
                if cur:
                    pe.wait_ge(s["m_done"], n + 1)
                    pe.wait_ge(s["dtx_done"], n + 1)
                    pe.wait_ge(s["t2_done"], n)
                    for h in range(HEADS):
                        last = nc.tensor.matmul(py[:, h * HD:(h + 1) * HD], mt[:, h, :], dtx[:, b, h * HD:(h + 1) * HD],
                                                start=True, stop=True)
                    last.then_inc(s["y_ready"], 1)
                if nxt:
                    correlate(nxt)
                if prev:
                    i, b = prev
                    n = num(prev)
                    pe.wait_ge(s["yT_copied"], n + 1)
                    for k in range(INNER // P):
                        last = nc.tensor.matmul(po, yT[:, k, :], wog[:, b, k, :], start=k == 0, stop=k == INNER // P - 1)
                    last.then_inc(s["o_ready"], 1)
            jobs(pe, step)


EX = 16
FE = 512
FT = FE // P
CAP = T * 2 // EX
ROW = C + EX
RX = B * EX
BITS = 30
RADIX = 16


def routing_scores(nc, m, w):
    with ExitStack() as ctx:
        sb, ps, sem = setup(nc, ctx)
        NJ, NBUF = NG * B, NG * B
        hx = sb("h_hx", [P, NBUF, GT, ROW])
        gw = sb("h_gw", [P, CH, EX])
        mx, sm = sb("h_mx", [P, 2, GT]), sb("h_sm", [P, 2, GT])
        lg, ex = sb("h_lg", [P, 2, GT, EX]), sb("h_ex", [P, 2, GT, EX])
        by_tile = sb("h_by_tile", [P, NTB, B, EX])
        pT = ps("h_pT", [P, 2, CH, GW])
        pg = ps("h_pg", [P, 2, 512])
        pS = ps("h_pS", [RX, 2, 512])
        names = ("loaded stat0 stat1 stat2 stat3 stat4 normed scaled shifted t_ready t_copied g_ready mx_done lg_done ex_done "
                 "sm_done rs_done sc_done bt_done s_ready s_copied shared_in").split()
        s = {n: sem("h_" + n) for n in names}
        rows_out = [sem(f"h_rows{q}") for q in range(NBUF)]
        block = ctx.enter_context(nc.Block())
        st_vector, st_gpsimd = finish_stats(nc, [s[f"stat{i}"] for i in range(5)], m, 0, NT)

        def tiles(n):
            first = n % B * NTB + n // B * GT
            return slice(first, first + GT)

        @block.sync
        def _(sp):
            sp.dma_start(gw[:], w["gate_wT"].rearrange("(h p) n -> p h n", p=P)).then_inc(s["loaded"], 16)
            for dst, src in ((m.wg, w["Ws_gT"]), (m.wu, w["Ws_uT"]), (m.wd, w["Ws_dT"])):
                sp.dma_start(dst[:], src.rearrange("(h p) n -> p h n", p=P)).then_inc(s["shared_in"], 16)
            for n in range(NJ):
                sp.wait_ge(s["sc_done"], n + 1)
                sp.dma_start(m.rows.rearrange("(t p) c -> p t c", p=P)[:, tiles(n), :], hx[:, n % NBUF]).then_inc(rows_out[n % NBUF], 16)
            sp.wait_ge(s["shared_in"], 48)
            for q in range(NBUF):
                sp.wait_ge(rows_out[q], 16 * NJ // NBUF)

        @block.gpsimd
        def _(pool):
            st_gpsimd()
            for n in range(NJ):
                hb = hx[:, n % NBUF, :, 0:C]
                pool.wait_ge(s["scaled"], n + 1)
                nc.gpsimd.tensor_tensor(hb, hb, over(m.mod[:, n % B, SB, :], GT), ALU.add).then_inc(s["shifted"], 1)

        @block.vector
        def _(dve):
            st_vector()
            dve.wait_ge(s["stat4"], 1)

            def normalise(n):
                if n >= NBUF:
                    dve.wait_ge(rows_out[n % NBUF], n // NBUF * 16)
                for k in range(GT):
                    t = slice(tiles(n).start + k, tiles(n).start + k + 1)
                    nc.vector.tensor_scalar(hx[:, n % NBUF, k, 0:C], m.x[:, t, :].squeeze(1), m.mean[:, t], m.rstd[:, t],
                                            ALU.subtract, ALU.mult).then_inc(s["normed"], 1)
                dve.wait_ge(s["normed"], (n + 1) * GT)
                hb = hx[:, n % NBUF, :, 0:C]
                nc.vector.tensor_tensor(hb, hb, over(m.mod[:, n % B, CB, :], GT), ALU.mult).then_inc(s["scaled"], 1)

            col = lambda t, n: t[:, n % 2].unsqueeze(2).to_broadcast([P, GT, EX])

            def centre(n):
                dve.wait_ge(s["g_ready"], n + 1)
                pl = pg[:, n % 2, 0:GT * EX].rearrange("p (t e) -> p t e", e=EX)
                nc.vector.tensor_reduce(mx[:, n % 2], pl, AX, ALU.max).then_inc(s["mx_done"], 1)
                dve.wait_ge(s["mx_done"], n + 1)
                nc.vector.tensor_tensor(lg[:, n % 2], pl, col(mx, n), ALU.subtract).then_inc(s["lg_done"], 1)

            def scores(n):
                e = ex[:, n % 2]
                dve.wait_ge(s["ex_done"], n + 1)
                nc.vector.tensor_reduce(sm[:, n % 2], e, AX, ALU.add).then_inc(s["sm_done"], 1)
                dve.wait_ge(s["sm_done"], n + 1)
                nc.vector.reciprocal(sm[:, n % 2], sm[:, n % 2]).then_inc(s["rs_done"], 1)
                dve.wait_ge(s["rs_done"], n + 1)
                nc.vector.tensor_tensor(hx[:, n % NBUF, :, C:ROW], e, col(sm, n), ALU.mult).then_inc(s["sc_done"], 1)
                nc.vector.tensor_tensor(by_tile[:, n // B * GT:(n // B + 1) * GT, n % B, :], e, col(sm, n), ALU.mult).then_inc(s["bt_done"], 1)

            def keep_scores(g):
                dve.wait_ge(s["s_ready"], g + 1)
                nc.vector.tensor_copy(m.sc[:, g * GW:(g + 1) * GW], pS[:, g % 2, :]).then_inc(s["s_copied"], 1)

            normalise(0)
            normalise(1)
            for n in range(NJ):
                if n + 2 < NJ:
                    normalise(n + 2)
                centre(n)
                if n:
                    scores(n - 1)
                if n >= 5 and n % 2:
                    keep_scores((n - 5) // 2)
            scores(NJ - 1)
            keep_scores(NG - 2)
            keep_scores(NG - 1)

        @block.scalar
        def _(act):
            def copy_t(n):
                act.wait_ge(s["t_ready"], n + 1)
                nc.scalar.copy(m.hT[:, :, tiles(n).start * P:tiles(n).stop * P], pT[:, n % 2]).then_inc(s["t_copied"], 1)

            copy_t(0)
            for n in range(NJ):
                if n + 1 < NJ:
                    copy_t(n + 1)
                act.wait_ge(s["lg_done"], n + 1)
                if n >= 2:
                    act.wait_ge(s["bt_done"], n - 1)
                nc.scalar.activation(ex[:, n % 2], lg[:, n % 2], ACT.Exp).then_inc(s["ex_done"], 1)

        @block.tensor
        def _(pe):
            def transposes(n):
                pe.wait_ge(s["shifted"], n + 1)
                if n >= 2:
                    pe.wait_ge(s["t_copied"], n - 1)
                for h in range(CH):
                    for k in range(GT):
                        last = nc.tensor.transpose(pT[:, n % 2, h, k * P:(k + 1) * P], hx[:, n % NBUF, k, h * P:(h + 1) * P], m.ident[:])
                last.then_inc(s["t_ready"], 1)

            def logits(n):
                pe.wait_ge(s["t_copied"], n + 1)
                if n >= 2:
                    pe.wait_ge(s["lg_done"], n - 1)
                for k in range(GT):
                    for h in range(CH):
                        tok = slice((tiles(n).start + k) * P, (tiles(n).start + k + 1) * P)
                        last = nc.tensor.matmul(pg[:, n % 2, k * EX:(k + 1) * EX], m.hT[:, h, tok], gw[:, h, :],
                                                start=h == 0, stop=h == CH - 1)
                last.then_inc(s["g_ready"], 1)

            def by_expert(g):
                pe.wait_ge(s["bt_done"], (g + 1) * B)
                if g >= 2:
                    pe.wait_ge(s["s_copied"], g - 1)
                for k in range(GT):
                    last = nc.tensor.transpose(pS[:, g % 2, k * P:(k + 1) * P],
                                               by_tile[:, g * GT + k].rearrange("p b e -> p (b e)"), m.ident[:])
                last.then_inc(s["s_ready"], 1)

            pe.wait_ge(s["loaded"], 16)
            transposes(0)
            for n in range(NJ):
                if n + 1 < NJ:
                    transposes(n + 1)
                logits(n)
                if n >= 3 and n % 2:
                    by_expert((n - 3) // 2)
            by_expert(NG - 1)


def shared_and_choice(nc, m, w, out):
    with ExitStack() as ctx:
        sb, ps, sem = setup(nc, ctx)
        act_g = sb("i_act_g", [P, 2, GW])
        hid = sb("i_hid", [P, B, FT, GW])
        ob = sb("i_ob", [P, B, GT, C])
        prefix, cand, add = [sb("i_" + n, [RX, 1], I32) for n in ("prefix", "cand", "add")]
        bits = sb("i_bits", [RX, BITS], I32)
        cnt, room = sb("i_cnt", [RX, 1]), sb("i_room", [RX, 1])
        junk = sb("i_junk", [RX, T])
        place = junk[:]
        NP, NQ = NTB * RX, 4
        A = sb("j_A", [P, NTB, RX, RADIX], BF16)
        R = sb("j_R", [P, NTB, RX, 2, RADIX], BF16)
        flat = A[0:RX].rearrange("p t e a -> p (t e a)").bitcast(F32)
        eq, rank = flat[:, 0:T], flat[:, T:2 * T]
        pl = sb("j_pl", [P, NP], I32)
        upper, lower = sb("j_upper", [P, NP], I32), sb("j_lower", [P, NP], I32)
        io, lid = sb("j_io", [P, RADIX]), sb("j_lid", [P, 1])
        dmask = sb("j_dmask", [P, 8])
        mk = sb("j_mk", [P, NQ, 8, 2 * RADIX])
        red = sb("j_red", [P, NQ, 2 * RADIX])
        ix = sb("j_ix", [P, NQ, RADIX])
        rows = sb("j_rows", [2 * RX, P])
        pg, pu, po = ps("i_pg", [P, 2, GW]), ps("i_pu", [P, 2, GW]), ps("i_po", [P, GT, C])
        pI = ps("j_pI", [P, NQ, 8 * 2 * RADIX])
        pW = pI[:, 0:2].rearrange("p q n -> p (q n)")
        pX = pI[:, 0, 0:2 * RX]
        names = ("gu_ready gelu_done hid_done o_ready ga_done ob_done bit0 bits cand cnt add prefix c0 c1 c2 c3 c4 c5 c6 placed "
                 "io w_ready w_done ul A0 B0 R0 R1 i_ready mk red ix rows_in x_ready dm").split()
        s = {n: sem("i_" + n) for n in names}
        stored = [sem(f"i_stored{b}") for b in range(B)]
        block = ctx.enter_context(nc.Block())
        NJ = NG * B
        SEARCHED = 5
        PER = BITS // SEARCHED
        CHUNKS = 4
        part = lambda t, c: t[:, c * NTB // CHUNKS:(c + 1) * NTB // CHUNKS]
        merged = lambda t: t.rearrange("p t e a -> p (t e) a")
        digit = lambda t, c: t[:, c * NP // CHUNKS:(c + 1) * NP // CHUNKS].unsqueeze(2).to_broadcast([P, NP // CHUNKS, RADIX])

        def groups(eng, group):
            with eng.Fori(0, SEARCHED // B) as i:
                for b in range(B):
                    group(i * B + b, i, b)
            for g in range(SEARCHED // B * B, NJ):
                group(g, g // B, g % B)

        @block.sync
        def _(sp):
            def group(g, i, b):
                sp.wait_ge(s["ob_done"], g + 1)
                sp.dma_start(out.rearrange("(t p) c -> p t c", p=P)[:, bass.ds(b * NTB + i * GT, GT), :],
                             ob[:, b]).then_inc(stored[b], 16)
            groups(sp, group)
            sp.wait_ge(s["ix"], 1)
            for q in range(NQ):
                sp.dma_start(rows[q * 16:(q + 1) * 16, :].rearrange("r (a b) -> r a b", a=8), ix[:, q, :]).then_inc(s["rows_in"], 16)
            for b in range(B):
                sp.wait_ge(stored[b], 16 * NG)

        @block.gpsimd
        def _(pool):
            g = nc.gpsimd
            g.iota(io[:], pattern=[[1, RADIX]], base=0, channel_multiplier=0, allow_small_or_imprecise_dtypes=True).then_inc(s["io"], 1)
            g.iota(lid[:], pattern=[[0, 1]], base=0, channel_multiplier=1, allow_small_or_imprecise_dtypes=True).then_inc(s["io"], 1)
            g.memset(dmask[:], 1.0).then_inc(s["dm"], 1)
            pool.wait_ge(s["dm"], 1)
            g.affine_select(out=dmask[:], in_=dmask[:], compare_op=ALU.is_ge, fill=0.0, base=0,
                            pattern=[[-RADIX, 8]], channel_multiplier=1).then_inc(s["dm"], 1)
            pool.wait_ge(s["dm"], 2)
            g.affine_select(out=dmask[:], in_=dmask[:], compare_op=ALU.is_ge, fill=0.0, base=RADIX - 1,
                            pattern=[[RADIX, 8]], channel_multiplier=-1).then_inc(s["dm"], 1)

        @block.scalar
        def _(act):
            def group(g, i, b):
                for f in range(FT):
                    n = g * FT + f
                    act.wait_ge(s["gu_ready"], n + 1)
                    act.wait_ge(s["hid_done"], n - 1) if (f >= 2) else act.wait_ge(s["hid_done"], g * FT)
                    nc.scalar.activation(act_g[:, f % 2], pg[:, f % 2], ACT.Gelu).then_inc(s["gelu_done"], 1)
                    if isinstance(g, int) and g == NJ - 1:
                        places(f)

            def places(c):
                act.wait_ge(s["R0"], (c + 1) * NTB // CHUNKS * B)
                one = merged(part(R, c)[:, :, :, 1, :])
                nc.scalar.activation(one, one, ACT.Copy, scale=lid[:]).then_inc(s["R1"], 1)

            act.wait_ge(s["io"], 2)
            groups(act, group)

        @block.tensor
        def _(pe):
            def group(g, i, b):
                at = g if isinstance(g, int) else None
                for f in range(FT):
                    n = g * FT + f
                    if f >= 2:
                        pe.wait_ge(s["hid_done"], n - 1)
                    else:
                        pe.wait_ge(s["hid_done"], g * FT)
                    for dst, wt in ((pg, m.wg), (pu, m.wu)):
                        for k in range(CH):
                            last = nc.tensor.matmul(dst[:, f % 2], wt[:, k, f * P:(f + 1) * P],
                                                    m.hT[:, k, bass.ds(b * T + i * GW, GW)], start=k == 0, stop=k == CH - 1)
                    last.then_inc(s["gu_ready"], 1)
                    if at == NJ - 2 and f == 0:
                        by_token()
                    if at == NJ - 1 and f == FT - 1:
                        products()
                pe.wait_ge(s["hid_done"], (g + 1) * FT)
                pe.wait_ge(s["ga_done"], g)
                for t in range(GT):
                    for f in range(FT):
                        last = nc.tensor.matmul(po[:, t], hid[:, b, f, t * P:(t + 1) * P], m.wd[:, f, :],
                                                start=f == 0, stop=f == FT - 1)
                last.then_inc(s["o_ready"], 1)

            def by_token():
                pe.wait_ge(s["placed"], 1)
                for t in range(NTB):
                    last = nc.tensor.transpose(pW[:, t * RX:(t + 1) * RX], place[:, t * P:(t + 1) * P], m.ident[0:RX, 0:RX])
                last.then_inc(s["w_ready"], 1)

            def products():
                pe.wait_ge(s["R1"], CHUNKS)
                pe.wait_ge(s["A0"], CHUNKS)
                for q in range(NQ):
                    for t in range(NTB):
                        last = nc.tensor.matmul(pI[:, q], A[:, t, q * 8:(q + 1) * 8, :].rearrange("p e a -> p (e a)"),
                                                R[:, t, q * 8:(q + 1) * 8].rearrange("p e k b -> p (e k b)"),
                                                start=t == 0, stop=t == NTB - 1)
                last.then_inc(s["i_ready"], 1)

            groups(pe, group)
            pe.wait_ge(s["rows_in"], 16 * NQ)
            nc.tensor.transpose(pX, rows[:], m.ident[0:2 * RX, 0:2 * RX]).then_inc(s["x_ready"], 1)

        @block.vector
        def _(dve):
            v = nc.vector
            prefix_f, cand_f = prefix[:].bitcast(F32), cand[:].bitcast(F32)
            v.memset(prefix[:], 0)
            v.memset(bits[:, 0:1], 1 << (BITS - 1)).then_inc(s["bit0"], 1)
            dve.wait_ge(s["bit0"], 1)
            for k in range(1, BITS):
                last = v.tensor_scalar(bits[:, k:k + 1], bits[:, 0:1], k, None, ALU.logical_shift_right)
            last.then_inc(s["bits"], 1)
            dve.wait_ge(s["bits"], 1)

            def search(j):
                bit = bits[:, bass.ds(j, 1)]
                dve.wait_ge(s["prefix"], j)
                v.tensor_tensor(cand[:], prefix[:], bit, ALU.bitwise_or).then_inc(s["cand"], 1)
                dve.wait_ge(s["cand"], j + 1)
                v.tensor_scalar(junk[:], m.sc[:], cand_f, 0.0, ALU.is_ge, ALU.add, accum_out=cnt[:]).then_inc(s["cnt"], 1)
                dve.wait_ge(s["cnt"], j + 1)
                v.scalar_tensor_tensor(out=add[:], in0=cnt[:], scalar=float(CAP), in1=bit, op0=ALU.is_ge, op1=ALU.mult).then_inc(s["add"], 1)
                dve.wait_ge(s["add"], j + 1)
                v.tensor_tensor(prefix[:], prefix[:], add[:], ALU.bitwise_or).then_inc(s["prefix"], 1)

            def choose(f):
                if f == 0:
                    dve.wait_ge(s["prefix"], BITS)
                    v.tensor_scalar(junk[:], m.sc[:], prefix_f, 0.0, ALU.is_gt, ALU.add, accum_out=cnt[:]).then_inc(s["c0"], 1)
                    v.tensor_scalar(eq, m.sc[:], prefix_f, None, ALU.is_equal).then_inc(s["c1"], 1)
                if f == 1:
                    dve.wait_ge(s["c1"], 1)
                    v.tensor_tensor_scan(rank, eq, eq, 0.0, ALU.add, ALU.bypass).then_inc(s["c2"], 1)
                    dve.wait_ge(s["c0"], 1)
                    v.tensor_scalar(room[:], cnt[:], -1.0, float(CAP), ALU.mult, ALU.add).then_inc(s["c3"], 1)
                if f == 2:
                    dve.wait_ge(s["c2"], 1)
                    dve.wait_ge(s["c3"], 1)
                    v.scalar_tensor_tensor(out=eq, in0=rank, scalar=room[:], in1=eq, op0=ALU.is_le, op1=ALU.mult).then_inc(s["c4"], 1)
                    dve.wait_ge(s["c4"], 1)
                    v.tensor_tensor(eq, eq, junk[:], ALU.add).then_inc(s["c5"], 1)
                if f == 3:
                    dve.wait_ge(s["c5"], 1)
                    v.tensor_tensor_scan(rank, eq, eq, 0.0, ALU.add, ALU.bypass).then_inc(s["c6"], 1)
                    dve.wait_ge(s["c6"], 1)
                    v.tensor_tensor(place, rank, eq, ALU.mult).then_inc(s["placed"], 1)

            def digits():
                dve.wait_ge(s["w_ready"], 1)
                v.tensor_scalar(pl[:], pW, -1.0, None, ALU.add).then_inc(s["w_done"], 1)
                dve.wait_ge(s["w_done"], 1)
                v.tensor_scalar(upper[:], pl[:], 4, None, ALU.arith_shift_right).then_inc(s["ul"], 1)
                v.tensor_scalar(lower[:], pl[:], RADIX - 1, None, ALU.bitwise_and).then_inc(s["ul"], 1)

            def upper_table(c):
                dve.wait_ge(s["ul"], 2)
                dve.wait_ge(s["io"], 2)
                v.tensor_tensor(merged(part(A, c)), digit(upper, c),
                                io[:].unsqueeze(1).to_broadcast([P, NP // CHUNKS, RADIX]), ALU.is_equal).then_inc(s["A0"], 1)

            def lower_table(c):
                dve.wait_ge(s["ul"], 2)
                v.tensor_tensor(merged(part(R, c)[:, :, :, 1, :]), digit(lower, c),
                                io[:].unsqueeze(1).to_broadcast([P, NP // CHUNKS, RADIX]), ALU.is_equal).then_inc(s["B0"], 1)
                dve.wait_ge(s["B0"], c + 1)
                for t in range(c * NTB // CHUNKS, (c + 1) * NTB // CHUNKS):
                    for b in range(B):
                        e = slice(b * EX, (b + 1) * EX)
                        v.tensor_scalar(R[:, t, e, 0, :], R[:, t, e, 1, :], float(b * NTB + t), None, ALU.mult).then_inc(s["R0"], 1)

            def lists():
                dve.wait_ge(s["i_ready"], 1)
                dve.wait_ge(s["dm"], 3)
                for q in range(NQ):
                    v.tensor_tensor(mk[:, q], pI[:, q].rearrange("p (e k) -> p e k", e=8),
                                    dmask[:].unsqueeze(2).to_broadcast([P, 8, 2 * RADIX]), ALU.mult).then_inc(s["mk"], 1)
                dve.wait_ge(s["mk"], NQ)
                v.tensor_reduce(red[:], mk[:].rearrange("p q e k -> p q k e"), AX, ALU.add).then_inc(s["red"], 1)
                dve.wait_ge(s["red"], 1)
                v.scalar_tensor_tensor(out=ix[:], in0=red[:, :, 0:RADIX], scalar=float(P), in1=red[:, :, RADIX:],
                                       op0=ALU.mult, op1=ALU.add).then_inc(s["ix"], 1)

            def group(g, i, b):
                at = g if isinstance(g, int) else None
                for f in range(FT):
                    n = g * FT + f
                    dve.wait_ge(s["gelu_done"], n + 1)
                    dve.wait_ge(s["o_ready"], g)
                    v.tensor_tensor(hid[:, b, f], act_g[:, f % 2], pu[:, f % 2], ALU.mult).then_inc(s["hid_done"], 1)
                    if at is None or at < SEARCHED:
                        for j in range(f * PER // FT, (f + 1) * PER // FT):
                            search(g * PER + j)
                    elif at == SEARCHED:
                        choose(f)
                    elif at == NJ - 2 and f == 1:
                        digits()
                    elif at == NJ - 2 and f == 2:
                        upper_table(0)
                    elif at == NJ - 2 and f == 3:
                        lower_table(0)
                    elif at == NJ - 1 and f == 0:
                        lower_table(2)
                    elif at == NJ - 1 and f == 1:
                        upper_table(3)
                    elif at == NJ - 1 and f == 2:
                        lower_table(3)
                if at == NJ - 2:
                    upper_table(1)
                    lower_table(1)
                    upper_table(2)
                if at == NJ - 1:
                    lists()
                dve.wait_ge(s["o_ready"], g + 1)
                if not (isinstance(i, int) and i == 0):
                    dve.wait_ge(stored[b], 16 * i)
                v.tensor_tensor(ob[:, b], po[:], over(m.mod[:, b, GB, :], GT), ALU.mult).then_inc(s["ga_done"], 1)
                dve.wait_ge(s["ga_done"], g + 1)
                v.tensor_tensor(ob[:, b], ob[:, b], m.x[:, bass.ds(b * NTB + i * GT, GT), :], ALU.add).then_inc(s["ob_done"], 1)

            groups(dve, group)
            dve.wait_ge(s["x_ready"], 1)
            v.tensor_copy(m.idx[:], pX)


def experts(nc, m, w, out):
    with ExitStack() as ctx:
        sb, ps, sem = setup(nc, ctx)
        NTOK = B * CAP // P
        xe, score = sb("k_xe", [P, 2, NTOK, ROW]), sb("k_score", [P, 2, NTOK, EX])
        xh, xl = sb("k_xh", [P, 2, CH, GW], FR), sb("k_xl", [P, 2, CH, GW], FR)
        WN = CH * FE
        wf = sb("k_wf", [P, 2, 3, WN])
        wh, wl = sb("k_wh", [P, 2, 3, WN], FR), sb("k_wl", [P, 2, 3, WN], FR)
        act_g = sb("k_act_g", [P, 2, GW])
        hid = sb("k_hid", [P, 2, GW])
        hh, hl = sb("k_hh", [P, 2, FT, GW], FR), sb("k_hl", [P, 2, FT, GW], FR)
        eo = sb("k_eo", [P, 2, NTOK, C])
        pg, pu, po, pT = ps("k_pg", [P, 2, GW]), ps("k_pu", [P, 2, GW]), ps("k_po", [P, NTOK, C]), ps("k_pT", [P, CH, GW])
        names = "t_ready xh_done xl_done wh_done wl_done gu_ready gelu_done hid_done hh_done hl_done o_ready eo_done score_kept".split()
        s = {n: sem("k_" + n) for n in names}
        gathered, w_in, added = [[sem(f"k_{n}{k}") for k in range(2)] for n in ("gathered", "w_in", "added")]
        block = ctx.enter_context(nc.Block())

        def column(e, t):
            b, half = divmod(t, 2)
            return m.idx[:, (b * EX + e) * 2 + half:(b * EX + e) * 2 + half + 1]

        def steps(eng, step):
            step(0, 0)
            step(0, 1)
            with eng.Fori(1, EX // 2 - 1) as i:
                step(i, 0)
                step(i, 1)
            step(EX // 2 - 1, 0)
            step(EX // 2 - 1, 1, True)

        def early(i):
            return isinstance(i, int) and i == 0

        @block.sync
        def _(sp):
            def load(i, k):
                e = i * 2 + k
                for j, name in enumerate(("WgT", "WuT", "WdT")):
                    src = w[name][bass.ds(e, 1)].squeeze(0).rearrange("(h p) n -> p h n", p=P)
                    sp.dma_start(wf[:, k, j].rearrange("p (h n) -> p h n", n=src.shape[-1]), src).then_inc(w_in[k], 16)
            load(0, 0)
            load(0, 1)
            with sp.Fori(1, EX // 2) as i:
                for k in range(2):
                    sp.wait_ge(s["wl_done"], ((i - 1) * 2 + k + 1) * 3)
                    load(i, k)

        @block.gpsimd
        def _(pool):
            def gather(e):
                if e >= 2:
                    pool.wait_ge(s["t_ready"], e - 1)
                    pool.wait_ge(s["score_kept"], e - 1)
                for t in range(NTOK):
                    nc.gpsimd.indirect_dma_start(out=xe[:, e % 2, t, :], out_offset=None, in_=m.rows,
                                                 in_offset=bass.IndirectOffsetOnAxis(ap=column(e, t), axis=0)).then_inc(gathered[e % 2], 16)

            gather(0)
            gather(1)
            for e in range(EX):
                if e + 2 < EX:
                    gather(e + 2)
                pool.wait_ge(s["eo_done"], e + 1)
                if e:
                    pool.wait_ge(added[(e - 1) % 2], 16 * NTOK * ((e - 1) // 2 + 1))
                for t in range(NTOK):
                    nc.gpsimd.indirect_dma_start(out=out, out_offset=bass.IndirectOffsetOnAxis(ap=column(e, t), axis=0),
                                                 in_=eo[:, e % 2, t, :], in_offset=None,
                                                 compute_op=ALU.add).then_inc(added[e % 2], 16)
            for k in range(2):
                pool.wait_ge(added[k], 16 * NTOK * EX // 2)

        @block.scalar
        def _(act):
            def rows_high(i, k):
                act.wait_ge(s["t_ready"], i * 2 + k + 1)
                nc.scalar.copy(xh[:, k], pT[:]).then_inc(s["xh_done"], 1)

            def weights_high(i, k, j):
                if j == 0:
                    act.wait_ge(w_in[k], 48 * (i + 1))
                if j == 2 and not early(i):
                    act.wait_ge(s["o_ready"], i * 2 + k - 1)
                nc.scalar.copy(wh[:, k, j], wf[:, k, j]).then_inc(s["wh_done"], 1)

            def hidden_high(i, k, f):
                e = i * 2 + k
                act.wait_ge(s["hid_done"], e * FT + f + 1)
                if f == 0 and not early(i):
                    act.wait_ge(s["o_ready"], e - 1)
                nc.scalar.copy(hh[:, k, f], hid[:, f % 2]).then_inc(s["hh_done"], 1)

            def step(i, k, last=False):
                for f in range(FT):
                    n = (i * 2 + k) * FT + f
                    act.wait_ge(s["gu_ready"], n + 1)
                    if not (early(i) and k == 0 and f < 2):
                        act.wait_ge(s["hid_done"], n - 1)
                    nc.scalar.activation(act_g[:, f % 2], pg[:, f % 2], ACT.Gelu).then_inc(s["gelu_done"], 1)
                    if f:
                        hidden_high(i, k, f - 1)
                    if f < 3 and not last:
                        weights_high(i + k, 1 - k, f)
                    if f == 2 and not last:
                        rows_high(i + k, 1 - k)
                hidden_high(i, k, FT - 1)

            for j in range(3):
                weights_high(0, 0, j)
            rows_high(0, 0)
            steps(act, step)

        @block.vector
        def _(dve):
            def rows_low(i, k):
                dve.wait_ge(s["xh_done"], i * 2 + k + 1)
                nc.vector.tensor_tensor(xl[:, k], pT[:], xh[:, k].bitcast(F32), ALU.subtract).then_inc(s["xl_done"], 1)
                nc.vector.tensor_copy(score[:, k], xe[:, k, :, C:ROW]).then_inc(s["score_kept"], 1)

            def weights_low(i, k, j):
                dve.wait_ge(s["wh_done"], (i * 2 + k) * 3 + j + 1)
                nc.vector.tensor_tensor(wl[:, k, j], wf[:, k, j], wh[:, k, j].bitcast(F32), ALU.subtract).then_inc(s["wl_done"], 1)

            def hidden_low(i, k, f):
                dve.wait_ge(s["hh_done"], (i * 2 + k) * FT + f + 1)
                nc.vector.tensor_tensor(hl[:, k, f], hid[:, f % 2], hh[:, k, f].bitcast(F32), ALU.subtract).then_inc(s["hl_done"], 1)

            def output(i, k):
                e = i * 2 + k
                dve.wait_ge(s["score_kept"], e + 1)
                dve.wait_ge(s["o_ready"], e + 1)
                if not early(i):
                    dve.wait_ge(added[k], 16 * NTOK * i)
                for t in range(NTOK):
                    last = nc.vector.scalar_tensor_tensor(out=eo[:, k, t, :], in0=po[:, t], scalar=score[:, k, t, bass.ds(e, 1)],
                                                          in1=m.mod[:, t // 2, GB, :], op0=ALU.mult, op1=ALU.mult)
                last.then_inc(s["eo_done"], 1)

            def step(i, k, last=False):
                for f in range(FT):
                    n = (i * 2 + k) * FT + f
                    dve.wait_ge(s["gelu_done"], n + 1)
                    if not (early(i) and k == 0 and f < 2):
                        dve.wait_ge(s["hl_done"], n - 1)
                    nc.vector.tensor_tensor(hid[:, f % 2], act_g[:, f % 2], pu[:, f % 2], ALU.mult).then_inc(s["hid_done"], 1)
                    if f == 0 and not (early(i) and k == 0):
                        output(i - 1 + k, 1 - k)
                    if f:
                        hidden_low(i, k, f - 1)
                    if f < 3 and not last:
                        weights_low(i + k, 1 - k, f)
                    if f == 2 and not last:
                        rows_low(i + k, 1 - k)
                hidden_low(i, k, FT - 1)

            for j in range(3):
                weights_low(0, 0, j)
            rows_low(0, 0)
            steps(dve, step)
            output(EX // 2 - 1, 1)

        @block.tensor
        def _(pe):
            def rows(i, k):
                n = i * 2 + k
                pe.wait_ge(gathered[k], 16 * NTOK * (i + 1))
                if not (early(i) and k == 0):
                    pe.wait_ge(s["xl_done"], n)
                for h in range(CH):
                    for t in range(NTOK):
                        last = nc.tensor.transpose(pT[:, h, t * P:(t + 1) * P], xe[:, k, t, h * P:(h + 1) * P], m.ident[:])
                last.then_inc(s["t_ready"], 1)

            def down(i, k):
                e = i * 2 + k
                pe.wait_ge(s["hl_done"], (e + 1) * FT)
                if not (early(i) and k == 0):
                    pe.wait_ge(s["eo_done"], e)
                for t in range(NTOK):
                    for f in range(FT):
                        tok, feat = slice(t * P, (t + 1) * P), slice(f * C, (f + 1) * C)
                        last = exact_matmul(nc, po[:, t], hh[:, k, f, tok], hl[:, k, f, tok], wh[:, k, 2, feat], wl[:, k, 2, feat],
                                            f == 0, f == FT - 1)
                last.then_inc(s["o_ready"], 1)

            def step(i, k, last_one=False):
                e = i * 2 + k
                pe.wait_ge(s["wl_done"], (e + 1) * 3)
                pe.wait_ge(s["xl_done"], e + 1)
                for f in range(FT):
                    n = e * FT + f
                    if not (early(i) and k == 0 and f < 2):
                        pe.wait_ge(s["hid_done"], n - 1)
                    for j, dst in enumerate((pg, pu)):
                        for h in range(CH):
                            feat = slice(h * FE + f * P, h * FE + (f + 1) * P)
                            last = exact_matmul(nc, dst[:, f % 2], wh[:, k, j, feat], wl[:, k, j, feat], xh[:, k, h, :], xl[:, k, h, :],
                                                h == 0, h == CH - 1)
                    last.then_inc(s["gu_ready"], 1)
                    if f == 0 and not (early(i) and k == 0):
                        down(i - 1 + k, 1 - k)
                    if f == 2 and not last_one:
                        rows(i + k, 1 - k)

            rows(0, 0)
            steps(pe, step)
            down(EX // 2 - 1, 1)


def program(nc, a, out):
    m = Shared()
    USED.clear()
    m.mod_dram = nc.dram_tensor("mod_dram", [2, B, NMOD, C], F32).ap()
    with ExitStack() as ctx:
        sb, ps, sem = setup(nc, ctx)
        m.x = sb("x", [P, NT, C])
        m.mod = sb("mod", [P, B, NMOD, C])
        m.ident, m.mask = sb("ident", [P, P]), sb("mask", [P, 2 * P])
        m.upto, m.after, m.ones = sb("upto", [P, P]), sb("after", [P, P]), sb("ones", [P, P])
        m.neghalf, m.st = sb("neghalf", [P, NT]), sb("st", [P, NT, 6])
        m.mean, m.rstd, m.tmp = sb("mean", [P, NT]), sb("rstd", [P, NT]), sb("tmp", [P, NT])
        m.idx = sb("idx", [P, 2 * RX], I32)
        constants(nc, m, a["x"])
        modulation(nc, m, a)
        with ExitStack() as scope:
            sb, _, _ = setup(nc, scope)
            m.qT, m.kT = sb("qT", [P, CH, B * T]), sb("kT", [P, CH, B * T])
            m.v = sb("v", [P, NT, C + 1])
            attention_projections(nc, m, a)
            attention(nc, m)
        with ExitStack() as scope:
            sb, _, _ = setup(nc, scope)
            m.seT, m.gx = sb("seT", [P, CH, NS]), sb("gx", [P, C])
            m.w1, m.w2 = sb("w1", [P, CH, HID]), sb("w2", [P, HT, C])
            slot_embeddings(nc, m, a)
            soft_mixture(nc, m)
        recycle(nc)
        with ExitStack() as scope:
            sb, _, _ = setup(nc, scope)
            m.cum_dram = nc.dram_tensor("cum_dram", [NT * HEADS, P], F32).ap()
            m.uT = sb("uT", [P, CH, B * T])
            m.dt, m.cs = sb("dt", [P, NT, HEADS]), sb("cs", [P, NT, 4, HEADS])
            m.etot = sb("etot", [STATE, NT, HEADS])
            state_inputs(nc, m, a)
            decays(nc, m, a)
            state_space(nc, m, a)
        recycle(nc)
        m.rows = nc.dram_tensor("rows_dram", [B * T, ROW], F32).ap()
        with ExitStack() as scope:
            sb, _, _ = setup(nc, scope)
            m.hT, m.sc = sb("hT", [P, CH, B * T]), sb("sc", [RX, T])
            m.wg, m.wu, m.wd = sb("ws_g", [P, CH, FE]), sb("ws_u", [P, CH, FE]), sb("ws_d", [P, FT, C])
            routing_scores(nc, m, a)
            shared_and_choice(nc, m, a, out)
        experts(nc, m, a, out)


def kernel(**inputs):
    import numpy as np
    import concourse.bacc as bacc
    from concourse.bass_utils import run_bass_kernel_spmd

    g = {k: np.asarray(v) for k, v in inputs.items()}
    cols = lambda v: np.ascontiguousarray(v.reshape(-1, P).T)
    arrays = {
        "x": g["L0_attn_x"].reshape(B * T, C),
        "c_cols": np.stack([np.ascontiguousarray(g[f"L{l}_c"].T.reshape(CH, P, B).transpose(1, 0, 2)) for l in range(2)]),
        "wmod0": g["L0_wmod"], "wmod1": g["L1_wmod"],
        "WqT": g["L0_attn_Wq"].T, "WkT": g["L0_attn_Wk"].T, "Wv": g["L0_attn_Wv"], "WoT": g["L0_attn_Wo"].T,
        "bq": cols(g["L0_attn_bq"]), "bk": cols(g["L0_attn_bk"]), "bv": cols(g["L0_attn_bv"]), "bo": g["L0_attn_bo"],
    }
    arrays |= {
        "slot_embeds": g["L0_ffn_slot_embeds"].reshape(NS, C), "gamma_slot": g["L0_ffn_gamma_slot"],
        "gamma_x": g["L0_ffn_gamma_x"], "w1": g["L0_ffn_w1"], "w2": g["L0_ffn_w2"],
    }
    arrays |= {n: g["L1_attn_" + n] for n in ("W_in", "b_in", "A_log", "D_skip", "dt_bias", "W_out", "b_out")}
    arrays["ln_cols"] = np.stack([cols(g["L1_attn_ln_gamma"]), cols(g["L1_attn_ln_beta"])], 1)
    arrays |= {
        "gate_wT": g["L1_ffn_gate_w"].T, "Ws_gT": g["L1_ffn_Ws_g"].T, "Ws_uT": g["L1_ffn_Ws_u"].T, "Ws_dT": g["L1_ffn_Ws_d"].T,
        "WgT": g["L1_ffn_Wg"].transpose(0, 2, 1), "WuT": g["L1_ffn_Wu"].transpose(0, 2, 1), "WdT": g["L1_ffn_Wd"].transpose(0, 2, 1),
    }
    nc = bacc.Bacc("TRN2", target_bir_lowering=False, num_devices=1)
    ins, feed = {}, {}
    for name, v in arrays.items():
        v = np.ascontiguousarray(v)
        feed[f"in_{name}"] = v
        ins[name] = nc.dram_tensor(f"in_{name}", v.shape, mybir.dt.from_np(v.dtype), kind="ExternalInput").ap()
    out = nc.dram_tensor("out", (B * T, C), F32, kind="ExternalOutput").ap()
    program(nc, ins, out)
    r = run_bass_kernel_spmd(nc, [feed], core_ids=[0])
    return r.results[0]["out"].reshape(B, T, C)
```

```python
import concourse.bass as bass
from concourse import mybir
from contextlib import ExitStack

F32 = mybir.dt.float32
BF16 = mybir.dt.bfloat16
I32 = mybir.dt.int32
ALU = mybir.AluOpType
FR = mybir.dt.float32r
ACT = mybir.ActivationFunctionType
AX = mybir.AxisListType.X

P = 128
B, T, C = 2, 2048, 256
CH = C // P
NTB = T // P
NT = B * NTB
GT = 4
GW = GT * P
NG = NTB // GT
NMOD = 6
SA, CA, GA, SB, CB, GB = range(NMOD)
WINDOW = 16
NEG = -1e30
LN_EPS = 1e-5
CREDIT = 1
USED = []


def setup(nc, ctx):
    def sb(name, shape, dt=F32):
        return ctx.enter_context(nc.sbuf_tensor(name, shape, dt))

    def ps(name, shape, dt=F32):
        return ctx.enter_context(nc.psum_tensor(name, shape, dt))

    def sem(name):
        USED.append(nc.alloc_semaphore(name))
        return USED[-1]
    return sb, ps, sem


def recycle(nc):
    nc.clear_and_free_semaphores(list(USED))
    USED.clear()
    nc.all_engine_barrier()


def over(row, n):
    return row.unsqueeze(1).to_broadcast([row.shape[0], n, row.shape[-1]])


def exact_matmul(nc, out, ah, al, bh, bl, start, stop):
    nc.tensor.matmul(out, ah, bh, start=start, stop=False)
    nc.tensor.matmul(out, al, bh, start=False, stop=False)
    return nc.tensor.matmul(out, ah, bl, start=False, stop=stop)


def fresh(engine, i):
    with engine.register() as r:
        engine.reg_add(r, i, 0)
        return engine.snap(r, min_val=0, max_val=i.max_val)


class Shared:
    pass


def beginnings(nc, m, w):
    with ExitStack() as ctx:
        sb, ps, sem = setup(nc, ctx)
        b = Shared()
        b.cc, b.wm = sb("c_cc", [P, 2, CH, B]), sb("c_wm", [P, 2, CH, NMOD * C])
        b.se, b.gamma = sb("s_se", [P, E, C]), sb("s_gamma", [P, C])
        b.wv, b.wo, b.vb, b.bo = sb("c_wv", [P, CH, C]), sb("c_wo", [P, CH, C]), sb("c_vb", [P, CH]), sb("c_bo", [P, C])
        b.x_in = [sem(f"c_x{i}") for i in range(NT // GT)]
        b.c_in, b.slots_in, b.fold_in, b.qk_in = [sem("c_" + n) for n in ("c_in", "slots_in", "fold_in", "qk_in")]
        b.wm_in = [sem(f"c_wm_in{l}") for l in range(2)]
        b.ones_set, b.x_stats, b.spread = sem("c_ones"), sem("c_x_stats"), sem("c_spread")
        b.shaped, b.half_set, b.silu = sem("c_shaped"), sem("c_half"), sem("c_silu")
        halves = lambda a: a.rearrange("(h p) n -> p h n", p=P)
        with nc.Block() as block:
            @block.sync
            def _(sp):
                sp.dma_start(b.cc[:], w["c_cols"].rearrange("l p h b -> p l h b")).then_inc(b.c_in, 16)
                sp.dma_start(b.wm[:, 0], halves(w["wmod0"])).then_inc(b.wm_in[0], 16)
                sp.dma_start(b.se[:], w["slot_embeds"].rearrange("(t p) c -> p t c", p=P)).then_inc(b.slots_in, 16)
                sp.dma_start(b.gamma[:], w["gamma_slot"].partition_broadcast(P)).then_inc(b.slots_in, 16)
                sp.dma_start(m.gx[:], w["gamma_x"].partition_broadcast(P)).then_inc(b.slots_in, 16)
                sp.dma_start(b.wm[:, 1], halves(w["wmod1"])).then_inc(b.wm_in[1], 16)

            @block.scalar
            def _(act):
                xt = w["x"].rearrange("(t p) c -> p t c", p=P)
                for i in range(NT // GT):
                    act.dma_start(m.x[:, i * GT:(i + 1) * GT, :], xt[:, i * GT:(i + 1) * GT, :]).then_inc(b.x_in[i], 16)
                act.dma_start(b.wv[:], halves(w["Wv"])).then_inc(b.fold_in, 16)
                act.dma_start(b.wo[:], halves(w["WoT"])).then_inc(b.fold_in, 16)
                act.dma_start(b.vb[:], w["bv"]).then_inc(b.fold_in, 16)
                act.dma_start(b.bo[:], w["bo"].partition_broadcast(P)).then_inc(b.fold_in, 16)
                act.dma_start(m.wq[:], halves(w["WqT"])).then_inc(b.qk_in, 16)
                act.dma_start(m.wk[:], halves(w["WkT"])).then_inc(b.qk_in, 16)
                act.dma_start(m.qb[:], w["bq"]).then_inc(b.qk_in, 16)
                act.dma_start(m.kb[:], w["bk"]).then_inc(b.qk_in, 16)

            constants(nc, m, b, block)
            row_stats(nc, m, b, block, range(0, 5))
            modulation(nc, m, b, block, ctx, 0)
            slot_norms(nc, m, b, block, ctx)
            row_stats(nc, m, b, block, range(5, NT // GT))
            first_stats(nc, m, b, block, ctx)
            modulation(nc, m, b, block, ctx, 1)
            output_weights(nc, m, b, block, ctx)
            slot_embeddings(nc, m, b, block, ctx)

            @block.sync
            def _(sp):
                sp.wait_ge(b.qk_in, 64)


def modulation(nc, m, b, block, ctx, layer):
    sb, ps, sem = setup(nc, ctx)
    L = f"m{layer}_"
    rows = sb(L + "rows", [B, NMOD, C])
    sgn, mag = sb(L + "sgn", [B, 2, C]), sb(L + "mag", [B, 2, C])
    if layer == 0:
        b.cs, b.pm, b.rows_cp = sb(L + "cs", [P, 2, CH, B]), ps(L + "pm", [B, NMOD * C]), sem(L + "rows_cp")
    names = "rows_ps neg mag sgn sgn2 scaled gated stored".split()
    s = {n: sem(L + n) for n in names}
    gates, scales = rows[:, GA:GB + 1:GB - GA, :], rows[:, CA:CB + 1:CB - CA, :]

    @block.sync
    def _(sp):
        sp.wait_ge(s["gated"], 1)
        sp.wait_ge(s["scaled"], 1)
        sp.dma_start(m.mod_dram[layer], rows[:]).then_inc(s["stored"], 16)
        sp.wait_ge(s["stored"], 16)
        if layer == 0:
            sp.dma_start(m.mod[:].rearrange("p b m c -> p (b m c)"),
                         m.mod_dram[0].rearrange("b m c -> (b m c)").partition_broadcast(P)).then_inc(b.spread, 16)

    if layer == 0:
        @block.scalar
        def _(act):
            act.wait_ge(b.c_in, 16)
            nc.scalar.activation(b.cs[:], b.cc[:], ACT.Silu).then_inc(b.silu, 1)

    @block.tensor
    def _(pe):
        pe.wait_ge(b.silu, 1)
        pe.wait_ge(b.wm_in[layer], 16)
        if layer:
            pe.wait_ge(b.rows_cp, layer)
        for n in range(NMOD * C // 512):
            for h in range(CH):
                last = nc.tensor.matmul(b.pm[:, n * 512:(n + 1) * 512], b.cs[:, layer, h, :],
                                        b.wm[:, layer, h, n * 512:(n + 1) * 512], start=h == 0, stop=h == CH - 1)
        last.then_inc(s["rows_ps"], 1)

    @block.vector
    def _(dve):
        dve.wait_ge(s["rows_ps"], 1)
        nc.vector.tensor_copy(rows[:].rearrange("b m c -> b (m c)"), b.pm[:]).then_inc(b.rows_cp, 1)
        dve.wait_ge(b.rows_cp, layer + 1)
        nc.vector.tensor_scalar(mag[:], gates, -1.0, None, ALU.mult).then_inc(s["neg"], 1)
        nc.vector.tensor_scalar(sgn[:], gates, 0.0, 2.0, ALU.is_ge, ALU.mult).then_inc(s["sgn"], 1)
        nc.vector.tensor_scalar_add(scales, scales, 1.0).then_inc(s["scaled"], 1)
        dve.wait_ge(s["sgn"], 1)
        nc.vector.tensor_scalar_add(sgn[:], sgn[:], -1.0).then_inc(s["sgn2"], 1)
        dve.wait_ge(s["neg"], 1)
        nc.vector.scalar_tensor_tensor(out=mag[:], in0=mag[:], scalar=0.25, in1=gates,
                                       op0=ALU.max, op1=ALU.max).then_inc(s["mag"], 1)
        dve.wait_ge(s["mag"], 1)
        dve.wait_ge(s["sgn2"], 1)
        nc.vector.tensor_tensor(gates, mag[:], sgn[:], ALU.mult).then_inc(s["gated"], 1)


def constants(nc, m, b, block):
    @block.gpsimd
    def _(pool):
        nc.gpsimd.memset(m.ident[:], 0.0).then_inc(b.ones_set, 1)
        nc.gpsimd.memset(m.mask[:], 0.0).then_inc(b.ones_set, 1)
        nc.gpsimd.memset(m.upto[:], 1.0).then_inc(b.ones_set, 1)
        nc.gpsimd.memset(m.after[:], 1.0).then_inc(b.ones_set, 1)
        nc.gpsimd.memset(m.ones[:], 1.0).then_inc(b.ones_set, 1)
        nc.gpsimd.memset(m.neghalf[:], -0.5).then_inc(b.half_set, 1)
        pool.wait_ge(b.ones_set, 5)
        nc.gpsimd.affine_select(out=m.ident[:], in_=m.ident[:], compare_op=ALU.not_equal, fill=1.0,
                                base=0, pattern=[[-1, P]], channel_multiplier=1).then_inc(b.shaped, 1)
        nc.gpsimd.affine_select(out=m.mask[:], in_=m.mask[:], compare_op=ALU.is_ge, fill=NEG,
                                base=WINDOW - P, pattern=[[1, 2 * P]], channel_multiplier=-1)
        nc.gpsimd.affine_select(out=m.upto[:], in_=m.upto[:], compare_op=ALU.is_ge, fill=0.0,
                                base=0, pattern=[[1, P]], channel_multiplier=-1)
        nc.gpsimd.affine_select(out=m.after[:], in_=m.after[:], compare_op=ALU.is_gt, fill=0.0,
                                base=0, pattern=[[-1, P]], channel_multiplier=1)


def row_stats(nc, m, b, block, groups):
    @block.vector
    def _(dve):
        for i in groups:
            dve.wait_ge(b.x_in[i], 16)
            for t in range(i * GT, (i + 1) * GT):
                nc.vector.bn_stats(m.st[:, t, :], m.x[:, t, :]).then_inc(b.x_stats, 1)


def first_stats(nc, m, b, block, ctx):
    _, _, sem = setup(nc, ctx)
    vector, gpsimd = finish_stats(nc, [sem(f"c_stat{i}") for i in range(5)], m, 0, NT)

    @block.vector
    def _(dve):
        dve.wait_ge(b.x_stats, NT)
        vector()

    @block.gpsimd
    def _(pool):
        pool.wait_ge(b.half_set, 1)
        gpsimd()


def output_weights(nc, m, b, block, ctx):
    sb, ps, sem = setup(nc, ctx)
    vbb = sb("o_vbb", [P, CH, P])
    pv = ps("o_pv", [P, CH + 1, C])
    vb_spread, fold_ps, fold1 = sem("o_vbs"), sem("o_fold_ps"), sem("o_fold1")

    @block.tensor
    def _(pe):
        pe.wait_ge(b.fold_in, 64)
        pe.wait_ge(vb_spread, 1)
        for o in range(CH):
            for k in range(CH):
                nc.tensor.matmul(pv[:, o, :], b.wv[:, k, o * P:(o + 1) * P], b.wo[:, k, :], start=k == 0, stop=k == CH - 1)
        for k in range(CH):
            last = nc.tensor.matmul(pv[:, CH, :], vbb[:, k, :], b.wo[:, k, :], start=k == 0, stop=k == CH - 1)
        last.then_inc(fold_ps, 1)

    @block.vector
    def _(dve):
        dve.wait_ge(b.fold_in, 64)
        nc.vector.tensor_copy(vbb[:], b.vb[:].unsqueeze(2).to_broadcast([P, CH, P])).then_inc(vb_spread, 1)
        dve.wait_ge(b.spread, 16)
        dve.wait_ge(fold_ps, 1)
        for k in range(B):
            nc.vector.tensor_tensor(m.wvo[:, k], pv[:, 0:CH, :], over(m.mod[:, k, GA, :], CH), ALU.mult)
            nc.vector.tensor_tensor(m.vrow[:, k], pv[:, CH, :], b.bo[:], ALU.add).then_inc(fold1, 1)
            dve.wait_ge(fold1, k + 1)
            nc.vector.tensor_tensor(m.vrow[:, k], m.vrow[:, k], m.mod[:, k, GA, :], ALU.mult)


def finish_stats(nc, sems, m, n0, n1, eps=LN_EPS):
    a, b, c, d, e = sems
    st = m.st[:, n0:n1, :]
    dve, pool = nc.vector, nc.gpsimd
    mean, rstd, tmp = m.mean[:, n0:n1], m.rstd[:, n0:n1], m.tmp[:, n0:n1]

    def vector():
        dve.tensor_tensor(mean, st[:, :, 1], st[:, :, 4], ALU.add).then_inc(a, 1)
        dve.tensor_tensor(tmp, st[:, :, 1], st[:, :, 4], ALU.subtract).then_inc(a, 1)
        dve.tensor_tensor(rstd, st[:, :, 2], st[:, :, 5], ALU.add).then_inc(a, 1)
        dve.wait_ge(a, 3)
        dve.tensor_scalar(mean, mean, 0.5, None, ALU.mult).then_inc(b, 1)
        dve.tensor_tensor(tmp, tmp, tmp, ALU.mult).then_inc(b, 1)
        dve.tensor_scalar(rstd, rstd, 1.0 / C, eps, ALU.mult, ALU.add).then_inc(b, 1)
        dve.wait_ge(b, 3)
        dve.scalar_tensor_tensor(out=rstd, in0=tmp, scalar=0.25, in1=rstd, op0=ALU.mult, op1=ALU.add).then_inc(c, 1)

    def gpsimd():
        pool.wait_ge(c, 1)
        pool.tensor_tensor(rstd, rstd, m.neghalf[:, n0:n1], ALU.pow).then_inc(e, 1)
    return vector, gpsimd


def attention_projections(nc, m):
    with ExitStack() as ctx:
        sb, ps, sem = setup(nc, ctx)
        h = sb("a_h", [P, B, GT, C])
        hT = sb("a_hT", [P, B, CH, GW])
        pT = ps("a_pT", [P, CH, GW])
        pq = ps("a_pq", [P, CH, GW])
        pk = ps("a_pk", [P, CH, GW])
        pv = ps("a_pv", [P, GT, C])
        cols = sb("a_cols", [P, B, 2, CH])
        pcols = pq[:].rearrange("p h (n q) -> p (h n) q", q=P)
        normed, cols_ready, cols_copied, t_ready, t_copied, q_ready, q_copied, k_ready, k_copied, v_ready, v_copied = [
            sem("a_" + n) for n in ("normed", "cols_ready", "cols_copied", "t_ready", "t_copied", "q_ready", "q_copied",
                                    "k_ready", "k_copied", "v_ready", "v_copied")]
        block = ctx.enter_context(nc.Block())

        @block.sync
        def _(sp):
            for owed in (q_copied, k_copied, v_copied):
                sp.sem_inc(owed, CREDIT)

        @block.vector
        def _(dve):
            nc.vector.memset(m.v[:, :, C:C + 1], 1.0)

            def normalise(i, b):
                for k in range(GT):
                    t = bass.ds(b * NTB + i * GT + k, 1)
                    nc.vector.tensor_scalar(h[:, b, k, :], m.x[:, t, :].squeeze(1), m.mean[:, t], m.rstd[:, t],
                                            ALU.subtract, ALU.mult).then_inc(normed, 1)

            def group(i, b, last):
                n = i * B + b + 1
                if not last:
                    if not (isinstance(i, int) and i == 0 and b == 0):
                        dve.wait_ge(t_ready, n - 1)
                    normalise(i + b, 1 - b)
                dve.wait_ge(k_ready, n)
                for o in range(CH):
                    ins = nc.vector.tensor_scalar(m.kT[:, o, bass.ds(b * T + i * GW, GW)], pk[:, o, :], m.kb[:, o:o + 1],
                                                  None, ALU.add)
                ins.then_inc(k_copied, 1)
                dve.wait_ge(v_ready, n)
                nc.vector.tensor_tensor(m.v[:, bass.ds(b * NTB + i * GT, GT), 0:C], pv[:], over(m.vrow[:, b], GT),
                                        ALU.add).then_inc(v_copied, 1)

            normalise(0, 0)
            group(0, 0, False)
            group(0, 1, False)
            with dve.Fori(1, NG - 1) as i:
                group(i, 0, False)
                group(i, 1, False)
            group(NG - 1, 0, False)
            group(NG - 1, 1, True)

        @block.scalar
        def _(act):
            act.wait_ge(cols_ready, 1)
            nc.scalar.copy(cols[:].rearrange("p b m h -> p (b m h)"), pcols[:, :, 0]).then_inc(cols_copied, 1)
            act.wait_ge(cols_copied, 1)

            def copy_t(i, b):
                act.wait_ge(t_ready, i * B + b + 1)
                for o in range(CH):
                    last = nc.scalar.activation(hT[:, b, o], pT[:, o], ACT.Identity, scale=cols[:, b, CA, o:o + 1],
                                                bias=cols[:, b, SA, o:o + 1])
                last.then_inc(t_copied, 1)

            copy_t(0, 0)

            def group(i, b, last=False):
                act.wait_ge(q_ready, i * B + b + 1)
                for o in range(CH):
                    ins = nc.scalar.activation(m.qT[:, o, bass.ds(b * T + i * GW, GW)], pq[:, o, :], ACT.Identity,
                                               bias=m.qb[:, o:o + 1])
                ins.then_inc(q_copied, 1)
                if not last:
                    copy_t(i + b, 1 - b)

            with act.Fori(0, NG - 1) as i:
                group(i, 0)
                group(i, 1)
            group(NG - 1, 0)
            group(NG - 1, 1, True)

        @block.tensor
        def _(pe):
            def transposes(i, b):
                n = i * B + b + 1
                pe.wait_ge(normed, n * GT)
                pe.wait_ge(t_copied, n - 1)
                for o in range(CH):
                    for k in range(GT):
                        last = nc.tensor.transpose(pT[:, o, k * P:(k + 1) * P], h[:, b, k, o * P:(o + 1) * P], m.ident[:])
                last.then_inc(t_ready, 1)

            for b in range(B):
                for c in (SA, CA):
                    for o in range(CH):
                        last = nc.tensor.transpose(pcols[:, (b * 2 + c) * CH + o, :], m.mod[:, b, c, o * P:(o + 1) * P], m.ident[:])
            last.then_inc(cols_ready, 1)
            pe.wait_ge(cols_copied, 1)
            transposes(0, 0)

            def group(i, b, last_one=False):
                n = i * B + b + 1
                pe.wait_ge(t_copied, n)
                for dst, wt, free, done in ((pq, m.wq, q_copied, q_ready), (pk, m.wk, k_copied, k_ready)):
                    pe.wait_ge(free, n - 1 + CREDIT)
                    for o in range(CH):
                        for k in range(CH):
                            last = nc.tensor.matmul(dst[:, o, :], wt[:, k, o * P:(o + 1) * P], hT[:, b, k, :],
                                                    start=k == 0, stop=k == CH - 1)
                    last.then_inc(done, 1)
                if not last_one:
                    transposes(i + b, 1 - b)
                pe.wait_ge(v_copied, n - 1 + CREDIT)
                for j in range(GT):
                    for k in range(CH):
                        last = nc.tensor.matmul(pv[:, j, :], hT[:, b, k, j * P:(j + 1) * P], m.wvo[:, b, k, :],
                                                start=k == 0, stop=k == CH - 1)
                last.then_inc(v_ready, 1)

            with pe.Fori(0, NG - 1) as i:
                group(i, 0)
                group(i, 1)
            group(NG - 1, 0)
            group(NG - 1, 1, True)


def attention(nc, m, w):
    scale = float(C) ** -0.5
    with ExitStack() as ctx:
        sb, ps, sem = setup(nc, ctx)
        qs = sb("b_q", [P, 2, CH, P])
        nmax = sb("b_nmax", [P, 2])
        pr = sb("b_p", [P, 2, T])
        pT = sb("b_pT", [P, 2, GW])
        rden = sb("b_rden", [P, 2])
        pS = ps("b_pS", [P, T])
        pTp = ps("b_pTp", [P, 2, GW])
        pO = ps("b_pO", [P, 2, 512])
        q_staged, s_ready, masked, max_done, nmax_done, exp_done, t_ready, t_copied, pv_done, rden_done, x_done = [
            sem("b_" + n) for n in ("q_staged", "s_ready", "masked", "max_done", "nmax_done", "exp_done", "t_ready",
                                    "t_copied", "pv_done", "rden_done", "x_done")]
        block = ctx.enter_context(nc.Block())
        w_in = sem("b_w_in")

        @block.sync
        def _(sp):
            for owed in (pv_done, s_ready, x_done, t_copied, exp_done):
                sp.sem_inc(owed, CREDIT)
            sp.dma_start(m.w1[:], w["w1"].rearrange("(h p) n -> p h n", p=P)).then_inc(w_in, 16)
            sp.dma_start(m.w2[:], w["w2"].rearrange("(h p) n -> p h n", p=P)).then_inc(w_in, 16)
            sp.wait_ge(w_in, 32)

        first = [max(it - 1, 0) for it in range(NTB)]
        nkeys = [NTB - f for f in first]
        ngroups = [-(-n // GT) for n in nkeys]
        before = [sum(ngroups[:it]) for it in range(NTB + 1)]

        def width(it, g):
            return min(GT, nkeys[it] - g * GT) * P

        @block.gpsimd
        def _(pool):
            with pool.Fori(0, B) as b:
                for it in range(NTB):
                    if it >= 2:
                        pool.wait_ge(s_ready, b * NTB + it - 1 + CREDIT)
                    else:
                        pool.wait_ge(s_ready, b * NTB + CREDIT)
                    nc.gpsimd.tensor_copy(qs[:, it % 2], m.qT[:, :, bass.ds(b * T + it * P, P)]).then_inc(q_staged, 1)

        @block.tensor
        def _(pe):
            def scores(b, it):
                pe.wait_ge(q_staged, b * NTB + it + 1)
                pe.wait_ge(exp_done, b * NTB + it + CREDIT)
                for g in range(ngroups[it]):
                    w = width(it, g)
                    for k in range(CH):
                        last = nc.tensor.matmul(pS[:, g * GW:g * GW + w], qs[:, it % 2, k, :],
                                                m.kT[:, k, bass.ds(b * T + first[it] * P + g * GW, w)],
                                                start=k == 0, stop=k == CH - 1)
                last.then_inc(s_ready, 1)

            def transposes(b, it, g, n):
                pe.wait_ge(t_copied, b * before[-1] + max(n - 1, 0) + CREDIT)
                for j in range(width(it, g) // P):
                    last = nc.tensor.transpose(pTp[:, n % 2, j * P:(j + 1) * P],
                                               pr[:, it % 2, g * GW + j * P:g * GW + (j + 1) * P], m.ident[:])
                last.then_inc(t_ready, 1)

            def values(b, it, g, n):
                pe.wait_ge(t_copied, b * before[-1] + n + 1 + CREDIT)
                for j in range(width(it, g) // P):
                    last = nc.tensor.matmul(pO[:, it % 2, 0:C + 1], pT[:, n % 2, j * P:(j + 1) * P],
                                            m.v[:, bass.ds(b * NTB + first[it] + g * GT + j, 1), :].squeeze(1),
                                            start=g == 0 and j == 0, stop=g * GT + j == nkeys[it] - 1)
                last.then_inc(pv_done, 1)

            with pe.Fori(0, B) as b:
                scores(b, 0)
                for it in range(NTB):
                    b = fresh(pe, b)
                    if it + 1 < NTB:
                        scores(b, it + 1)
                    pe.wait_ge(x_done, b * NTB + max(it - 1, 0) + CREDIT)
                    pe.wait_ge(exp_done, b * NTB + it + 1 + CREDIT)
                    base = before[it]
                    transposes(b, it, 0, base)
                    for g in range(ngroups[it]):
                        if g + 1 < ngroups[it]:
                            transposes(b, it, g + 1, base + g + 1)
                        values(b, it, g, base + g)

        @block.scalar
        def _(act):
            def exps(b, it):
                act.wait_ge(nmax_done, b * NTB + it + 1)
                if it >= 2:
                    act.wait_ge(pv_done, b * before[-1] + before[it - 1] + CREDIT)
                else:
                    act.wait_ge(pv_done, b * before[-1] + CREDIT)
                nc.scalar.activation(pr[:, it % 2, 0:nkeys[it] * P], pS[:, 0:nkeys[it] * P], ACT.Exp,
                                     bias=nmax[:, it % 2:it % 2 + 1], scale=scale).then_inc(exp_done, 1)

            def copies(b, it):
                for g in range(ngroups[it]):
                    n = before[it] + g
                    act.wait_ge(t_ready, b * before[-1] + n + 1)
                    act.wait_ge(pv_done, b * before[-1] + max(n - 1, 0) + CREDIT)
                    w = width(it, g)
                    nc.scalar.copy(pT[:, n % 2, 0:w], pTp[:, n % 2, 0:w]).then_inc(t_copied, 1)

            with act.Fori(0, B) as b:
                exps(b, 0)
                for it in range(NTB):
                    b = fresh(act, b)
                    copies(b, it)
                    if it + 1 < NTB:
                        exps(b, it + 1)

        @block.vector
        def _(dve):
            def maxima(b, it):
                dve.wait_ge(s_ready, b * NTB + it + 1 + CREDIT)
                n, lo = min(it + 1, 2), max(1 - it, 0) * P
                nc.vector.tensor_tensor(pS[:, 0:n * P], pS[:, 0:n * P], m.mask[:, lo:2 * P], ALU.add).then_inc(masked, 1)
                dve.wait_ge(masked, b * NTB + it + 1)
                nc.vector.reduce_max(nmax[:, it % 2:it % 2 + 1], pS[:, 0:nkeys[it] * P], axis=AX).then_inc(max_done, 1)
                dve.wait_ge(max_done, b * NTB + it + 1)
                nc.vector.tensor_scalar(nmax[:, it % 2:it % 2 + 1], nmax[:, it % 2:it % 2 + 1], -scale, None,
                                        ALU.mult).then_inc(nmax_done, 1)

            def update(b, it):
                r = rden[:, it % 2:it % 2 + 1]
                xt = m.x[:, bass.ds(b * NTB + it, 1), :].squeeze(1)
                dve.wait_ge(pv_done, b * before[-1] + before[it + 1] + CREDIT)
                nc.vector.reciprocal(r, pO[:, it % 2, C:C + 1]).then_inc(rden_done, 1)
                dve.wait_ge(rden_done, b * NTB + it + 1)
                nc.vector.scalar_tensor_tensor(out=xt, in0=pO[:, it % 2, 0:C], scalar=r, in1=xt,
                                               op0=ALU.mult, op1=ALU.add).then_inc(x_done, 1)
                dve.wait_ge(x_done, b * NTB + it + 1 + CREDIT)
                nc.vector.bn_stats(m.st[:, bass.ds(b * NTB + it, 1), :].squeeze(1), xt)

            with dve.Fori(0, B) as b:
                maxima(b, 0)
                for it in range(NTB):
                    b = fresh(dve, b)
                    if it + 1 < NTB:
                        maxima(b, it + 1)
                    update(b, it)


E, SL = 8, 128
NS = E * SL
HID = 4 * C
HT = HID // P
SH = NS // 512


def row_norms(nc, m, ss, clamped, powed, n, value, dve_side):
    if dve_side:
        nc.vector.tensor_scalar(ss, ss, 1e-24, None, ALU.max).then_inc(clamped, 1)
    else:
        nc.gpsimd.wait_ge(clamped, value)
        nc.gpsimd.tensor_tensor(ss, ss, m.neghalf[:, 0:n], ALU.pow).then_inc(powed, 1)


def slot_norms(nc, m, b, block, ctx):
    sb, ps, sem = setup(nc, ctx)
    sq = sb("s_sq", [P, C])
    b.ss = ss = sb("s_ss", [P, E])
    squared, clamped = sem("s_squared"), sem("s_clamped")
    b.powed, b.gammaed = sem("s_powed"), sem("s_gammaed")

    @block.scalar
    def _(act):
        act.wait_ge(b.slots_in, 48)
        for t in range(E):
            if t:
                act.wait_ge(squared, t)
            nc.scalar.activation(sq[:], b.se[:, t], ACT.Square, accum_out=ss[:, t:t + 1]).then_inc(squared, 1)

    @block.gpsimd
    def _(pool):
        pool.wait_ge(b.half_set, 1)
        row_norms(nc, m, ss[:], clamped, b.powed, E, 1, False)

    @block.vector
    def _(dve):
        dve.wait_ge(squared, E)
        row_norms(nc, m, ss[:], clamped, b.powed, E, 1, True)
        nc.vector.tensor_scalar(b.gamma[:], b.gamma[:], float(C) ** 0.5, None, ALU.mult).then_inc(b.gammaed, 1)
        nc.vector.tensor_scalar(m.gx[:], m.gx[:], float(C) ** 0.5, None, ALU.mult)


def slot_embeddings(nc, m, b, block, ctx):
    sb, ps, sem = setup(nc, ctx)
    pT = ps("s_pT", [P, CH, GW])
    scaled, t_ready, t_copied = sem("s_scaled"), sem("s_t_ready"), sem("s_t_copied")

    @block.vector
    def _(dve):
        dve.wait_ge(b.powed, 1)
        dve.wait_ge(b.gammaed, 1)
        for t in range(E):
            nc.vector.scalar_tensor_tensor(out=b.se[:, t], in0=b.se[:, t], scalar=b.ss[:, t:t + 1], in1=b.gamma[:],
                                           op0=ALU.mult, op1=ALU.mult).then_inc(scaled, 1)
        for a in range(E // GT):
            dve.wait_ge(t_ready, a + 1)
            nc.vector.tensor_copy(m.seT[:, :, a * GW:(a + 1) * GW], pT[:]).then_inc(t_copied, 1)

    @block.tensor
    def _(pe):
        pe.wait_ge(b.shaped, 1)
        for a in range(E // GT):
            pe.wait_ge(scaled, (a + 1) * GT)
            if a:
                pe.wait_ge(t_copied, a)
            for t in range(GT):
                for h in range(CH):
                    last = nc.tensor.transpose(pT[:, h, t * P:(t + 1) * P], b.se[:, a * GT + t, h * P:(h + 1) * P], m.ident[:])
            last.then_inc(t_ready, 1)


def soft_mixture(nc, m):
    with ExitStack() as ctx:
        sb, ps, sem = setup(nc, ctx)
        xn = sb("d_xn", [P, NTB, C])
        xn_at = nc.sbuf_base - NTB * C * 4
        xnT = sb("d_xnT", [P, CH, T])
        raw = sb("d_raw", [P, E, T])
        work = sb("d_work", [P, 2, T])
        work_at = nc.sbuf_base - 2 * T * 4
        slotsT = sb("d_slotsT", [P, CH, NS])
        slotsT_at = nc.sbuf_base - CH * NS * 4
        proc = sb("d_proc", [P, E, C])
        sl = sb("d_sl", [P, 2, C])
        ss = sb("d_ss", [P, NTB])
        sq = sl[:, 0]
        nmax, esum = sb("d_nmax", [P, 2]), sb("d_esum", [P, 2])
        rsum = sb("d_rsum", [P, 2])
        cmax, csum, crs = sb("d_cmax", [P, 2]), sb("d_csum", [P, 2]), sb("d_crs", [P, 2])
        eT = sb("d_eT", [P, 2, GW])
        pL = ps("d_pL", [P, T])
        pT = ps("d_pT", [P, 2, GW])
        pO = ps("d_pO", [P, 2, 512])
        hg = work[:].rearrange("p s (k c) -> p s k c", c=C)[:, :, 0:GT, :]
        hid = work[:].rearrange("p s n -> p (s n)").rearrange("p (t n) -> p t n", n=512)
        pc = work[:, 0, :].rearrange("p (s n) -> p s n", s=2)
        pch = nc.alloc_sbuf_tensor_at("d_pch", [P, 2, NS], FR, offset=work_at + T * 4)
        pcl = nc.alloc_sbuf_tensor_at("d_pcl", [P, 2, NS], FR, offset=xn_at)
        proch = nc.alloc_sbuf_tensor_at("d_proch", [P, E * C], FR, offset=xn_at + 2 * NS * 4)[:]
        procl = nc.alloc_sbuf_tensor_at("d_procl", [P, E * C], FR, offset=slotsT_at)[:]
        names = ("own stat0 stat1 stat2 stat3 stat4 normed scaled shifted squared clamped powed xn_done xT_ready xT_copied "
                 "l_ready max_done nmax_done exp_done raw_done t_ready t_copied_a t_copied_d sl_ready rsum_done sl_scaled "
                 "h_ready h_done y_ready y_done r_ready cmax_done cnmax_done cexp_done pt_ready pt_copied o_ready "
                 "crs_done x_done spread pch_done proch_done procl_done").split()
        s = {n: sem("d_" + n) for n in names}
        block = ctx.enter_context(nc.Block())

        @block.sync
        def _(sp):
            for owed in [s[n] for n in "x_done cexp_done sl_ready crs_done pt_ready pt_copied sl_scaled o_ready".split()]:
                sp.sem_inc(owed, CREDIT)
            sp.wait_ge(s["y_done"], B * E)
            sp.dma_start(m.mod[:].rearrange("p b m c -> p (b m c)"),
                         m.mod_dram[1].rearrange("b m c -> (b m c)").partition_broadcast(P)).then_inc(s["spread"], 16)
            sp.wait_ge(s["spread"], 16)

        st_vector, _ = finish_stats(nc, [s[f"stat{i}"] for i in range(5)], m, 0, NT)
        own = m.mod[:, 0, SA:CA + 1, :]
        seq = []
        for et in range(E):
            seq += [("exp", et, g) for g in range(NG)] + ([("slots", et - 1, 0)] if et else [])
        seq.append(("slots", E - 1, 0))
        at = {k: n for n, k in enumerate(seq)}
        owner = ["a" if kind == "exp" and g < 2 else "d" for kind, et, g in seq]
        nth = [owner[:n + 1].count(o) for n, o in enumerate(owner)]

        def await_copy(engine, b, n):
            o = owner[n]
            engine.wait_ge(s["t_copied_" + o], b * owner.count(o) + nth[n])

        @block.gpsimd
        def _(pool):
            pool.wait_ge(s["stat2"], 1)
            with pool.Fori(0, B) as b:
                rstd = m.rstd[:, bass.ds(b * NTB, NTB)]
                nc.gpsimd.tensor_tensor(rstd, rstd, m.neghalf[:, 0:NTB], ALU.pow).then_inc(s["stat4"], 1)
                nc.gpsimd.tensor_copy(own, m.mod[:, bass.ds(b, 1), SB:CB + 1, :].squeeze(1)).then_inc(s["own"], 1)
                pool.wait_ge(s["own"], b + 1)
                for g in range(NG):
                    n = b * NG + g + 1
                    hb = hg[:, g % 2]
                    pool.wait_ge(s["scaled"], n)
                    nc.gpsimd.tensor_tensor(hb, hb, over(own[:, 0], GT), ALU.add).then_inc(s["shifted"], 1)
                    row_norms(nc, m, ss[:, g * GT:(g + 1) * GT], s["clamped"], s["powed"], GT, n, False)

        @block.vector
        def _(dve):
            st_vector()

            def normalise(b, g):
                for k in range(GT):
                    t = bass.ds(b * NTB + g * GT + k, 1)
                    nc.vector.tensor_scalar(hg[:, g % 2, k, :], m.x[:, t, :].squeeze(1), m.mean[:, t], m.rstd[:, t],
                                            ALU.subtract, ALU.mult).then_inc(s["normed"], 1)
                dve.wait_ge(s["own"], b + 1)
                dve.wait_ge(s["normed"], (b * NG + g + 1) * GT)
                nc.vector.tensor_tensor(hg[:, g % 2], hg[:, g % 2], over(own[:, 1], GT), ALU.mult).then_inc(s["scaled"], 1)

            def rows(b, g):
                n = b * NG + g + 1
                dve.wait_ge(s["squared"], n * GT)
                row_norms(nc, m, ss[:, g * GT:(g + 1) * GT], s["clamped"], s["powed"], GT, n, True)
                dve.wait_ge(s["powed"], n)
                for k in range(GT):
                    t = g * GT + k
                    nc.vector.scalar_tensor_tensor(out=xn[:, t, :], in0=hg[:, g % 2, k, :], scalar=ss[:, t:t + 1],
                                                   in1=m.gx[:], op0=ALU.mult, op1=ALU.mult).then_inc(s["xn_done"], 1)

            def maxima(b, et):
                n = b * E + et + 1
                dve.wait_ge(s["l_ready"], n)
                nc.vector.reduce_max(nmax[:, et % 2:et % 2 + 1], pL[:], axis=AX).then_inc(s["max_done"], 1)
                dve.wait_ge(s["max_done"], n)
                nc.vector.tensor_scalar(nmax[:, et % 2:et % 2 + 1], nmax[:, et % 2:et % 2 + 1], -1.0, None,
                                        ALU.mult).then_inc(s["nmax_done"], 1)

            def copy_t(b, key):
                n = at[key]
                dve.wait_ge(s["t_ready"], b * len(seq) + n + 1)
                kind, et, g = key
                if kind == "exp":
                    nc.vector.tensor_copy(eT[:, g % 2], pT[:, n % 2]).then_inc(s["t_copied_d"], 1)
                else:
                    nc.vector.tensor_copy(slotsT[:, :, et * P:(et + 1) * P],
                                          pT[:, n % 2, 0:C].rearrange("p (h n) -> p h n", h=CH)).then_inc(s["t_copied_d"], 1)

            def scale_slots(b, et):
                n = b * E + et + 1
                r = rsum[:, et % 2:et % 2 + 1]
                dve.wait_ge(s["exp_done"], n)
                nc.vector.reciprocal(r, esum[:, et % 2:et % 2 + 1]).then_inc(s["rsum_done"], 1)
                dve.wait_ge(s["rsum_done"], n)
                dve.wait_ge(s["sl_ready"], n + CREDIT)
                nc.vector.tensor_scalar(sl[:, et % 2], pO[:, et % 2, 0:C], r, None, ALU.mult).then_inc(s["sl_scaled"], 1)

            with dve.Fori(0, B) as b:
                dve.wait_ge(s["o_ready"], b * NTB + CREDIT)
                dve.wait_ge(s["stat4"], b + 1)
                normalise(b, 0)
                for g in range(NG):
                    if g + 1 < NG:
                        if g:
                            dve.wait_ge(s["xn_done"], b * NTB + g * GT)
                        normalise(b, g + 1)
                    rows(b, g)
                b0 = b
                maxima(b, 0)
                for et in range(E):
                    b = fresh(dve, b0)
                    if et + 1 < E:
                        maxima(b, et + 1)
                    for g in range(2, NG):
                        copy_t(b, ("exp", et, g))
                    scale_slots(b, et)
                    if et:
                        copy_t(b, ("slots", et - 1, 0))
                copy_t(b, ("slots", E - 1, 0))
                b = fresh(dve, b0)
                for et in range(E):
                    dve.wait_ge(s["y_ready"], b * E + et + 1)
                    nc.vector.tensor_tensor(proc[:, et], pO[:, et % 2, 0:C], m.mod[:, bass.ds(b, 1), GB, :].squeeze(1),
                                            ALU.mult).then_inc(s["y_done"], 1)

                def cmaxima(b, t):
                    n = b * NTB + t + 1
                    dve.wait_ge(s["r_ready"], n)
                    nc.vector.reduce_max(cmax[:, t % 2:t % 2 + 1], pL[:, t % 2 * NS:(t % 2 + 1) * NS], axis=AX).then_inc(s["cmax_done"], 1)
                    dve.wait_ge(s["cmax_done"], n)
                    nc.vector.tensor_scalar(cmax[:, t % 2:t % 2 + 1], cmax[:, t % 2:t % 2 + 1], -1.0, None,
                                            ALU.mult).then_inc(s["cnmax_done"], 1)

                def update(b, t):
                    n = b * NTB + t + 1
                    r = crs[:, t % 2:t % 2 + 1]
                    xt = m.x[:, bass.ds(b * NTB + t, 1), :].squeeze(1)
                    dve.wait_ge(s["o_ready"], n + CREDIT)
                    dve.wait_ge(s["crs_done"], n + CREDIT)
                    nc.vector.scalar_tensor_tensor(out=xt, in0=pO[:, t % 2, 0:C], scalar=r, in1=xt,
                                                   op0=ALU.mult, op1=ALU.add).then_inc(s["x_done"], 1)
                    dve.wait_ge(s["x_done"], n + CREDIT)
                    nc.vector.bn_stats(m.st[:, bass.ds(b * NTB + t, 1), :].squeeze(1), xt)

                cmaxima(b, 0)
                dve.wait_ge(s["proch_done"], b + 1)
                nc.vector.tensor_tensor(procl, proc[:].rearrange("p e c -> p (e c)"), proch.bitcast(F32),
                                        ALU.subtract).then_inc(s["procl_done"], 1)
                for t in range(NTB):
                    b = fresh(dve, b0)
                    if t + 1 < NTB:
                        cmaxima(b, t + 1)
                    dve.wait_ge(s["pt_ready"], b * NTB + t + 1 + CREDIT)
                    dve.wait_ge(s["pch_done"], b * NTB + t + 1)
                    nc.vector.tensor_tensor(pcl[:, t % 2], pT[:].rearrange("p s n -> p (s n)"), pch[:, t % 2].bitcast(F32),
                                            ALU.subtract).then_inc(s["pt_copied"], 1)
                    nc.vector.reciprocal(crs[:, t % 2:t % 2 + 1], csum[:, t % 2:t % 2 + 1]).then_inc(s["crs_done"], 1)
                    if t:
                        update(b, t - 1)
                update(b, NTB - 1)

        @block.scalar
        def _(act):
            def exps(b, et):
                n = b * E + et + 1
                act.wait_ge(s["nmax_done"], n)
                act.wait_ge(s["sl_ready"], b * E + max(et - 1, 0) + CREDIT)
                nc.scalar.activation(work[:, et % 2], pL[:], ACT.Exp, bias=nmax[:, et % 2:et % 2 + 1],
                                     accum_out=esum[:, et % 2:et % 2 + 1]).then_inc(s["exp_done"], 1)
                nc.scalar.copy(raw[:, et, :], pL[:]).then_inc(s["raw_done"], 1)

            def cexps(b, t):
                n = b * NTB + t + 1
                act.wait_ge(s["cnmax_done"], n)
                act.wait_ge(s["pt_ready"], b * NTB + max(t - 1, 0) + CREDIT)
                act.wait_ge(s["crs_done"], b * NTB + max(t - 1, 0) + CREDIT)
                nc.scalar.activation(pc[:, t % 2], pL[:, t % 2 * NS:(t % 2 + 1) * NS], ACT.Exp,
                                     bias=cmax[:, t % 2:t % 2 + 1], accum_out=csum[:, t % 2:t % 2 + 1]).then_inc(s["cexp_done"], 1)

            def copy_xT(b, g):
                act.wait_ge(s["xT_ready"], b * NG + g + 1)
                nc.scalar.copy(xnT[:, :, g * GW:(g + 1) * GW], (pT if g % 2 == 0 else pO)[:]).then_inc(s["xT_copied"], 1)

            with act.Fori(0, B) as b0:
                b = b0
                for g in range(NG):
                    n = b * NG + g + 1
                    act.wait_ge(s["shifted"], n)
                    for k in range(GT):
                        if g or k:
                            act.wait_ge(s["squared"], b * NTB + g * GT + k)
                        nc.scalar.activation(sq, hg[:, g % 2, k, :], ACT.Square,
                                             accum_out=ss[:, g * GT + k:g * GT + k + 1]).then_inc(s["squared"], 1)
                    if g:
                        copy_xT(b, g - 1)
                copy_xT(b, NG - 1)
                b = fresh(act, b0)
                act.wait_ge(s["xn_done"], b * NTB + NTB)
                exps(b, 0)
                for et in range(E):
                    b = fresh(act, b0)
                    for g in range(2):
                        n = at["exp", et, g]
                        act.wait_ge(s["t_ready"], b * len(seq) + n + 1)
                        nc.scalar.copy(eT[:, g % 2], pT[:, n % 2]).then_inc(s["t_copied_a"], 1)
                    if et + 1 < E:
                        exps(b, et + 1)
                b = fresh(act, b0)
                act.wait_ge(s["sl_ready"], b * E + E + CREDIT)
                for a in range(SH):
                    for j in range(HT):
                        n = b * SH * HT + a * HT + j + 1
                        act.wait_ge(s["h_ready"], n)
                        if a and j == 0:
                            act.wait_ge(s["y_ready"], b * E + a * E // SH)
                        nc.scalar.activation(hid[:, j, :], pL[:, j % 4 * 512:(j % 4 + 1) * 512], ACT.Gelu).then_inc(s["h_done"], 1)
                b = fresh(act, b0)
                act.wait_ge(s["y_done"], b * E + E)
                nc.scalar.copy(proch, proc[:].rearrange("p e c -> p (e c)")).then_inc(s["proch_done"], 1)
                cexps(b, 0)
                for t in range(NTB):
                    b = fresh(act, b0)
                    act.wait_ge(s["pt_ready"], b * NTB + t + 1 + CREDIT)
                    nc.scalar.copy(pch[:, t % 2], pT[:].rearrange("p s n -> p (s n)")).then_inc(s["pch_done"], 1)
                    if t + 1 < NTB:
                        cexps(b, t + 1)

        @block.tensor
        def _(pe):
            def logits_of(et, g):
                for k in range(CH):
                    last = nc.tensor.matmul(pL[:, g * GW:(g + 1) * GW], m.seT[:, k, et * P:(et + 1) * P],
                                            xnT[:, k, g * GW:(g + 1) * GW], start=k == 0, stop=k == CH - 1)
                return last

            def logits(b, et):
                pe.wait_ge(s["raw_done"], b * E + et)
                for g in range(NG):
                    last = logits_of(et, g)
                last.then_inc(s["l_ready"], 1)

            def transposes(b, key):
                n = at[key]
                kind, et, g = key
                if n >= 2:
                    await_copy(pe, b, n - 2)
                if kind == "exp":
                    for j in range(GT):
                        last = nc.tensor.transpose(pT[:, n % 2, j * P:(j + 1) * P],
                                                   work[:, et % 2, g * GW + j * P:g * GW + (j + 1) * P], m.ident[:])
                else:
                    for h in range(CH):
                        last = nc.tensor.transpose(pT[:, n % 2, h * P:(h + 1) * P], sl[:, et % 2, h * P:(h + 1) * P], m.ident[:])
                last.then_inc(s["t_ready"], 1)

            def slots(b, et, g):
                await_copy(pe, b, at["exp", et, g])
                for j in range(GT):
                    last = nc.tensor.matmul(pO[:, et % 2, 0:C], eT[:, g % 2, j * P:(j + 1) * P], xn[:, g * GT + j, :],
                                            start=g == 0 and j == 0, stop=g == NG - 1 and j == GT - 1)
                if g == NG - 1:
                    last.then_inc(s["sl_ready"], 1)

            with pe.Fori(0, B) as b0:
                b = b0
                for g in range(NG):
                    pe.wait_ge(s["xn_done"], b * NTB + (g + 1) * GT)
                    if g == 0:
                        pe.wait_ge(s["pt_copied"], b * NTB + CREDIT)
                        pe.wait_ge(s["x_done"], b * NTB + CREDIT)
                    if g >= 2:
                        pe.wait_ge(s["xT_copied"], b * NG + g - 1)
                    for h in range(CH):
                        for k in range(GT):
                            last = nc.tensor.transpose((pT if g % 2 == 0 else pO)[:, h, k * P:(k + 1) * P],
                                                       xn[:, g * GT + k, h * P:(h + 1) * P], m.ident[:])
                    last.then_inc(s["xT_ready"], 1)
                    if g == 0:
                        pe.wait_ge(s["cexp_done"], b * NTB + CREDIT)
                    else:
                        pe.wait_ge(s["xT_copied"], b * NG + g)
                        logits_of(0, g - 1)
                pe.wait_ge(s["xT_copied"], b * NG + NG)
                logits_of(0, NG - 1).then_inc(s["l_ready"], 1)
                for et in range(E):
                    b = fresh(pe, b0)
                    if et + 1 < E:
                        logits(b, et + 1)
                    pe.wait_ge(s["exp_done"], b * E + et + 1)
                    pe.wait_ge(s["sl_scaled"], b * E + max(et - 1, 0) + CREDIT)
                    transposes(b, ("exp", et, 0))
                    for g in range(NG):
                        if g + 1 < NG:
                            transposes(b, ("exp", et, g + 1))
                        slots(b, et, g)
                    if et:
                        pe.wait_ge(s["sl_scaled"], b * E + et + CREDIT)
                        transposes(b, ("slots", et - 1, 0))
                pe.wait_ge(s["sl_scaled"], b * E + E + CREDIT)
                transposes(b, ("slots", E - 1, 0))
                b = fresh(pe, b0)
                await_copy(pe, b, len(seq) - 1)
                pe.wait_ge(s["raw_done"], b * E + E)
                for a in range(SH):
                    for j in range(HT):
                        n = b * SH * HT + a * HT + j
                        if a or j >= 4:
                            pe.wait_ge(s["h_done"], n - 3)
                        for k in range(CH):
                            last = nc.tensor.matmul(pL[:, j % 4 * 512:(j % 4 + 1) * 512], m.w1[:, k, j * P:(j + 1) * P],
                                                    slotsT[:, k, a * 512:(a + 1) * 512], start=k == 0, stop=k == CH - 1)
                        last.then_inc(s["h_ready"], 1)
                    pe.wait_ge(s["h_done"], b * SH * HT + (a + 1) * HT)
                    for e in range(4):
                        et = a * 4 + e
                        if et >= 2:
                            pe.wait_ge(s["y_done"], b * E + et - 1)
                        for j in range(HT):
                            last = nc.tensor.matmul(pO[:, et % 2, 0:C], hid[:, j, e * P:(e + 1) * P], m.w2[:, j, :],
                                                    start=j == 0, stop=j == HT - 1)
                        last.then_inc(s["y_ready"], 1)

                def by_token(b, t):
                    pe.wait_ge(s["cexp_done"], b * NTB + max(t - 1, 0) + CREDIT)
                    for e in range(E):
                        o = t % 2 * NS + e * P
                        last = nc.tensor.transpose(pL[:, o:o + P], raw[:, e, t * P:(t + 1) * P], m.ident[:])
                    last.then_inc(s["r_ready"], 1)

                def combine(b, t):
                    pe.wait_ge(s["pt_copied"], b * NTB + t + 1 + CREDIT)
                    pe.wait_ge(s["x_done"], b * NTB + max(t - 1, 0) + CREDIT)
                    for e in range(E):
                        tok, feat = slice(e * P, (e + 1) * P), slice(e * C, (e + 1) * C)
                        last = exact_matmul(nc, pO[:, t % 2, 0:C], pch[:, t % 2, tok], pcl[:, t % 2, tok], proch[:, feat],
                                            procl[:, feat], e == 0, e == E - 1)
                    last.then_inc(s["o_ready"], 1)

                b = fresh(pe, b0)
                pe.wait_ge(s["y_done"], b * E + E)
                by_token(b, 0)
                pe.wait_ge(s["procl_done"], b + 1)
                for t in range(NTB):
                    b = fresh(pe, b0)
                    n = b * NTB + t + 1
                    if t + 1 < NTB:
                        by_token(b, t + 1)
                    pe.wait_ge(s["cexp_done"], n + CREDIT)
                    pe.wait_ge(s["pt_copied"], n - 1 + CREDIT)
                    for e in range(E):
                        last = nc.tensor.transpose(pT[:, e // 4, e % 4 * P:(e % 4 + 1) * P], pc[:, t % 2, e * P:(e + 1) * P], m.ident[:])
                    last.then_inc(s["pt_ready"], 1)
                    if t:
                        combine(b, t - 1)
                combine(b, NTB - 1)


STATE, HEADS = 64, 8
INNER = 2 * C
HD = INNER // HEADS
PROJ = 2 * INNER + 2 * STATE + HEADS
ZX = 2 * INNER
DT0 = ZX + 2 * STATE


def least(v):
    return max(v, 0) if isinstance(v, int) else v


def state_inputs(nc, m, w):
    with ExitStack() as ctx:
        sb, ps, sem = setup(nc, ctx)
        hg, un = sb("e_hg", [P, B, GT, C]), sb("e_un", [P, B, GT, C])
        ug = sb("e_ug", [P, B, CH, GW])
        gated = sb("e_gated", [P, B, GT, C])
        wdt = sb("e_wdt", [P, CH, HEADS])
        gb = sb("e_gb", [P, 2, CH])
        bout = sb("e_bout", [P, C])
        b3 = sb("e_b3", [3, 3, DT0])
        bdt, bdt2 = sb("e_bdt", [P, HEADS]), sb("e_bdt2", [P, HEADS])
        st2, mv = sb("e_st2", [P, B, GT, 6]), sb("e_mv", [P, B, GT, 2])
        rs = sb("e_rs", [P, B, GT])
        pT = ps("e_pT", [P, 2, CH, GW])
        pd = ps("e_pd", [P, 2, 512])
        names = ("loaded bias stat0 stat1 stat2 stat3 stat4 normed scaled shifted st2 mv var_done powed un_done kept gated x_done t_ready "
                 "t_copied d_ready d_done b_in w_in b0 b1 b2 b3").split()
        s = {n: sem("e_" + n) for n in names}
        u_out = [sem(f"e_u_out{b}") for b in range(B)]
        block = ctx.enter_context(nc.Block())
        st_vector, st_gpsimd = finish_stats(nc, [s[f"stat{i}"] for i in range(5)], m, 0, NT)

        @block.sync
        def _(sp):
            sp.dma_start(b3[:, 0], w["b_in"][0:DT0].partition_broadcast(3)).then_inc(s["b_in"], 16)
            sp.dma_start(wdt[:], w["W_in"][:, DT0:PROJ].rearrange("(h p) n -> p h n", p=P)).then_inc(s["loaded"], 16)
            sp.dma_start(gb[:], w["ln_cols"]).then_inc(s["loaded"], 16)
            sp.dma_start(bout[:], w["b_out"].partition_broadcast(P)).then_inc(s["loaded"], 16)
            sp.dma_start(bdt[:], w["b_in"][DT0:PROJ].partition_broadcast(P)).then_inc(s["loaded"], 16)
            sp.dma_start(bdt2[:], w["dt_bias"].partition_broadcast(P)).then_inc(s["loaded"], 16)
            sp.dma_start(m.win, w["W_in"][:, 0:DT0].rearrange("(h p) n -> p h n", p=P)).then_inc(s["w_in"], 16)
            sp.dma_start(m.wout[:], w["W_out"].rearrange("(h p) n -> p h n", p=P)).then_inc(s["w_in"], 16)
            with sp.Fori(0, NG) as i:
                for b in range(B):
                    sp.wait_ge(s["t_copied"], i * B + b + 1)
                    sp.dma_start(m.uT[:, :, bass.ds(b * T + i * GW, GW)], ug[:, b]).then_inc(u_out[b], 16)
            for b in range(B):
                sp.wait_ge(u_out[b], 16 * NG)

        def split_bias():
            v = nc.vector
            v.memset(m.ones3[:], 1.0)
            v.wait_ge(s["b_in"], 16)
            for k in range(2):
                v.tensor_copy(m.bb[:, k], b3[:, k]).then_inc(s["b0"], 1)
                v.wait_ge(s["b0"], k + 1)
                v.tensor_tensor(b3[:, k + 1], b3[:, k], m.bb[:, k], ALU.subtract).then_inc(s["b1"], 1)
                v.wait_ge(s["b1"], k + 1)
            i3 = m.ident[0:3, :]
            v.tensor_scalar(b3[:, 0], m.bb[:, 0], i3[:, 0:1], None, ALU.mult).then_inc(s["b2"], 1)
            v.wait_ge(s["b2"], 1)
            v.scalar_tensor_tensor(out=b3[:, 0], in0=m.bb[:, 1], scalar=i3[:, 1:2], in1=b3[:, 0],
                                   op0=ALU.mult, op1=ALU.add).then_inc(s["b3"], 1)
            v.wait_ge(s["b3"], 1)
            v.scalar_tensor_tensor(out=m.bb[:, 0], in0=b3[:, 2], scalar=i3[:, 2:3], in1=b3[:, 0],
                                   op0=ALU.mult, op1=ALU.add)

        def steps(eng, step):
            step(0, 0, 0, first=True)
            step(1, 0, 1)
            with eng.Fori(1, NG - 1) as i:
                step(i * B, i, 0)
                step(i * B + 1, i, 1)
            step(NG * B - 2, NG - 1, 0)
            step(NG * B - 1, NG - 1, 1, last=True)

        @block.gpsimd
        def _(pool):
            st_gpsimd()

            def shift(n, b):
                pool.wait_ge(s["scaled"], n + 1)
                nc.gpsimd.tensor_tensor(hg[:, b], hg[:, b], over(m.mod[:, b, SA, :], GT), ALU.add).then_inc(s["shifted"], 1)

            def step(n, i, b, first=False, last=False):
                if not last:
                    shift(n + 1, 1 - b)
                pool.wait_ge(s["var_done"], n + 1)
                nc.gpsimd.tensor_tensor(rs[:, b], rs[:, b], m.neghalf[:, 0:GT], ALU.pow).then_inc(s["powed"], 1)
                pool.wait_ge(s["kept"], n + 1)
                nc.gpsimd.tensor_tensor(gated[:, b], gated[:, b], over(m.mod[:, b, GA, :], GT), ALU.mult).then_inc(s["gated"], 1)

            shift(0, 0)
            steps(pool, step)

        @block.vector
        def _(dve):
            st_vector()
            split_bias()
            dve.wait_ge(s["stat4"], 1)

            def normalise(n, i, b):
                for k in range(GT):
                    t = bass.ds(b * NTB + i * GT + k, 1)
                    nc.vector.tensor_scalar(hg[:, b, k, :], m.x[:, t, :].squeeze(1), m.mean[:, t], m.rstd[:, t],
                                            ALU.subtract, ALU.mult).then_inc(s["normed"], 1)
                dve.wait_ge(s["normed"], (n + 1) * GT)
                nc.vector.tensor_tensor(hg[:, b], hg[:, b], over(m.mod[:, b, CA, :], GT), ALU.mult).then_inc(s["scaled"], 1)

            def finish(n, i, b):
                xg = m.x[:, bass.ds(b * NTB + i * GT, GT), :]
                dve.wait_ge(s["gated"], n + 1)
                nc.vector.tensor_tensor(xg, xg, gated[:, b], ALU.add).then_inc(s["x_done"], 1)
                dve.wait_ge(s["d_ready"], n + 1)
                nc.vector.tensor_tensor(m.dt[:, bass.ds(b * NTB + i * GT, GT), :],
                                        pd[:, b, 0:GT * HEADS].rearrange("p (t h) -> p t h", h=HEADS),
                                        bdt[:].unsqueeze(1).to_broadcast([P, GT, HEADS]), ALU.add).then_inc(s["d_done"], 1)

            def step(n, i, b, first=False, last=False):
                if not last:
                    if not first:
                        dve.wait_ge(s["kept"], n)
                        dve.wait_ge(s["un_done"], n * GT)
                    normalise(n + 1, i + b, 1 - b)
                dve.wait_ge(s["shifted"], n + 1)
                for k in range(GT):
                    nc.vector.bn_stats(st2[:, b, k, :], hg[:, b, k, :]).then_inc(s["st2"], 1)
                dve.wait_ge(s["st2"], (n + 1) * GT)
                if not (isinstance(n, int) and n < 2):
                    dve.wait_ge(s["x_done"], n - 1)
                nc.vector.tensor_tensor(gated[:, b], hg[:, b], over(bout[:], GT), ALU.add).then_inc(s["kept"], 1)
                for k in range(GT):
                    nc.vector.bn_aggr(mv[:, b, k, :], st2[:, b, k, :]).then_inc(s["mv"], 1)
                dve.wait_ge(s["mv"], (n + 1) * GT)
                nc.vector.tensor_scalar(rs[:, b], mv[:, b, :, 1], LN_EPS, None, ALU.add).then_inc(s["var_done"], 1)
                if not first:
                    finish(n - 1, i - 1 + b, 1 - b)
                dve.wait_ge(s["powed"], n + 1)
                if not (isinstance(n, int) and n < 2):
                    dve.wait_ge(s["t_ready"], n - 1)
                for k in range(GT):
                    nc.vector.tensor_scalar(un[:, b, k, :], hg[:, b, k, :], mv[:, b, k, 0:1], rs[:, b, k:k + 1],
                                            ALU.subtract, ALU.mult).then_inc(s["un_done"], 1)
                if last:
                    finish(n, i, b)

            normalise(0, 0, 0)
            dve.wait_ge(s["loaded"], 80)
            nc.vector.tensor_tensor(bdt[:], bdt[:], bdt2[:], ALU.add).then_inc(s["bias"], 1)
            dve.wait_ge(s["bias"], 1)
            steps(dve, step)

        @block.scalar
        def _(act):
            act.wait_ge(s["loaded"], 80)

            def group(i, b):
                n = i * B + b + 1
                act.wait_ge(s["t_ready"], n)
                if not isinstance(i, int):
                    act.wait_ge(u_out[b], 16 * i)
                    act.wait_ge(s["d_ready"], n - 2)
                for h in range(CH):
                    last = nc.scalar.activation(ug[:, b, h, :], pT[:, b, h, :], ACT.Identity,
                                                scale=gb[:, 0, h:h + 1], bias=gb[:, 1, h:h + 1])
                last.then_inc(s["t_copied"], 1)

            group(0, 0)
            group(0, 1)
            act.wait_ge(s["w_in"], 32)
            nc.scalar.copy(m.winh[:], m.win)
            with act.Fori(1, NG) as i:
                group(i, 0)
                group(i, 1)

        @block.tensor
        def _(pe):
            pe.wait_ge(s["loaded"], 80)
            with pe.Fori(0, NG) as i:
                for b in range(B):
                    n = i * B + b + 1
                    pe.wait_ge(s["un_done"], n * GT)
                    for h in range(CH):
                        for k in range(GT):
                            last = nc.tensor.transpose(pT[:, b, h, k * P:(k + 1) * P], un[:, b, k, h * P:(h + 1) * P], m.ident[:])
                    last.then_inc(s["t_ready"], 1)
                    pe.wait_ge(s["t_copied"], n)
                    for k in range(GT):
                        for h in range(CH):
                            last = nc.tensor.matmul(pd[:, b, k * HEADS:(k + 1) * HEADS], ug[:, b, h, k * P:(k + 1) * P],
                                                    wdt[:, h, :], start=h == 0, stop=h == CH - 1)
                    last.then_inc(s["d_ready"], 1)


def decays(nc, m, w):
    with ExitStack() as ctx:
        sb, ps, sem = setup(nc, ctx)
        NC_ = NT * HEADS
        raw = m.dt[:].rearrange("p t h -> p (t h)")
        a, e, u, d, z, l, lw, dA, cum = [sb("f_" + n, [P, NC_]) for n in ("a", "e", "u", "d", "z", "l", "lw", "dA", "cum")]
        neg = sb("f_neg", [P, HEADS])
        cumT = sb("f_cumT", [P, 2, P])
        pc, psf, pt, pT = [ps("f_" + n, [P, 512]) for n in ("pc", "psf", "pt", "pT")]
        names = ("loaded a0 a1 a2 a3 a4 v0 v1 v2 v3 v4 v5 v6 v7 v8 cum_ready cum_copied t_ready t_copied wog wogh").split()
        s = {n: sem("f_" + n) for n in names}
        block = ctx.enter_context(nc.Block())
        dt, wdt, ecum, cums = [m.cs[:, :, k, :] for k in range(4)]
        tiles = lambda t: t.rearrange("p (t h) -> p t h", h=HEADS)

        @block.sync
        def _(sp):
            sp.dma_start(neg[:], w["A_log"].partition_broadcast(P)).then_inc(s["loaded"], 16)
            sp.wait_ge(s["t_copied"], 1)
            sp.dma_start(m.cum_dram.rearrange("(a p) t -> p a t", p=P), cumT[:]).then_inc(s["loaded"], 16)
            sp.wait_ge(s["loaded"], 32)

        @block.scalar
        def _(act):
            nc.scalar.activation(a[:], raw, ACT.Abs).then_inc(s["a0"], 1)
            act.wait_ge(s["a0"], 1)
            nc.scalar.activation(e[:], a[:], ACT.Exp, scale=-1.0).then_inc(s["a1"], 1)
            act.wait_ge(s["loaded"], 16)
            nc.scalar.activation(neg[:], neg[:], ACT.Exp).then_inc(s["a2"], 1)
            act.wait_ge(s["v0"], 1)
            nc.scalar.activation(lw[:], u[:], ACT.Ln).then_inc(s["a3"], 1)
            act.wait_ge(s["wog"], B)
            nc.scalar.copy(m.wogh[:], m.wog).then_inc(s["wogh"], 1)
            act.wait_ge(s["cum_ready"], 1)
            nc.scalar.activation(ecum, tiles(pc[:, 0:NC_]), ACT.Exp)
            nc.scalar.activation(m.etot[:].rearrange("p t h -> p (t h)"), pt[0:STATE, 0:NC_], ACT.Exp)
            nc.scalar.activation(z[:], psf[:, 0:NC_], ACT.Exp).then_inc(s["a4"], 1)

        @block.vector
        def _(dve):
            for b in range(B):
                nc.vector.scalar_tensor_tensor(out=m.wog[:, b], in0=m.wout[:], scalar=0.5, in1=over(m.mod[:, b, GA, :], INNER // P),
                                               op0=ALU.mult, op1=ALU.mult).then_inc(s["wog"], 1)
            dve.wait_ge(s["a1"], 1)
            nc.vector.tensor_scalar_add(u[:], e[:], 1.0).then_inc(s["v0"], 1)
            dve.wait_ge(s["v0"], 1)
            nc.vector.tensor_scalar_add(d[:], u[:], -1.0).then_inc(s["v1"], 1)
            dve.wait_ge(s["v1"], 1)
            nc.vector.tensor_scalar(z[:], d[:], 0.0, None, ALU.is_equal).then_inc(s["v2"], 1)
            dve.wait_ge(s["v2"], 1)
            nc.vector.tensor_tensor(d[:], d[:], z[:], ALU.add).then_inc(s["v3"], 1)
            dve.wait_ge(s["v3"], 1)
            nc.vector.reciprocal(d[:], d[:]).then_inc(s["v4"], 1)
            nc.vector.tensor_tensor(z[:], z[:], e[:], ALU.mult).then_inc(s["v4"], 1)
            dve.wait_ge(s["v4"], 2)
            nc.vector.tensor_tensor(d[:], d[:], e[:], ALU.mult).then_inc(s["v5"], 1)
            dve.wait_ge(s["a3"], 1)
            dve.wait_ge(s["v5"], 1)
            nc.vector.tensor_tensor(l[:], lw[:], d[:], ALU.mult).then_inc(s["v6"], 1)
            dve.wait_ge(s["v6"], 1)
            nc.vector.tensor_tensor(l[:], l[:], z[:], ALU.add).then_inc(s["v6"], 1)
            dve.wait_ge(s["v6"], 2)
            nc.vector.scalar_tensor_tensor(out=dt, in0=tiles(raw), scalar=0.0, in1=tiles(l[:]),
                                           op0=ALU.max, op1=ALU.add).then_inc(s["v7"], 1)
            dve.wait_ge(s["a2"], 1)
            dve.wait_ge(s["v7"], 1)
            nc.vector.scalar_tensor_tensor(out=tiles(dA[:]), in0=dt, scalar=-1.0,
                                           in1=neg[:].unsqueeze(1).to_broadcast([P, NT, HEADS]),
                                           op0=ALU.mult, op1=ALU.mult).then_inc(s["v8"], 1)
            nc.vector.tensor_tensor(m.winl[:], m.win, m.winh[:].bitcast(F32), ALU.subtract)
            dve.wait_ge(s["cum_ready"], 1)
            dve.wait_ge(s["a4"], 1)
            nc.vector.tensor_copy(cum[:], pc[:, 0:NC_]).then_inc(s["cum_copied"], 1)
            nc.vector.tensor_copy(cums, tiles(pc[:, 0:NC_]))
            nc.vector.tensor_tensor(wdt, dt, tiles(z[:]), ALU.mult)
            dve.wait_ge(s["wogh"], 1)
            nc.vector.tensor_tensor(m.wogl[:], m.wog, m.wogh[:].bitcast(F32), ALU.subtract)
            dve.wait_ge(s["t_ready"], 1)
            nc.vector.tensor_copy(cumT[:].rearrange("p a t -> p (a t)"), pT[:, 0:2 * P]).then_inc(s["t_copied"], 1)

        @block.tensor
        def _(pe):
            pe.wait_ge(s["v8"], 1)
            nc.tensor.matmul(pc[:, 0:NC_], m.upto[:], dA[:], start=True, stop=True)
            nc.tensor.matmul(psf[:, 0:NC_], m.after[:], dA[:], start=True, stop=True)
            nc.tensor.matmul(pt[0:STATE, 0:NC_], m.ones[:, 0:STATE], dA[:], start=True, stop=True).then_inc(s["cum_ready"], 1)
            pe.wait_ge(s["cum_copied"], 1)
            for k in range(2):
                last = nc.tensor.transpose(pT[:, k * P:(k + 1) * P], cum[:, k * P:(k + 1) * P], m.ident[:])
            last.then_inc(s["t_ready"], 1)


def state_space(nc, m, w):
    with ExitStack() as ctx:
        sb, ps, sem = setup(nc, ctx)
        winh, winl, wogh, wogl, bb, ones3, cumb = m.winh, m.winl, m.wogh, m.wogl, m.bb, m.ones3, m.cumb
        dskip = sb("g_dskip", [P, HEADS])
        uh, ul = sb("g_uh", [P, B, CH, P], FR), sb("g_ul", [P, B, CH, P], FR)
        cs = sb("g_cs", [P, B, 4, HEADS])
        et = sb("g_et", [STATE, B, HEADS])
        bc = sb("g_bc", [P, B, 2 * STATE])
        bcT = sb("g_bcT", [STATE, B, 2, P])
        wide6 = sb("g_wide", [P, 6, B, INNER])
        xs, dtx, xw, xD, zr, y = [wide6[:, k] for k in range(6)]
        th = sb("g_th", [P, INNER])
        gm = sb("g_gm", [P, B, P])
        dd, le, mt = [m.dlm[:, k] for k in range(3)]
        H = sb("g_H", [STATE, B, INNER])
        yh, yl = sb("g_yh", [P, INNER // P, P], FR), sb("g_yl", [P, INNER // P, P], FR)
        pz, px, pbc, pbt, py, pi, pst, pyT = [ps("g_p" + n, [P, 512]) for n in ("z", "x", "bc", "bt", "y", "i", "st", "yT")]
        po = pyT[:, 0:C]
        names = ("loaded ip_ready bc_copied xs_copied th_done bt_ready bt_copied g_ready gm_done "
                 "zr_done lcm_done le_done m_done dtx_done xw_done xD_done i_ready st_ready y_ready "
                 "t1_done t2_done y_done hs_done h_done yg_done yT_ready yh_done yl_done o_ready x_done uh_done ul_done").split()
        s = {n: sem("g_" + n) for n in names}
        cs_in = [sem(f"g_cs_in{b}") for b in range(B)]
        block = ctx.enter_context(nc.Block())
        heads = lambda t: t.rearrange("p (h d) -> p h d", h=HEADS)
        wide = lambda col, p=P: col.unsqueeze(2).to_broadcast([p, HEADS, HD])

        def jobs(eng, step):
            step(None, (0, 0), (0, 1))
            step((0, 0), (0, 1), (1, 0))
            with eng.Fori(1, NTB - 1) as i:
                step((i - 1, 1), (i, 0), (i, 1))
                step((i, 0), (i, 1), (i + 1, 0))
            i = NTB - 1
            step((i - 1, 1), (i, 0), (i, 1))
            step((i, 0), (i, 1), None)
            step((i, 1), None, None)

        def num(job):
            return job[0] * B + job[1]

        def after(job):
            i, b = job
            return None if b and isinstance(i, int) and i == NTB - 1 else (i + b, 1 - b)

        @block.sync
        def _(sp):
            sp.dma_start(dskip[:], w["D_skip"].partition_broadcast(P)).then_inc(s["loaded"], 16)

            def stage(i, b):
                n = i * B + b
                t = b * NTB + i
                if not (isinstance(i, int) and i == 0):
                    sp.wait_ge(s["lcm_done"], (n - 1) * HEADS)
                    sp.wait_ge(s["t1_done"], n - 1)
                    sp.wait_ge(s["hs_done"], n - 1)
                    sp.wait_ge(s["xw_done"], n - 1)
                sp.dma_start(cs[:, b], m.cs[:, bass.ds(t, 1)].squeeze(1)).then_inc(cs_in[b], 16)
                sp.dma_start(et[:, b], m.etot[:, bass.ds(t, 1)].squeeze(1)).then_inc(cs_in[b], 16)
                sp.dma_start(cumb[:, b].rearrange("p h t -> p (h t)"),
                             m.cum_dram[bass.ds(t * HEADS, HEADS), :].rearrange("h t -> (h t)").partition_broadcast(P)).then_inc(cs_in[b], 16)

            stage(0, 0)
            stage(0, 1)
            with sp.Fori(1, NTB) as i:
                stage(i, 0)
                stage(i, 1)

        @block.gpsimd
        def _(pool):
            def products(job):
                i, b = job
                n = num(job)
                pool.wait_ge(s["xs_copied"], n + 1)
                pool.wait_ge(cs_in[b], (i + 1) * 48)
                pool.wait_ge(s["y_ready"], least(n - 1))
                nc.gpsimd.tensor_tensor(heads(dtx[:, b]), heads(xs[:, b]), wide(cs[:, b, 0]), ALU.mult).then_inc(s["dtx_done"], 1)
                pool.wait_ge(s["st_ready"], least(n - 1))
                nc.gpsimd.tensor_tensor(heads(xw[:, b]), heads(xs[:, b]), wide(cs[:, b, 1]), ALU.mult).then_inc(s["xw_done"], 1)
                pool.wait_ge(s["t2_done"], least(n - 1))
                nc.gpsimd.tensor_tensor(heads(xD[:, b]), heads(xs[:, b]), wide(dskip[:]), ALU.mult).then_inc(s["xD_done"], 1)

            def gate(job):
                i, b = job
                n = num(job)
                pool.wait_ge(s["y_done"], n + 1)
                nc.gpsimd.tensor_tensor(y[:, b], y[:, b], zr[:, b], ALU.mult).then_inc(s["yg_done"], 1)

            pool.wait_ge(s["loaded"], 16)
            products((0, 0))

            def step(prev, cur, nxt):
                if nxt:
                    products(nxt)
                if cur:
                    gate(cur)
            jobs(pool, step)

        @block.scalar
        def _(act):
            def high(job):
                i, b = job
                n = num(job)
                if not (isinstance(i, int) and i == 0):
                    act.wait_ge(s["ip_ready"], n - 1)
                nc.scalar.copy(uh[:, b], m.uT[:, :, bass.ds((b * NTB + i) * P, P)]).then_inc(s["uh_done"], 1)

            def evacuate(job):
                i, b = job
                n = num(job)
                act.wait_ge(s["ip_ready"], n + 1)
                act.wait_ge(s["st_ready"], least(n - 1))
                nc.scalar.copy(bc[:, b], pbc[:, 0:2 * STATE]).then_inc(s["bc_copied"], 1)
                act.wait_ge(s["xD_done"], least(n - 1))
                nc.scalar.copy(xs[:, b], px[:]).then_inc(s["xs_copied"], 1)
                act.wait_ge(s["zr_done"], n)
                nc.scalar.activation(th[:], pz[:], ACT.Tanh, scale=0.5).then_inc(s["th_done"], 1)

            def by_state(job):
                i, b = job
                n = num(job)
                act.wait_ge(s["bt_ready"], n + 1)
                act.wait_ge(s["i_ready"], least(n - 1))
                nc.scalar.copy(bcT[:, b].rearrange("p a t -> p (a t)"), pbt[0:STATE, 0:2 * P]).then_inc(s["bt_copied"], 1)

            high((0, 0))
            high((0, 1))
            evacuate((0, 0))
            by_state((0, 0))

            def step(prev, cur, nxt):
                if cur:
                    n = num(cur)
                    act.wait_ge(s["lcm_done"], (n + 1) * HEADS)
                    act.wait_ge(s["m_done"], n)
                    nc.scalar.activation(le, dd, ACT.Exp).then_inc(s["le_done"], 1)
                if nxt:
                    evacuate(nxt)
                if prev:
                    n = num(prev)
                    act.wait_ge(s["yT_ready"], n + 1)
                    act.wait_ge(s["o_ready"], n)
                    nc.scalar.copy(yh[:].rearrange("p k t -> p (k t)"), pyT[:]).then_inc(s["yh_done"], 1)
                if nxt:
                    by_state(nxt)
                if nxt and after(nxt):
                    high(after(nxt))
            jobs(act, step)

        @block.vector
        def _(dve):
            nc.vector.memset(H[:], 0.0)

            def low(job):
                i, b = job
                n = num(job)
                dve.wait_ge(s["uh_done"], n + 1)
                if not (isinstance(i, int) and i == 0):
                    dve.wait_ge(s["ip_ready"], n - 1)
                nc.vector.tensor_tensor(ul[:, b], m.uT[:, :, bass.ds((b * NTB + i) * P, P)], uh[:, b].bitcast(F32),
                                        ALU.subtract).then_inc(s["ul_done"], 1)

            low((0, 0))
            low((0, 1))

            def gates(job):
                i, b = job
                n = num(job)
                dve.wait_ge(s["th_done"], n + 1)
                dve.wait_ge(s["yg_done"], least(n - 1))
                nc.vector.scalar_tensor_tensor(out=zr[:, b], in0=th[:], scalar=1.0, in1=pz[:],
                                               op0=ALU.add, op1=ALU.mult).then_inc(s["zr_done"], 1)

            def masked(job):
                i, b = job
                n = num(job)
                dve.wait_ge(s["g_ready"], n + 1)
                nc.vector.tensor_tensor(gm[:, b], pbt[:, 2 * P:3 * P], m.upto[:], ALU.mult).then_inc(s["gm_done"], 1)

            def decay(job):
                i, b = job
                n = num(job)
                dve.wait_ge(cs_in[b], (i + 1) * 48)
                dve.wait_ge(s["le_done"], n)
                for h in range(HEADS):
                    nc.vector.tensor_scalar(dd[:, h, :], cumb[:, b, h, :], cs[:, b, 3, h:h + 1], 0.0,
                                            ALU.subtract, ALU.min).then_inc(s["lcm_done"], 1)

            def y_low(job):
                dve.wait_ge(s["yh_done"], num(job) + 1)
                nc.vector.tensor_tensor(yl[:].rearrange("p k t -> p (k t)"), pyT[:],
                                        yh[:].rearrange("p k t -> p (k t)").bitcast(F32), ALU.subtract).then_inc(s["yl_done"], 1)

            def body(job, prev, nxt):
                i, b = job
                n = num(job)
                dve.wait_ge(s["le_done"], n + 1)
                dve.wait_ge(s["gm_done"], n + 1)
                dve.wait_ge(s["y_ready"], n)
                nc.vector.tensor_tensor(mt, le, over(gm[:, b], HEADS), ALU.mult).then_inc(s["m_done"], 1)
                dve.wait_ge(s["i_ready"], n + 1)
                nc.vector.tensor_tensor(heads(y[:, b]), heads(pi[:]), wide(cs[:, b, 2]), ALU.mult).then_inc(s["t1_done"], 1)
                dve.wait_ge(s["h_done"], n)
                nc.vector.tensor_tensor(heads(H[:, b]), heads(H[:, b]), wide(et[:, b], STATE), ALU.mult).then_inc(s["hs_done"], 1)
                if prev:
                    y_low(prev)
                dve.wait_ge(s["hs_done"], n + 1)
                dve.wait_ge(s["st_ready"], n + 1)
                nc.vector.tensor_tensor(H[:, b], H[:, b], pst[0:STATE, :], ALU.add).then_inc(s["h_done"], 1)
                if nxt:
                    gates(nxt)
                if nxt and after(nxt):
                    low(after(nxt))
                dve.wait_ge(s["y_ready"], n + 1)
                dve.wait_ge(s["xD_done"], n + 1)
                nc.vector.tensor_tensor(xD[:, b], py[:], xD[:, b], ALU.add).then_inc(s["t2_done"], 1)
                dve.wait_ge(s["t2_done"], n + 1)
                nc.vector.tensor_tensor(y[:, b], y[:, b], xD[:, b], ALU.add).then_inc(s["y_done"], 1)

            def finish(job):
                i, b = job
                n = num(job)
                t = bass.ds(b * NTB + i, 1)
                xt = m.x[:, t, :].squeeze(1)
                dve.wait_ge(s["o_ready"], n + 1)
                nc.vector.tensor_tensor(xt, xt, po, ALU.add).then_inc(s["x_done"], 1)
                dve.wait_ge(s["x_done"], n + 1)
                nc.vector.bn_stats(m.st[:, t, :].squeeze(1), xt)

            gates((0, 0))
            masked((0, 0))

            def step(prev, cur, nxt):
                if cur:
                    decay(cur)
                    body(cur, prev, nxt)
                elif prev:
                    y_low(prev)
                if nxt:
                    masked(nxt)
                if prev:
                    finish(prev)
            jobs(dve, step)

        @block.tensor
        def _(pe):
            def project(job):
                i, b = job
                n = num(job)
                pe.wait_ge(s["ul_done"], n + 1)
                pe.wait_ge(s["bc_copied"], n)
                pe.wait_ge(s["zr_done"], n)
                pe.wait_ge(s["xs_copied"], n)
                for dst, o, width in ((pbc, ZX, 2 * STATE), (px, INNER, INNER), (pz, 0, INNER)):
                    for k in range(CH):
                        exact_matmul(nc, dst[:, 0:width], uh[:, b, k, :], ul[:, b, k, :], winh[:, k, o:o + width],
                                     winl[:, k, o:o + width], k == 0, False)
                    last = nc.tensor.matmul(dst[:, 0:width], ones3[:], bb[:, 0, o:o + width], start=False, stop=True)
                last.then_inc(s["ip_ready"], 1)

            def state_rows(job):
                i, b = job
                for k in range(2):
                    last = nc.tensor.transpose(pbt[0:STATE, k * P:(k + 1) * P], bc[:, b, k * STATE:(k + 1) * STATE], m.ident[:])
                last.then_inc(s["bt_ready"], 1)

            def await_bc(job):
                pe.wait_ge(s["bc_copied"], num(job) + 1)
                pe.wait_ge(s["gm_done"], num(job))

            def correlate(job):
                i, b = job
                n = num(job)
                pe.wait_ge(s["bt_copied"], n + 1)
                nc.tensor.matmul(pbt[:, 2 * P:3 * P], bcT[:, b, 0, :], bcT[:, b, 1, :], start=True, stop=True).then_inc(s["g_ready"], 1)

            project((0, 0))
            await_bc((0, 0))
            state_rows((0, 0))
            correlate((0, 0))

            def step(prev, cur, nxt):
                if nxt:
                    project(nxt)
                if prev:
                    i, b = prev
                    n = num(prev)
                    pe.wait_ge(s["yg_done"], n + 1)
                    pe.wait_ge(s["x_done"], n)
                    for k in range(INNER // P):
                        last = nc.tensor.transpose(pyT[:, k * P:(k + 1) * P], y[:, b, k * P:(k + 1) * P], m.ident[:])
                    last.then_inc(s["yT_ready"], 1)
                if cur:
                    i, b = cur
                    n = num(cur)
                    pe.wait_ge(s["h_done"], n)
                    pe.wait_ge(s["t1_done"], n)
                    nc.tensor.matmul(pi[:], bcT[:, b, 1, :], H[:, b], start=True, stop=True).then_inc(s["i_ready"], 1)
                    pe.wait_ge(s["xw_done"], n + 1)
                    if nxt:
                        await_bc(nxt)
                    nc.tensor.matmul(pst[0:STATE, :], bc[:, b, 0:STATE], xw[:, b], start=True, stop=True).then_inc(s["st_ready"], 1)
                if nxt:
                    state_rows(nxt)
                if cur:
                    pe.wait_ge(s["m_done"], n + 1)
                    pe.wait_ge(s["dtx_done"], n + 1)
                    pe.wait_ge(s["t2_done"], n)
                    for h in range(HEADS):
                        last = nc.tensor.matmul(py[:, h * HD:(h + 1) * HD], mt[:, h, :], dtx[:, b, h * HD:(h + 1) * HD],
                                                start=True, stop=True)
                    last.then_inc(s["y_ready"], 1)
                if nxt:
                    correlate(nxt)
                if prev:
                    i, b = prev
                    n = num(prev)
                    pe.wait_ge(s["yl_done"], n + 1)
                    for k in range(INNER // P):
                        last = exact_matmul(nc, po, yh[:, k, :], yl[:, k, :], wogh[:, b, k, :], wogl[:, b, k, :],
                                            k == 0, k == INNER // P - 1)
                    last.then_inc(s["o_ready"], 1)
            jobs(pe, step)


EX = 16
FE = 512
FT = FE // P
CAP = T * 2 // EX
ROW = C + EX
RX = B * EX
BITS = 30
RADIX = 16


def routing_scores(nc, m, w):
    with ExitStack() as ctx:
        sb, ps, sem = setup(nc, ctx)
        NJ, NBUF = NG * B, NG * B
        hx = sb("h_hx", [P, NBUF, GT, ROW])
        gw = sb("h_gw", [P, CH, EX])
        mx, sm = sb("h_mx", [P, 2, GT]), sb("h_sm", [P, 2, GT])
        lg, ex = sb("h_lg", [P, 2, GT, EX]), sb("h_ex", [P, 2, GT, EX])
        by_tile = sb("h_by_tile", [P, NTB, B, EX])
        pT = ps("h_pT", [P, 2, CH, GW])
        pg = ps("h_pg", [P, 2, 512])
        pS = ps("h_pS", [RX, 2, 512])
        names = ("loaded stat0 stat1 stat2 stat3 stat4 normed scaled shifted t_ready t_copied g_ready mx_done lg_done ex_done "
                 "sm_done rs_done sc_done bt_done s_ready s_copied shared_in").split()
        s = {n: sem("h_" + n) for n in names}
        rows_out = [sem(f"h_rows{q}") for q in range(NBUF)]
        block = ctx.enter_context(nc.Block())
        st_vector, st_gpsimd = finish_stats(nc, [s[f"stat{i}"] for i in range(5)], m, 0, NT)

        def tiles(n):
            first = n % B * NTB + n // B * GT
            return slice(first, first + GT)

        @block.sync
        def _(sp):
            sp.dma_start(gw[:], w["gate_wT"].rearrange("(h p) n -> p h n", p=P)).then_inc(s["loaded"], 16)
            for dst, src in ((m.wg, w["Ws_gT"]), (m.wu, w["Ws_uT"]), (m.wd, w["Ws_dT"])):
                sp.dma_start(dst[:], src.rearrange("(h p) n -> p h n", p=P)).then_inc(s["shared_in"], 16)
            for n in range(NJ):
                sp.wait_ge(s["sc_done"], n + 1)
                sp.dma_start(m.rows.rearrange("(t p) c -> p t c", p=P)[:, tiles(n), :], hx[:, n % NBUF]).then_inc(rows_out[n % NBUF], 16)
            sp.wait_ge(s["shared_in"], 48)
            for q in range(NBUF):
                sp.wait_ge(rows_out[q], 16 * NJ // NBUF)

        @block.gpsimd
        def _(pool):
            st_gpsimd()
            for n in range(NJ):
                hb = hx[:, n % NBUF, :, 0:C]
                pool.wait_ge(s["scaled"], n + 1)
                nc.gpsimd.tensor_tensor(hb, hb, over(m.mod[:, n % B, SB, :], GT), ALU.add).then_inc(s["shifted"], 1)

        @block.vector
        def _(dve):
            st_vector()
            dve.wait_ge(s["stat4"], 1)

            def normalise(n):
                if n >= NBUF:
                    dve.wait_ge(rows_out[n % NBUF], n // NBUF * 16)
                for k in range(GT):
                    t = slice(tiles(n).start + k, tiles(n).start + k + 1)
                    nc.vector.tensor_scalar(hx[:, n % NBUF, k, 0:C], m.x[:, t, :].squeeze(1), m.mean[:, t], m.rstd[:, t],
                                            ALU.subtract, ALU.mult).then_inc(s["normed"], 1)
                dve.wait_ge(s["normed"], (n + 1) * GT)
                hb = hx[:, n % NBUF, :, 0:C]
                nc.vector.tensor_tensor(hb, hb, over(m.mod[:, n % B, CB, :], GT), ALU.mult).then_inc(s["scaled"], 1)

            col = lambda t, n: t[:, n % 2].unsqueeze(2).to_broadcast([P, GT, EX])

            def centre(n):
                dve.wait_ge(s["g_ready"], n + 1)
                pl = pg[:, n % 2, 0:GT * EX].rearrange("p (t e) -> p t e", e=EX)
                nc.vector.tensor_reduce(mx[:, n % 2], pl, AX, ALU.max).then_inc(s["mx_done"], 1)
                dve.wait_ge(s["mx_done"], n + 1)
                nc.vector.tensor_tensor(lg[:, n % 2], pl, col(mx, n), ALU.subtract).then_inc(s["lg_done"], 1)

            def scores(n):
                e = ex[:, n % 2]
                dve.wait_ge(s["ex_done"], n + 1)
                nc.vector.tensor_reduce(sm[:, n % 2], e, AX, ALU.add).then_inc(s["sm_done"], 1)
                dve.wait_ge(s["sm_done"], n + 1)
                nc.vector.reciprocal(sm[:, n % 2], sm[:, n % 2]).then_inc(s["rs_done"], 1)
                dve.wait_ge(s["rs_done"], n + 1)
                nc.vector.tensor_tensor(hx[:, n % NBUF, :, C:ROW], e, col(sm, n), ALU.mult).then_inc(s["sc_done"], 1)
                nc.vector.tensor_tensor(by_tile[:, n // B * GT:(n // B + 1) * GT, n % B, :], e, col(sm, n), ALU.mult).then_inc(s["bt_done"], 1)

            def keep_scores(g):
                dve.wait_ge(s["s_ready"], g + 1)
                nc.vector.tensor_copy(m.sc[:, g * GW:(g + 1) * GW], pS[:, g % 2, :]).then_inc(s["s_copied"], 1)

            normalise(0)
            normalise(1)
            for n in range(NJ):
                if n + 2 < NJ:
                    normalise(n + 2)
                centre(n)
                if n:
                    scores(n - 1)
                if n >= 5 and n % 2:
                    keep_scores((n - 5) // 2)
            scores(NJ - 1)
            keep_scores(NG - 2)
            keep_scores(NG - 1)

        @block.scalar
        def _(act):
            def copy_t(n):
                act.wait_ge(s["t_ready"], n + 1)
                nc.scalar.copy(m.hT[:, :, tiles(n).start * P:tiles(n).stop * P], pT[:, n % 2]).then_inc(s["t_copied"], 1)

            copy_t(0)
            for n in range(NJ):
                if n + 1 < NJ:
                    copy_t(n + 1)
                act.wait_ge(s["lg_done"], n + 1)
                if n >= 2:
                    act.wait_ge(s["bt_done"], n - 1)
                nc.scalar.activation(ex[:, n % 2], lg[:, n % 2], ACT.Exp).then_inc(s["ex_done"], 1)

        @block.tensor
        def _(pe):
            def transposes(n):
                pe.wait_ge(s["shifted"], n + 1)
                if n >= 2:
                    pe.wait_ge(s["t_copied"], n - 1)
                for h in range(CH):
                    for k in range(GT):
                        last = nc.tensor.transpose(pT[:, n % 2, h, k * P:(k + 1) * P], hx[:, n % NBUF, k, h * P:(h + 1) * P], m.ident[:])
                last.then_inc(s["t_ready"], 1)

            def logits(n):
                pe.wait_ge(s["t_copied"], n + 1)
                if n >= 2:
                    pe.wait_ge(s["lg_done"], n - 1)
                for k in range(GT):
                    for h in range(CH):
                        tok = slice((tiles(n).start + k) * P, (tiles(n).start + k + 1) * P)
                        last = nc.tensor.matmul(pg[:, n % 2, k * EX:(k + 1) * EX], m.hT[:, h, tok], gw[:, h, :],
                                                start=h == 0, stop=h == CH - 1)
                last.then_inc(s["g_ready"], 1)

            def by_expert(g):
                pe.wait_ge(s["bt_done"], (g + 1) * B)
                if g >= 2:
                    pe.wait_ge(s["s_copied"], g - 1)
                for k in range(GT):
                    last = nc.tensor.transpose(pS[:, g % 2, k * P:(k + 1) * P],
                                               by_tile[:, g * GT + k].rearrange("p b e -> p (b e)"), m.ident[:])
                last.then_inc(s["s_ready"], 1)

            pe.wait_ge(s["loaded"], 16)
            transposes(0)
            for n in range(NJ):
                if n + 1 < NJ:
                    transposes(n + 1)
                logits(n)
                if n >= 3 and n % 2:
                    by_expert((n - 3) // 2)
            by_expert(NG - 1)


def shared_and_choice(nc, m, w, out):
    with ExitStack() as ctx:
        sb, ps, sem = setup(nc, ctx)
        act_g = sb("i_act_g", [P, 2, GW])
        hid = sb("i_hid", [P, B, FT, GW])
        ob = sb("i_ob", [P, B, GT, C])
        prefix, cand, add = [sb("i_" + n, [RX, 1], I32) for n in ("prefix", "cand", "add")]
        bits = sb("i_bits", [RX, BITS], I32)
        cnt, room = sb("i_cnt", [RX, 1]), sb("i_room", [RX, 1])
        junk = sb("i_junk", [RX, T])
        place = junk[:]
        NP, NQ = NTB * RX, 4
        A = sb("j_A", [P, NTB, RX, RADIX], BF16)
        R = sb("j_R", [P, NTB, RX, 2, RADIX], BF16)
        flat = A[0:RX].rearrange("p t e a -> p (t e a)").bitcast(F32)
        eq, rank = flat[:, 0:T], flat[:, T:2 * T]
        pl = sb("j_pl", [P, NP], I32)
        upper, lower = sb("j_upper", [P, NP], I32), sb("j_lower", [P, NP], I32)
        io, lid = sb("j_io", [P, RADIX]), sb("j_lid", [P, 1])
        dmask = sb("j_dmask", [P, 8])
        mk = sb("j_mk", [P, NQ, 8, 2 * RADIX])
        red = sb("j_red", [P, NQ, 2 * RADIX])
        ix = sb("j_ix", [P, NQ, RADIX])
        rows = sb("j_rows", [2 * RX, P])
        pg, pu, po = ps("i_pg", [P, 2, GW]), ps("i_pu", [P, 2, GW]), ps("i_po", [P, GT, C])
        pI = ps("j_pI", [P, NQ, 8 * 2 * RADIX])
        pW = pI[:, 0:2].rearrange("p q n -> p (q n)")
        pX = pI[:, 0, 0:2 * RX]
        names = ("gu_ready gelu_done hid_done o_ready ga_done ob_done bit0 bits cand cnt add prefix c0 c1 c2 c3 c4 c5 c6 placed "
                 "io w_ready w_done ul A0 B0 R0 R1 i_ready mk red ix rows_in x_ready dm").split()
        s = {n: sem("i_" + n) for n in names}
        stored = [sem(f"i_stored{b}") for b in range(B)]
        block = ctx.enter_context(nc.Block())
        NJ = NG * B
        SEARCHED = 5
        PER = BITS // SEARCHED
        CHUNKS = 4
        part = lambda t, c: t[:, c * NTB // CHUNKS:(c + 1) * NTB // CHUNKS]
        merged = lambda t: t.rearrange("p t e a -> p (t e) a")
        digit = lambda t, c: t[:, c * NP // CHUNKS:(c + 1) * NP // CHUNKS].unsqueeze(2).to_broadcast([P, NP // CHUNKS, RADIX])

        def groups(eng, group):
            with eng.Fori(0, SEARCHED // B) as i:
                for b in range(B):
                    group(i * B + b, i, b)
            for g in range(SEARCHED // B * B, NJ):
                group(g, g // B, g % B)

        @block.sync
        def _(sp):
            for owed in [s[n] for n in "o_ready hid_done ga_done prefix".split()] + stored:
                sp.sem_inc(owed, CREDIT)
            def group(g, i, b):
                sp.wait_ge(s["ob_done"], g + 1)
                sp.dma_start(out.rearrange("(t p) c -> p t c", p=P)[:, bass.ds(b * NTB + i * GT, GT), :],
                             ob[:, b]).then_inc(stored[b], 16)
            groups(sp, group)
            sp.wait_ge(s["ix"], 1)
            for q in range(NQ):
                sp.dma_start(rows[q * 16:(q + 1) * 16, :].rearrange("r (a b) -> r a b", a=8), ix[:, q, :]).then_inc(s["rows_in"], 16)
            for b in range(B):
                sp.wait_ge(stored[b], 16 * NG + CREDIT)

        @block.gpsimd
        def _(pool):
            g = nc.gpsimd
            g.iota(io[:], pattern=[[1, RADIX]], base=0, channel_multiplier=0, allow_small_or_imprecise_dtypes=True).then_inc(s["io"], 1)
            g.iota(lid[:], pattern=[[0, 1]], base=0, channel_multiplier=1, allow_small_or_imprecise_dtypes=True).then_inc(s["io"], 1)
            g.memset(dmask[:], 1.0).then_inc(s["dm"], 1)
            pool.wait_ge(s["dm"], 1)
            g.affine_select(out=dmask[:], in_=dmask[:], compare_op=ALU.is_ge, fill=0.0, base=0,
                            pattern=[[-RADIX, 8]], channel_multiplier=1).then_inc(s["dm"], 1)
            pool.wait_ge(s["dm"], 2)
            g.affine_select(out=dmask[:], in_=dmask[:], compare_op=ALU.is_ge, fill=0.0, base=RADIX - 1,
                            pattern=[[RADIX, 8]], channel_multiplier=-1).then_inc(s["dm"], 1)

            def group(n, i, b):
                pool.wait_ge(s["ga_done"], n + 1 + CREDIT)
                g.tensor_tensor(ob[:, b], ob[:, b], m.x[:, bass.ds(b * NTB + i * GT, GT), :], ALU.add).then_inc(s["ob_done"], 1)
            groups(pool, group)

        @block.scalar
        def _(act):
            def group(g, i, b):
                for f in range(FT):
                    n = g * FT + f
                    act.wait_ge(s["gu_ready"], n + 1)
                    act.wait_ge(s["hid_done"], n - 1 + CREDIT) if (f >= 2) else act.wait_ge(s["hid_done"], g * FT + CREDIT)
                    nc.scalar.activation(act_g[:, f % 2], pg[:, f % 2], ACT.Gelu).then_inc(s["gelu_done"], 1)
                    if isinstance(g, int) and g == NJ - 1:
                        places(f)

            def places(c):
                act.wait_ge(s["R0"], (c + 1) * NTB // CHUNKS * B)
                one = merged(part(R, c)[:, :, :, 1, :])
                nc.scalar.activation(one, one, ACT.Copy, scale=lid[:]).then_inc(s["R1"], 1)

            act.wait_ge(s["io"], 2)
            groups(act, group)

        @block.tensor
        def _(pe):
            def group(g, i, b):
                at = g if isinstance(g, int) else None
                for f in range(FT):
                    n = g * FT + f
                    if f >= 2:
                        pe.wait_ge(s["hid_done"], n - 1 + CREDIT)
                    else:
                        pe.wait_ge(s["hid_done"], g * FT + CREDIT)
                    for dst, wt in ((pg, m.wg), (pu, m.wu)):
                        for k in range(CH):
                            last = nc.tensor.matmul(dst[:, f % 2], wt[:, k, f * P:(f + 1) * P],
                                                    m.hT[:, k, bass.ds(b * T + i * GW, GW)], start=k == 0, stop=k == CH - 1)
                    last.then_inc(s["gu_ready"], 1)
                    if at == NJ - 2 and f == 0:
                        by_token()
                    if at == NJ - 1 and f == FT - 1:
                        products()
                pe.wait_ge(s["hid_done"], (g + 1) * FT + CREDIT)
                pe.wait_ge(s["ga_done"], g + CREDIT)
                for t in range(GT):
                    for f in range(FT):
                        last = nc.tensor.matmul(po[:, t], hid[:, b, f, t * P:(t + 1) * P], m.wd[:, f, :],
                                                start=f == 0, stop=f == FT - 1)
                last.then_inc(s["o_ready"], 1)

            def by_token():
                pe.wait_ge(s["placed"], 1)
                for t in range(NTB):
                    last = nc.tensor.transpose(pW[:, t * RX:(t + 1) * RX], place[:, t * P:(t + 1) * P], m.ident[0:RX, 0:RX])
                last.then_inc(s["w_ready"], 1)

            def products():
                pe.wait_ge(s["R1"], CHUNKS)
                pe.wait_ge(s["A0"], CHUNKS)
                for q in range(NQ):
                    for t in range(NTB):
                        last = nc.tensor.matmul(pI[:, q], A[:, t, q * 8:(q + 1) * 8, :].rearrange("p e a -> p (e a)"),
                                                R[:, t, q * 8:(q + 1) * 8].rearrange("p e k b -> p (e k b)"),
                                                start=t == 0, stop=t == NTB - 1)
                last.then_inc(s["i_ready"], 1)

            groups(pe, group)
            pe.wait_ge(s["rows_in"], 16 * NQ)
            nc.tensor.transpose(pX, rows[:], m.ident[0:2 * RX, 0:2 * RX]).then_inc(s["x_ready"], 1)

        @block.vector
        def _(dve):
            v = nc.vector
            prefix_f, cand_f = prefix[:].bitcast(F32), cand[:].bitcast(F32)
            v.memset(prefix[:], 0)
            v.memset(bits[:, 0:1], 1 << (BITS - 1)).then_inc(s["bit0"], 1)
            dve.wait_ge(s["bit0"], 1)
            for k in range(1, BITS):
                last = v.tensor_scalar(bits[:, k:k + 1], bits[:, 0:1], k, None, ALU.logical_shift_right)
            last.then_inc(s["bits"], 1)
            dve.wait_ge(s["bits"], 1)

            def search(j):
                bit = bits[:, bass.ds(j, 1)]
                dve.wait_ge(s["prefix"], j + CREDIT)
                v.tensor_tensor(cand[:], prefix[:], bit, ALU.bitwise_or).then_inc(s["cand"], 1)
                dve.wait_ge(s["cand"], j + 1)
                v.tensor_scalar(junk[:], m.sc[:], cand_f, 0.0, ALU.is_ge, ALU.add, accum_out=cnt[:]).then_inc(s["cnt"], 1)
                dve.wait_ge(s["cnt"], j + 1)
                v.scalar_tensor_tensor(out=add[:], in0=cnt[:], scalar=float(CAP), in1=bit, op0=ALU.is_ge, op1=ALU.mult).then_inc(s["add"], 1)
                dve.wait_ge(s["add"], j + 1)
                v.tensor_tensor(prefix[:], prefix[:], add[:], ALU.bitwise_or).then_inc(s["prefix"], 1)

            def choose(f):
                if f == 0:
                    dve.wait_ge(s["prefix"], BITS + CREDIT)
                    v.tensor_scalar(junk[:], m.sc[:], prefix_f, 0.0, ALU.is_gt, ALU.add, accum_out=cnt[:]).then_inc(s["c0"], 1)
                    v.tensor_scalar(eq, m.sc[:], prefix_f, None, ALU.is_equal).then_inc(s["c1"], 1)
                if f == 1:
                    dve.wait_ge(s["c1"], 1)
                    v.tensor_tensor_scan(rank, eq, eq, 0.0, ALU.add, ALU.bypass).then_inc(s["c2"], 1)
                    dve.wait_ge(s["c0"], 1)
                    v.tensor_scalar(room[:], cnt[:], -1.0, float(CAP), ALU.mult, ALU.add).then_inc(s["c3"], 1)
                if f == 2:
                    dve.wait_ge(s["c2"], 1)
                    dve.wait_ge(s["c3"], 1)
                    v.scalar_tensor_tensor(out=eq, in0=rank, scalar=room[:], in1=eq, op0=ALU.is_le, op1=ALU.mult).then_inc(s["c4"], 1)
                    dve.wait_ge(s["c4"], 1)
                    v.tensor_tensor(eq, eq, junk[:], ALU.add).then_inc(s["c5"], 1)
                if f == 3:
                    dve.wait_ge(s["c5"], 1)
                    v.tensor_tensor_scan(rank, eq, eq, 0.0, ALU.add, ALU.bypass).then_inc(s["c6"], 1)
                    dve.wait_ge(s["c6"], 1)
                    v.tensor_tensor(place, rank, eq, ALU.mult).then_inc(s["placed"], 1)

            def digits():
                dve.wait_ge(s["w_ready"], 1)
                v.tensor_scalar(pl[:], pW, -1.0, None, ALU.add).then_inc(s["w_done"], 1)
                dve.wait_ge(s["w_done"], 1)
                v.tensor_scalar(upper[:], pl[:], 4, None, ALU.arith_shift_right).then_inc(s["ul"], 1)
                v.tensor_scalar(lower[:], pl[:], RADIX - 1, None, ALU.bitwise_and).then_inc(s["ul"], 1)

            def upper_table(c):
                dve.wait_ge(s["ul"], 2)
                dve.wait_ge(s["io"], 2)
                v.tensor_tensor(merged(part(A, c)), digit(upper, c),
                                io[:].unsqueeze(1).to_broadcast([P, NP // CHUNKS, RADIX]), ALU.is_equal).then_inc(s["A0"], 1)

            def lower_table(c):
                dve.wait_ge(s["ul"], 2)
                v.tensor_tensor(merged(part(R, c)[:, :, :, 1, :]), digit(lower, c),
                                io[:].unsqueeze(1).to_broadcast([P, NP // CHUNKS, RADIX]), ALU.is_equal).then_inc(s["B0"], 1)
                dve.wait_ge(s["B0"], c + 1)
                for t in range(c * NTB // CHUNKS, (c + 1) * NTB // CHUNKS):
                    for b in range(B):
                        e = slice(b * EX, (b + 1) * EX)
                        v.tensor_scalar(R[:, t, e, 0, :], R[:, t, e, 1, :], float(b * NTB + t), None, ALU.mult).then_inc(s["R0"], 1)

            def lists():
                dve.wait_ge(s["i_ready"], 1)
                dve.wait_ge(s["dm"], 3)
                for q in range(NQ):
                    v.tensor_tensor(mk[:, q], pI[:, q].rearrange("p (e k) -> p e k", e=8),
                                    dmask[:].unsqueeze(2).to_broadcast([P, 8, 2 * RADIX]), ALU.mult).then_inc(s["mk"], 1)
                dve.wait_ge(s["mk"], NQ)
                v.tensor_reduce(red[:], mk[:].rearrange("p q e k -> p q k e"), AX, ALU.add).then_inc(s["red"], 1)
                dve.wait_ge(s["red"], 1)
                v.scalar_tensor_tensor(out=ix[:], in0=red[:, :, 0:RADIX], scalar=float(P), in1=red[:, :, RADIX:],
                                       op0=ALU.mult, op1=ALU.add).then_inc(s["ix"], 1)

            def group(g, i, b):
                at = g if isinstance(g, int) else None
                for f in range(FT):
                    n = g * FT + f
                    dve.wait_ge(s["gelu_done"], n + 1)
                    dve.wait_ge(s["o_ready"], g + CREDIT)
                    v.tensor_tensor(hid[:, b, f], act_g[:, f % 2], pu[:, f % 2], ALU.mult).then_inc(s["hid_done"], 1)
                    if at is None or at < SEARCHED:
                        search(g * PER + f)
                    elif at == SEARCHED:
                        choose(f)
                    elif at == NJ - 2 and f == 1:
                        digits()
                    elif at == NJ - 2 and f == 2:
                        upper_table(0)
                    elif at == NJ - 2 and f == 3:
                        lower_table(0)
                    elif at == NJ - 1 and f == 0:
                        lower_table(2)
                    elif at == NJ - 1 and f == 1:
                        upper_table(3)
                    elif at == NJ - 1 and f == 2:
                        lower_table(3)
                if at is None or at < SEARCHED:
                    for j in range(FT, PER):
                        search(g * PER + j)
                if at == NJ - 2:
                    upper_table(1)
                    lower_table(1)
                    upper_table(2)
                if at == NJ - 1:
                    lists()
                dve.wait_ge(s["o_ready"], g + 1 + CREDIT)
                if not (isinstance(i, int) and i == 0):
                    dve.wait_ge(stored[b], 16 * i + CREDIT)
                v.tensor_tensor(ob[:, b], po[:], over(m.mod[:, b, GB, :], GT), ALU.mult).then_inc(s["ga_done"], 1)

            groups(dve, group)
            dve.wait_ge(s["x_ready"], 1)
            v.tensor_copy(m.idx[:], pX)


def experts(nc, m, w, out):
    with ExitStack() as ctx:
        sb, ps, sem = setup(nc, ctx)
        NTOK = B * CAP // P
        xe, score = sb("k_xe", [P, 2, NTOK, ROW]), sb("k_score", [P, 2, NTOK, EX])
        xh, xl = sb("k_xh", [P, 2, CH, GW], FR), sb("k_xl", [P, 2, CH, GW], FR)
        WN = CH * FE
        wf = sb("k_wf", [P, 2, 3, WN])
        wh, wl = sb("k_wh", [P, 2, 3, WN], FR), sb("k_wl", [P, 2, 3, WN], FR)
        act_g = sb("k_act_g", [P, 2, GW])
        hid = sb("k_hid", [P, 2, GW])
        hh, hl = sb("k_hh", [P, 2, FT, GW], FR), sb("k_hl", [P, 2, FT, GW], FR)
        eo = sb("k_eo", [P, 2, NTOK, C])
        pg, pu, po, pT = ps("k_pg", [P, 2, GW]), ps("k_pu", [P, 2, GW]), ps("k_po", [P, NTOK, C]), ps("k_pT", [P, CH, GW])
        names = "t_ready xh_done xl_done wh_done wl_done gu_ready gelu_done hid_done hh_done hl_done o_ready eo_done score_kept".split()
        s = {n: sem("k_" + n) for n in names}
        gathered, w_in, added = [[sem(f"k_{n}{k}") for k in range(2)] for n in ("gathered", "w_in", "added")]
        block = ctx.enter_context(nc.Block())

        def column(e, t):
            b, half = divmod(t, 2)
            return m.idx[:, (b * EX + e) * 2 + half:(b * EX + e) * 2 + half + 1]

        def steps(eng, step, ahead=1):
            for i in range(ahead):
                step(i, 0)
                step(i, 1)
            with eng.Fori(ahead, EX // 2 - 1) as i:
                step(i, 0)
                step(i, 1)
            step(EX // 2 - 1, 0)
            step(EX // 2 - 1, 1, True)

        def early(i):
            return isinstance(i, int) and i == 0

        @block.sync
        def _(sp):
            def load(i, k):
                e = i * 2 + k
                for j, name in enumerate(("WgT", "WuT", "WdT")):
                    src = w[name][bass.ds(e, 1)].squeeze(0).rearrange("(h p) n -> p h n", p=P)
                    sp.dma_start(wf[:, k, j].rearrange("p (h n) -> p h n", n=src.shape[-1]), src).then_inc(w_in[k], 16)
            load(0, 0)
            load(0, 1)
            with sp.Fori(1, EX // 2) as i:
                for k in range(2):
                    sp.wait_ge(s["wl_done"], ((i - 1) * 2 + k + 1) * 3)
                    load(i, k)

        @block.gpsimd
        def _(pool):
            def gather(e):
                if e >= 2:
                    pool.wait_ge(s["t_ready"], e - 1)
                    pool.wait_ge(s["score_kept"], e - 1)
                for t in range(NTOK):
                    nc.gpsimd.indirect_dma_start(out=xe[:, e % 2, t, :], out_offset=None, in_=m.rows,
                                                 in_offset=bass.IndirectOffsetOnAxis(ap=column(e, t), axis=0)).then_inc(gathered[e % 2], 16)

            gather(0)
            gather(1)
            for e in range(EX):
                if e + 2 < EX:
                    gather(e + 2)
                pool.wait_ge(s["eo_done"], e + 1)
                if e:
                    pool.wait_ge(added[(e - 1) % 2], 16 * NTOK * ((e - 1) // 2 + 1))
                for t in range(NTOK):
                    nc.gpsimd.indirect_dma_start(out=out, out_offset=bass.IndirectOffsetOnAxis(ap=column(e, t), axis=0),
                                                 in_=eo[:, e % 2, t, :], in_offset=None,
                                                 compute_op=ALU.add).then_inc(added[e % 2], 16)
            for k in range(2):
                pool.wait_ge(added[k], 16 * NTOK * EX // 2)

        @block.scalar
        def _(act):
            def rows_high(i, k):
                act.wait_ge(s["t_ready"], i * 2 + k + 1)
                nc.scalar.copy(xh[:, k], pT[:]).then_inc(s["xh_done"], 1)

            def weights_high(i, k, j):
                if j == 0:
                    act.wait_ge(w_in[k], 48 * (i + 1))
                if j == 2 and not early(i):
                    act.wait_ge(s["o_ready"], i * 2 + k - 1)
                nc.scalar.copy(wh[:, k, j], wf[:, k, j]).then_inc(s["wh_done"], 1)

            def hidden_high(i, k, f):
                e = i * 2 + k
                act.wait_ge(s["hid_done"], e * FT + f + 1)
                if f == 0 and not early(i):
                    act.wait_ge(s["o_ready"], e - 1)
                nc.scalar.copy(hh[:, k, f], hid[:, f % 2]).then_inc(s["hh_done"], 1)

            def step(i, k, last=False):
                for f in range(FT):
                    n = (i * 2 + k) * FT + f
                    act.wait_ge(s["gu_ready"], n + 1)
                    if not (early(i) and k == 0 and f < 2):
                        act.wait_ge(s["hid_done"], n - 1)
                    nc.scalar.activation(act_g[:, f % 2], pg[:, f % 2], ACT.Gelu).then_inc(s["gelu_done"], 1)
                    if f:
                        hidden_high(i, k, f - 1)
                    if f < 3 and not last:
                        weights_high(i + k, 1 - k, f)
                    if f == 1 and not last:
                        rows_high(i + k, 1 - k)
                hidden_high(i, k, FT - 1)

            for j in range(3):
                weights_high(0, 0, j)
            rows_high(0, 0)
            steps(act, step)

        @block.vector
        def _(dve):
            def rows_low(i, k):
                dve.wait_ge(s["xh_done"], i * 2 + k + 1)
                nc.vector.tensor_tensor(xl[:, k], pT[:], xh[:, k].bitcast(F32), ALU.subtract).then_inc(s["xl_done"], 1)
                if not early(i):
                    dve.wait_ge(s["eo_done"], i * 2 + k - 1)
                nc.vector.tensor_copy(score[:, k], xe[:, k, :, C:ROW]).then_inc(s["score_kept"], 1)

            def weights_low(i, k, j):
                dve.wait_ge(s["wh_done"], (i * 2 + k) * 3 + j + 1)
                nc.vector.tensor_tensor(wl[:, k, j], wf[:, k, j], wh[:, k, j].bitcast(F32), ALU.subtract).then_inc(s["wl_done"], 1)

            def hidden_low(i, k, f):
                dve.wait_ge(s["hh_done"], (i * 2 + k) * FT + f + 1)
                nc.vector.tensor_tensor(hl[:, k, f], hid[:, f % 2], hh[:, k, f].bitcast(F32), ALU.subtract).then_inc(s["hl_done"], 1)

            def output(i, k):
                e = i * 2 + k
                dve.wait_ge(s["score_kept"], e + 1)
                dve.wait_ge(s["o_ready"], e + 1)
                if not early(i):
                    dve.wait_ge(added[k], 16 * NTOK * i)
                for t in range(NTOK):
                    last = nc.vector.scalar_tensor_tensor(out=eo[:, k, t, :], in0=po[:, t], scalar=score[:, k, t, bass.ds(e, 1)],
                                                          in1=m.mod[:, t // 2, GB, :], op0=ALU.mult, op1=ALU.mult)
                last.then_inc(s["eo_done"], 1)

            def step(i, k, last=False):
                for f in range(FT):
                    n = (i * 2 + k) * FT + f
                    dve.wait_ge(s["gelu_done"], n + 1)
                    if not (early(i) and k == 0 and f < 2):
                        dve.wait_ge(s["hl_done"], n - 1)
                    nc.vector.tensor_tensor(hid[:, f % 2], act_g[:, f % 2], pu[:, f % 2], ALU.mult).then_inc(s["hid_done"], 1)
                    if f == 0 and not (early(i) and k == 0):
                        output(i - 1 + k, 1 - k)
                    if f:
                        hidden_low(i, k, f - 1)
                    if f < 3 and not last:
                        weights_low(i + k, 1 - k, f)
                    if f == 1 and not last:
                        rows_low(i + k, 1 - k)
                hidden_low(i, k, FT - 1)

            for j in range(3):
                weights_low(0, 0, j)
            rows_low(0, 0)
            steps(dve, step, 2)
            output(EX // 2 - 1, 1)

        @block.tensor
        def _(pe):
            def rows(i, k):
                n = i * 2 + k
                pe.wait_ge(gathered[k], 16 * NTOK * (i + 1))
                if not (early(i) and k == 0):
                    pe.wait_ge(s["xl_done"], n)
                for h in range(CH):
                    for t in range(NTOK):
                        last = nc.tensor.transpose(pT[:, h, t * P:(t + 1) * P], xe[:, k, t, h * P:(h + 1) * P], m.ident[:])
                last.then_inc(s["t_ready"], 1)

            def down(i, k):
                e = i * 2 + k
                pe.wait_ge(s["hl_done"], (e + 1) * FT)
                if not (early(i) and k == 0):
                    pe.wait_ge(s["eo_done"], e)
                for t in range(NTOK):
                    for f in range(FT):
                        tok, feat = slice(t * P, (t + 1) * P), slice(f * C, (f + 1) * C)
                        last = exact_matmul(nc, po[:, t], hh[:, k, f, tok], hl[:, k, f, tok], wh[:, k, 2, feat], wl[:, k, 2, feat],
                                            f == 0, f == FT - 1)
                last.then_inc(s["o_ready"], 1)

            def step(i, k, last_one=False):
                e = i * 2 + k
                pe.wait_ge(s["wl_done"], (e + 1) * 3)
                pe.wait_ge(s["xl_done"], e + 1)
                for f in range(FT):
                    n = e * FT + f
                    if not (early(i) and k == 0 and f < 2):
                        pe.wait_ge(s["hid_done"], n - 1)
                    for j, dst in enumerate((pg, pu)):
                        for h in range(CH):
                            feat = slice(h * FE + f * P, h * FE + (f + 1) * P)
                            last = exact_matmul(nc, dst[:, f % 2], wh[:, k, j, feat], wl[:, k, j, feat], xh[:, k, h, :], xl[:, k, h, :],
                                                h == 0, h == CH - 1)
                    last.then_inc(s["gu_ready"], 1)
                    if f == 0 and not (early(i) and k == 0):
                        down(i - 1 + k, 1 - k)
                    if f == 1 and not last_one:
                        rows(i + k, 1 - k)

            rows(0, 0)
            steps(pe, step)
            down(EX // 2 - 1, 1)


def program(nc, a, out):
    m = Shared()
    USED.clear()
    m.mod_dram = nc.dram_tensor("mod_dram", [2, B, NMOD, C], F32).ap()
    with ExitStack() as ctx:
        sb, ps, sem = setup(nc, ctx)
        m.x = sb("x", [P, NT, C])
        m.mod = sb("mod", [P, B, NMOD, C])
        m.ident, m.mask = sb("ident", [P, P]), sb("mask", [P, 2 * P])
        m.upto, m.after, m.ones = sb("upto", [P, P]), sb("after", [P, P]), sb("ones", [P, P])
        m.neghalf, m.st = sb("neghalf", [P, NT]), sb("st", [P, NT, 6])
        m.mean, m.rstd, m.tmp = sb("mean", [P, NT]), sb("rstd", [P, NT]), sb("tmp", [P, NT])
        m.idx = sb("idx", [P, 2 * RX], I32)
        with ExitStack() as scope:
            sb, _, _ = setup(nc, scope)
            m.seT, m.gx = sb("seT", [P, CH, NS]), sb("gx", [P, C])
            m.w1, m.w2 = sb("w1", [P, CH, HID]), sb("w2", [P, HT, C])
            with ExitStack() as inner:
                sb, _, _ = setup(nc, inner)
                m.wq, m.wk, m.wvo = sb("wq", [P, CH, C]), sb("wk", [P, CH, C]), sb("wvo", [P, B, CH, C])
                m.qb, m.kb, m.vrow = sb("qb", [P, CH]), sb("kb", [P, CH]), sb("vrow", [P, B, C])
                beginnings(nc, m, a)
                m.qT, m.kT = sb("qT", [P, CH, B * T]), sb("kT", [P, CH, B * T])
                m.v = sb("v", [P, NT, C + 1])
                attention_projections(nc, m)
                attention(nc, m, a)
            soft_mixture(nc, m)
        recycle(nc)
        with ExitStack() as scope:
            sb, _, _ = setup(nc, scope)
            m.cum_dram = nc.dram_tensor("cum_dram", [NT * HEADS, P], F32).ap()
            m.uT = sb("uT", [P, CH, B * T])
            m.dt, m.cs = sb("dt", [P, NT, HEADS]), sb("cs", [P, NT, 4, HEADS])
            m.etot = sb("etot", [STATE, NT, HEADS])
            m.wout = sb("g_wout", [P, INNER // P, C])
            m.winh, m.winl = sb("g_winh", [P, CH, DT0], FR), sb("g_winl", [P, CH, DT0], FR)
            m.wogh, m.wogl = sb("g_wogh", [P, B, INNER // P, C], FR), sb("g_wogl", [P, B, INNER // P, C], FR)
            m.bb, m.ones3 = sb("g_bb", [3, 2, DT0], BF16), sb("g_ones3", [3, P], BF16)
            m.dlm, m.cumb = sb("g_dlm", [P, 3, HEADS, P]), sb("g_cumb", [P, B, HEADS, P])
            m.win = m.dlm[:].rearrange("p k h t -> p (k h t)")[:, 0:CH * DT0].rearrange("p (k n) -> p k n", k=CH)
            m.wog = m.cumb[:].rearrange("p b h t -> p (b h t)").rearrange("p (b k c) -> p b k c", b=B, c=C)
            state_inputs(nc, m, a)
            decays(nc, m, a)
            state_space(nc, m, a)
        recycle(nc)
        m.rows = nc.dram_tensor("rows_dram", [B * T, ROW], F32).ap()
        with ExitStack() as scope:
            sb, _, _ = setup(nc, scope)
            m.hT, m.sc = sb("hT", [P, CH, B * T]), sb("sc", [RX, T])
            m.wg, m.wu, m.wd = sb("ws_g", [P, CH, FE]), sb("ws_u", [P, CH, FE]), sb("ws_d", [P, FT, C])
            routing_scores(nc, m, a)
            shared_and_choice(nc, m, a, out)
        experts(nc, m, a, out)


def kernel(**inputs):
    import numpy as np
    import concourse.bacc as bacc
    from concourse.bass_utils import run_bass_kernel_spmd

    g = {k: np.asarray(v) for k, v in inputs.items()}
    cols = lambda v: np.ascontiguousarray(v.reshape(-1, P).T)
    arrays = {
        "x": g["L0_attn_x"].reshape(B * T, C),
        "c_cols": np.stack([np.ascontiguousarray(g[f"L{l}_c"].T.reshape(CH, P, B).transpose(1, 0, 2)) for l in range(2)]),
        "wmod0": g["L0_wmod"], "wmod1": g["L1_wmod"],
        "WqT": g["L0_attn_Wq"].T, "WkT": g["L0_attn_Wk"].T, "Wv": g["L0_attn_Wv"], "WoT": g["L0_attn_Wo"].T,
        "bq": cols(g["L0_attn_bq"]), "bk": cols(g["L0_attn_bk"]), "bv": cols(g["L0_attn_bv"]), "bo": g["L0_attn_bo"],
    }
    arrays |= {
        "slot_embeds": g["L0_ffn_slot_embeds"].reshape(NS, C), "gamma_slot": g["L0_ffn_gamma_slot"],
        "gamma_x": g["L0_ffn_gamma_x"], "w1": g["L0_ffn_w1"], "w2": g["L0_ffn_w2"],
    }
    arrays |= {n: g["L1_attn_" + n] for n in ("W_in", "b_in", "A_log", "D_skip", "dt_bias", "W_out", "b_out")}
    arrays["ln_cols"] = np.stack([cols(g["L1_attn_ln_gamma"]), cols(g["L1_attn_ln_beta"])], 1)
    arrays |= {
        "gate_wT": g["L1_ffn_gate_w"].T, "Ws_gT": g["L1_ffn_Ws_g"].T, "Ws_uT": g["L1_ffn_Ws_u"].T, "Ws_dT": g["L1_ffn_Ws_d"].T,
        "WgT": g["L1_ffn_Wg"].transpose(0, 2, 1), "WuT": g["L1_ffn_Wu"].transpose(0, 2, 1), "WdT": g["L1_ffn_Wd"].transpose(0, 2, 1),
    }
    nc = bacc.Bacc("TRN2", target_bir_lowering=False, num_devices=1)
    ins, feed = {}, {}
    for name, v in arrays.items():
        v = np.ascontiguousarray(v)
        feed[f"in_{name}"] = v
        ins[name] = nc.dram_tensor(f"in_{name}", v.shape, mybir.dt.from_np(v.dtype), kind="ExternalInput").ap()
    out = nc.dram_tensor("out", (B * T, C), F32, kind="ExternalOutput").ap()
    program(nc, ins, out)
    r = run_bass_kernel_spmd(nc, [feed], core_ids=[0])
    return r.results[0]["out"].reshape(B, T, C)
```
